# Optimizing a Trainium2 kernel written in Bass

```python
import numpy as np
import jax
import jax.numpy as jnp

def _softmax(x, axis=-1):
    return jax.nn.softmax(x, axis=axis)

def _gelu(x):
    return jax.nn.gelu(x, approximate=True)

def _silu(x):
    return jax.nn.silu(x)

def _sigmoid(x):
    return jax.nn.sigmoid(x)

def _layernorm(x, axis=-1, eps=1e-05):
    m = jnp.mean(x, axis=axis, keepdims=True)
    v = jnp.var(x, axis=axis, keepdims=True)
    return (x - m) / jnp.sqrt(v + eps)

def _scatter_add(tgt, idx, src, axis=0):
    return tgt.at[idx].add(src)

def _segment_sum(src, seg, n):
    return jax.ops.segment_sum(src, seg, n)
kernel_name = 'mk_seq_postln_d1_jaxref_r8_e10f01'

def setup_inputs(seed: int=0):
    np.random.seed(seed)
    _w = jnp.asarray

    def _L0_attn_setup():
        import jax, jax.numpy as jnp
        import numpy as np
        EMBED_DIM = 128
        NUM_HEADS = 16
        HEAD_DIM = EMBED_DIM // NUM_HEADS
        WL_CHANNELS = 16
        BATCH = 1
        SEQ = 128
        KERR = 2.7e-18 * 1000000.0
        SCALE = 1.0 / np.sqrt(HEAD_DIM)
        W_INIT = 0.02
        key = jax.random.key(seed)
        ks = jax.random.split(key, 7)
        x = jax.random.normal(ks[0], (BATCH, SEQ, EMBED_DIM), dtype=jnp.float32)
        Wq = jax.random.normal(ks[1], (EMBED_DIM, EMBED_DIM), dtype=jnp.float32) * W_INIT
        Wk = jax.random.normal(ks[2], (EMBED_DIM, EMBED_DIM), dtype=jnp.float32) * W_INIT
        Wv = jax.random.normal(ks[3], (EMBED_DIM, EMBED_DIM), dtype=jnp.float32) * W_INIT
        Wo = jax.random.normal(ks[4], (EMBED_DIM, EMBED_DIM), dtype=jnp.float32) * W_INIT
        bq = jnp.zeros((EMBED_DIM,), jnp.float32)
        bk = jnp.zeros((EMBED_DIM,), jnp.float32)
        bv = jnp.zeros((EMBED_DIM,), jnp.float32)
        bo = jnp.zeros((EMBED_DIM,), jnp.float32)
        phase_modulators = jax.random.normal(ks[5], (WL_CHANNELS, NUM_HEADS), dtype=jnp.float32)
        interference_weights = jnp.ones((WL_CHANNELS,), jnp.float32)
        return {'x': x, 'Wq': Wq, 'bq': bq, 'Wk': Wk, 'bk': bk, 'Wv': Wv, 'bv': bv, 'Wo': Wo, 'bo': bo, 'phase_modulators': phase_modulators, 'interference_weights': interference_weights}
    _L0_attn_in = _L0_attn_setup()

    def _L0_ffn_setup():
        import jax, jax.numpy as jnp
        import numpy as np
        EPS = 1e-05

        def _ln(x, g, b):
            mu = jnp.mean(x, axis=-1, keepdims=True)
            var = jnp.mean(jnp.square(x - mu), axis=-1, keepdims=True)
            return (x - mu) * jax.lax.rsqrt(var + EPS) * g + b

        def _forward(x, index_b, index_t, sw1, sb1, sw2, sb2, sw3, sb3, s_ln_g, s_ln_b, sg_w, sg_b, eg_w, eg_b, exp_bias, ew1, eb1, ew2, eb2, ew3, eb3, sel_ln_g, sel_ln_b):
            x1 = jnp.einsum('btd,hd->bth', x, sw1) + sb1
            x2 = jnp.einsum('btd,hd->bth', x, sw2) + sb2
            sh = _ln(jax.nn.silu(x1) * x2, s_ln_g, s_ln_b)
            shared_out = jnp.einsum('bth,dh->btd', sh, sw3) + sb3
            x_moe = x[index_b, index_t]
            shared_scores = jax.nn.sigmoid(x_moe @ sg_w.T + sg_b)
            expert_scores = jax.nn.sigmoid(x_moe @ eg_w.T + eg_b)
            top1_idx = jnp.argmax(expert_scores + exp_bias, axis=-1)
            top1_score = jnp.take_along_axis(expert_scores, top1_idx[:, None], axis=-1)
            weights = jax.nn.softmax(jnp.concatenate([shared_scores, top1_score], axis=-1), axis=-1)
            shared_w, expert_w = (weights[:, 0], weights[:, 1])
            shared_moe_out = shared_out[index_b, index_t] * shared_w[:, None]
            h1 = jnp.einsum('md,ehd->meh', x_moe, ew1) + eb1
            h2 = jnp.einsum('md,ehd->meh', x_moe, ew2) + eb2
            z = _ln(jax.nn.silu(h1) * h2, sel_ln_g, sel_ln_b)
            out_all = jnp.einsum('meh,edh->med', z, ew3) + eb3
            expert_out = jnp.take_along_axis(out_all, top1_idx[:, None, None], axis=1)[:, 0]
            expert_moe_out = expert_out * expert_w[:, None]
            final_out = shared_out.at[index_b, index_t].set(shared_moe_out + expert_moe_out)
            return final_out
        B, T, D, E, H, M = (2, 256, 128, 8, 64, 256)
        key = jax.random.key(seed)
        ks = jax.random.split(key, 24)
        s = 0.02
        inp = {}
        inp['x'] = jax.random.normal(ks[0], (B, T, D), jnp.float32)
        flat = jnp.arange(M, dtype=jnp.int32) * 2
        inp['index_b'] = flat // T
        inp['index_t'] = flat % T
        inp['sw1'] = jax.random.normal(ks[1], (H, D), jnp.float32) * s
        inp['sb1'] = jnp.zeros((H,), jnp.float32)
        inp['sw2'] = jax.random.normal(ks[2], (H, D), jnp.float32) * s
        inp['sb2'] = jnp.zeros((H,), jnp.float32)
        inp['sw3'] = jax.random.normal(ks[3], (D, H), jnp.float32) * s
        inp['sb3'] = jnp.zeros((D,), jnp.float32)
        inp['s_ln_g'] = jnp.ones((H,), jnp.float32)
        inp['s_ln_b'] = jnp.zeros((H,), jnp.float32)
        inp['sg_w'] = jax.random.normal(ks[4], (1, D), jnp.float32) * s
        inp['sg_b'] = jnp.zeros((1,), jnp.float32)
        inp['eg_w'] = jax.random.normal(ks[5], (E, D), jnp.float32) * s
        inp['eg_b'] = jnp.zeros((E,), jnp.float32)
        inp['exp_bias'] = jnp.zeros((E,), jnp.float32)
        inp['ew1'] = jax.random.normal(ks[6], (E, H, D), jnp.float32) * s
        inp['eb1'] = jnp.zeros((E, H), jnp.float32)
        inp['ew2'] = jax.random.normal(ks[7], (E, H, D), jnp.float32) * s
        inp['eb2'] = jnp.zeros((E, H), jnp.float32)
        inp['ew3'] = jax.random.normal(ks[8], (E, D, H), jnp.float32) * s
        inp['eb3'] = jnp.zeros((E, D), jnp.float32)
        inp['sel_ln_g'] = jnp.ones((H,), jnp.float32)
        inp['sel_ln_b'] = jnp.zeros((H,), jnp.float32)
        return inp
    _L0_ffn_in = _L0_ffn_setup()
    _d = {'L0_attn_x': _L0_attn_in['x'], 'L0_attn_Wq': _L0_attn_in['Wq'], 'L0_attn_bq': _L0_attn_in['bq'], 'L0_attn_Wk': _L0_attn_in['Wk'], 'L0_attn_bk': _L0_attn_in['bk'], 'L0_attn_Wv': _L0_attn_in['Wv'], 'L0_attn_bv': _L0_attn_in['bv'], 'L0_attn_Wo': _L0_attn_in['Wo'], 'L0_attn_bo': _L0_attn_in['bo'], 'L0_attn_phase_modulators': _L0_attn_in['phase_modulators'], 'L0_attn_interference_weights': _L0_attn_in['interference_weights'], 'L0_ffn_index_b': _L0_ffn_in['index_b'], 'L0_ffn_index_t': _L0_ffn_in['index_t'], 'L0_ffn_sw1': _L0_ffn_in['sw1'], 'L0_ffn_sb1': _L0_ffn_in['sb1'], 'L0_ffn_sw2': _L0_ffn_in['sw2'], 'L0_ffn_sb2': _L0_ffn_in['sb2'], 'L0_ffn_sw3': _L0_ffn_in['sw3'], 'L0_ffn_sb3': _L0_ffn_in['sb3'], 'L0_ffn_s_ln_g': _L0_ffn_in['s_ln_g'], 'L0_ffn_s_ln_b': _L0_ffn_in['s_ln_b'], 'L0_ffn_sg_w': _L0_ffn_in['sg_w'], 'L0_ffn_sg_b': _L0_ffn_in['sg_b'], 'L0_ffn_eg_w': _L0_ffn_in['eg_w'], 'L0_ffn_eg_b': _L0_ffn_in['eg_b'], 'L0_ffn_exp_bias': _L0_ffn_in['exp_bias'], 'L0_ffn_ew1': _L0_ffn_in['ew1'], 'L0_ffn_eb1': _L0_ffn_in['eb1'], 'L0_ffn_ew2': _L0_ffn_in['ew2'], 'L0_ffn_eb2': _L0_ffn_in['eb2'], 'L0_ffn_ew3': _L0_ffn_in['ew3'], 'L0_ffn_eb3': _L0_ffn_in['eb3'], 'L0_ffn_sel_ln_g': _L0_ffn_in['sel_ln_g'], 'L0_ffn_sel_ln_b': _L0_ffn_in['sel_ln_b']}
    _x0 = _d['L0_attn_x']
    _d['L0_attn_x'] = jax.random.normal(jax.random.fold_in(jax.random.key(seed), 1), (8, 512, 128), dtype=_x0.dtype)
    del _x0
    return _d

def reference(L0_attn_x, L0_attn_Wq, L0_attn_bq, L0_attn_Wk, L0_attn_bk, L0_attn_Wv, L0_attn_bv, L0_attn_Wo, L0_attn_bo, L0_attn_phase_modulators, L0_attn_interference_weights, L0_ffn_index_b, L0_ffn_index_t, L0_ffn_sw1, L0_ffn_sb1, L0_ffn_sw2, L0_ffn_sb2, L0_ffn_sw3, L0_ffn_sb3, L0_ffn_s_ln_g, L0_ffn_s_ln_b, L0_ffn_sg_w, L0_ffn_sg_b, L0_ffn_eg_w, L0_ffn_eg_b, L0_ffn_exp_bias, L0_ffn_ew1, L0_ffn_eb1, L0_ffn_ew2, L0_ffn_eb2, L0_ffn_ew3, L0_ffn_eb3, L0_ffn_sel_ln_g, L0_ffn_sel_ln_b):

    def _L0_attn_ref(x, Wq, bq, Wk, bk, Wv, bv, Wo, bo, phase_modulators, interference_weights):
        import jax, jax.numpy as jnp
        import numpy as np
        EMBED_DIM = 128
        NUM_HEADS = 16
        HEAD_DIM = EMBED_DIM // NUM_HEADS
        WL_CHANNELS = 16
        BATCH = 1
        SEQ = 128
        KERR = 2.7e-18 * 1000000.0
        SCALE = 1.0 / np.sqrt(HEAD_DIM)
        W_INIT = 0.02
        B, S, E = x.shape
        H, D = (NUM_HEADS, HEAD_DIM)

        def proj(W, b):
            y = jnp.einsum('bse,ef->bsf', x, W) + b
            return y.reshape(B, S, H, D).transpose(0, 2, 1, 3)
        Q = proj(Wq, bq)
        K = proj(Wk, bk)
        V = proj(Wv, bv)
        cos_pm = jnp.cos(phase_modulators)

        def wl_step(acc, wl):
            cpm, iw = wl
            m = cpm[None, :, None, None]
            Qw = Q * m
            Kw = K * m
            scores = jnp.einsum('bhqd,bhkd->bhqk', Qw, Kw) * SCALE
            scores = scores * jnp.cos(KERR * scores * scores)
            attn = jax.nn.softmax(scores, axis=-1)
            out = jnp.einsum('bhqk,bhkd->bhqd', attn, V)
            return (acc + out * iw, None)
        acc0 = jnp.zeros((B, H, S, D), x.dtype)
        acc, _ = jax.lax.scan(wl_step, acc0, (cos_pm, interference_weights))
        combined = acc / WL_CHANNELS
        combined = combined.transpose(0, 2, 1, 3).reshape(B, S, E)
        return jnp.einsum('bse,ef->bsf', combined, Wo) + bo

    def _L0_ffn_ref(x, index_b, index_t, sw1, sb1, sw2, sb2, sw3, sb3, s_ln_g, s_ln_b, sg_w, sg_b, eg_w, eg_b, exp_bias, ew1, eb1, ew2, eb2, ew3, eb3, sel_ln_g, sel_ln_b):
        import jax, jax.numpy as jnp
        import numpy as np
        EPS = 1e-05

        def _ln(x, g, b):
            mu = jnp.mean(x, axis=-1, keepdims=True)
            var = jnp.mean(jnp.square(x - mu), axis=-1, keepdims=True)
            return (x - mu) * jax.lax.rsqrt(var + EPS) * g + b

        def _forward(x, index_b, index_t, sw1, sb1, sw2, sb2, sw3, sb3, s_ln_g, s_ln_b, sg_w, sg_b, eg_w, eg_b, exp_bias, ew1, eb1, ew2, eb2, ew3, eb3, sel_ln_g, sel_ln_b):
            x1 = jnp.einsum('btd,hd->bth', x, sw1) + sb1
            x2 = jnp.einsum('btd,hd->bth', x, sw2) + sb2
            sh = _ln(jax.nn.silu(x1) * x2, s_ln_g, s_ln_b)
            shared_out = jnp.einsum('bth,dh->btd', sh, sw3) + sb3
            x_moe = x[index_b, index_t]
            shared_scores = jax.nn.sigmoid(x_moe @ sg_w.T + sg_b)
            expert_scores = jax.nn.sigmoid(x_moe @ eg_w.T + eg_b)
            top1_idx = jnp.argmax(expert_scores + exp_bias, axis=-1)
            top1_score = jnp.take_along_axis(expert_scores, top1_idx[:, None], axis=-1)
            weights = jax.nn.softmax(jnp.concatenate([shared_scores, top1_score], axis=-1), axis=-1)
            shared_w, expert_w = (weights[:, 0], weights[:, 1])
            shared_moe_out = shared_out[index_b, index_t] * shared_w[:, None]
            h1 = jnp.einsum('md,ehd->meh', x_moe, ew1) + eb1
            h2 = jnp.einsum('md,ehd->meh', x_moe, ew2) + eb2
            z = _ln(jax.nn.silu(h1) * h2, sel_ln_g, sel_ln_b)
            out_all = jnp.einsum('meh,edh->med', z, ew3) + eb3
            expert_out = jnp.take_along_axis(out_all, top1_idx[:, None, None], axis=1)[:, 0]
            expert_moe_out = expert_out * expert_w[:, None]
            final_out = shared_out.at[index_b, index_t].set(shared_moe_out + expert_moe_out)
            return final_out
        return _forward(x, index_b, index_t, sw1, sb1, sw2, sb2, sw3, sb3, s_ln_g, s_ln_b, sg_w, sg_b, eg_w, eg_b, exp_bias, ew1, eb1, ew2, eb2, ew3, eb3, sel_ln_g, sel_ln_b)
    x = L0_attn_x
    x = _layernorm(x + _L0_attn_ref(x, L0_attn_Wq, L0_attn_bq, L0_attn_Wk, L0_attn_bk, L0_attn_Wv, L0_attn_bv, L0_attn_Wo, L0_attn_bo, L0_attn_phase_modulators, L0_attn_interference_weights), axis=-1)
    x = _layernorm(x + _L0_ffn_ref(x, L0_ffn_index_b, L0_ffn_index_t, L0_ffn_sw1, L0_ffn_sb1, L0_ffn_sw2, L0_ffn_sb2, L0_ffn_sw3, L0_ffn_sb3, L0_ffn_s_ln_g, L0_ffn_s_ln_b, L0_ffn_sg_w, L0_ffn_sg_b, L0_ffn_eg_w, L0_ffn_eg_b, L0_ffn_exp_bias, L0_ffn_ew1, L0_ffn_eb1, L0_ffn_ew2, L0_ffn_eb2, L0_ffn_ew3, L0_ffn_eb3, L0_ffn_sel_ln_g, L0_ffn_sel_ln_b), axis=-1)
    return x

_drawn_inputs = setup_inputs


def setup_inputs(seed=0):
    import zlib

    import numpy as np

    out = dict(_drawn_inputs(seed))
    spreads = {'L0_attn_bq': (0.0, 0.8),
     'L0_attn_bk': (0.0, 2.0),
     'L0_attn_bv': (0.0, 0.37),
     'L0_attn_bo': (0.0, 0.1),
     'L0_attn_interference_weights': (1.0, 0.6),
     'L0_ffn_sb1': (0.0, 0.1),
     'L0_ffn_sb2': (0.0, 0.1),
     'L0_ffn_sb3': (0.0, 0.1),
     'L0_ffn_s_ln_g': (1.0, 0.2),
     'L0_ffn_s_ln_b': (0.0, 0.481),
     'L0_ffn_eg_b': (0.0, 0.8),
     'L0_ffn_exp_bias': (0.0, 0.1),
     'L0_ffn_eb1': (0.0, 0.8),
     'L0_ffn_eb2': (0.0, 0.8),
     'L0_ffn_eb3': (0.0, 0.69),
     'L0_ffn_sel_ln_g': (1.0, 0.6),
     'L0_ffn_sel_ln_b': (0.0, 0.8)}
    factors = {'L0_attn_Wq': 8.0,
     'L0_attn_Wk': 8.0,
     'L0_attn_Wv': 8.0,
     'L0_attn_Wo': 2.883,
     'L0_attn_phase_modulators': 8.0,
     'L0_ffn_sg_w': 95.34,
     'L0_ffn_eg_w': 4.593,
     'L0_ffn_ew1': 2.945,
     'L0_ffn_ew2': 2.891,
     'L0_ffn_ew3': 2.697}
    for name, (base, spread) in spreads.items():
        noise = np.random.default_rng([zlib.crc32(name.encode()), seed]).standard_normal(out[name].shape)
        drawn = base * np.exp(spread * noise) if base else spread * noise
        out[name] = jnp.asarray(drawn.astype(out[name].dtype))
    for name, factor in factors.items():
        out[name] = (out[name] * factor).astype(out[name].dtype)
    return out
```

```python
from contextlib import ExitStack

import numpy as np
import concourse.bass as bass
from concourse import mybir

ALU = mybir.AluOpType
ACT = mybir.ActivationFunctionType
AX = mybir.AxisListType
F32 = mybir.dt.float32
F32R = mybir.dt.float32r
I32 = mybir.dt.int32

P = 128
B, S, E = 8, 512, 128
H, D = 16, 8
W = 16
HID = 64
EXPERTS = 8
M = 256
NB = 4
NG = B // NB
T = S // P
GT = NB * T
NT = B * T
UNITS = NG * H
L = 32
SCALE = float(1.0 / np.sqrt(D))
EPS = 1e-5
MAGIC = float(1.5 * 2 ** 23)
TWO_PI_PARTS = (6.28125, 0.0019350051879882812, 3.019916050561733e-07)
RSQRT_MAGIC = float(0x5f3759df)
NEWTON_STEPS = 3

SLOTS = 3
W_GROUPS = [(0, 3), (3, 3), (6, 3), (9, 3), (12, 2), (14, 2)]
NWG = len(W_GROUPS)
FIRST_OF = {w0: g for g, (w0, n) in enumerate(W_GROUPS)}
LAST_OF = {w0 + n - 1: g for g, (w0, n) in enumerate(W_GROUPS)}
SLOT_OF = {w: w - w0 for w0, n in W_GROUPS for w in range(w0, w0 + n)}
R_S = 3 * D
R_AUG = R_S + 2
HIGH_BITS = -4096
PREP_LINKS = 6
A = D + 1
VPAD = (SLOTS - 1) * A

LOOP_TILES, LOOP_CHUNKS = 2, GT // 2
TAIL_TILES, TAIL_CHUNKS = 4, GT // 4
E_LOADS = 16 * 11
MOE_DONE = 7
FF_STEPS = {1: 1, 5: 2, 8: 3, 12: 4, 17: 5, 20: 6, 24: 7}
FF_EXP_STEP = 14


def postln_kernel(nc, a):
    with ExitStack() as ctx:
        def sb(name, shape, dt=F32):
            return ctx.enter_context(nc.sbuf_tensor(name, shape, dt))

        def sem(name):
            return ctx.enter_context(nc.semaphore(name))

        x_group = sb("x_group", [P, NB * S])
        comb = sb("comb", [P, NT, E])
        s_t = sb("s_t", [P, 2, T * NB * S])
        x_rows = s_t[:, 1, 0:NT * E].rearrange("p (j e) -> p j e", e=E)
        probs = sb("probs", [P, 2, T * NB * S])
        weighted = sb("weighted", [P, W, GT * D])
        x_next = weighted[:].rearrange("p w n -> p (w n)")
        o_sb = sb("o_sb", [P, 2, S])
        q_t = sb("q_t", [P, S])
        k_t = sb("k_t", [P, S])
        v_t = sb("v_t", [P, S])
        q_s = sb("q_s", [P, S], F32R)
        k_s = sb("k_s", [P, S], F32R)
        high = sb("high", [P, 2, S])
        low_rows = sb("low_rows", [P, 2, 2])
        m_pad = sb("m_pad", [P, T, P])
        v_pad = sb("v_pad", [P, 2, GT, A + 2 * VPAD])
        r_z = sb("r_z", [P, GT * SLOTS])
        ident = sb("ident", [P, P])
        w_qkv = sb("w_qkv", [P, 3, E])
        b_qkv = sb("b_qkv", [P, 3, H])
        w_head = sb("w_head", [P, 2, 3, L])
        b_head = sb("b_head", [P, 2, 3])
        c2 = sb("c2", [P, W, H])
        c2_head = sb("c2_head", [P, 2, W])
        iw = sb("iw", [P, W])
        half_pi = sb("half_pi", [P, 1])
        pm = probs[:, 1, 0:4 * W * H].rearrange("p (k n) -> p k n", k=4)

        w_o = sb("w_o", [P, E])
        sw12 = sb("sw12", [P, E])
        sw12_t = sb("sw12_t", [P, 2 * HID])
        sw3 = sb("sw3", [P, 2, 2, HID])
        sw3_t = sb("sw3_t", [P, 2, P])
        rows = sb("rows", [P, 5, E])
        BO, SB12, SB3, LN_S, LN_X = range(5)

        class Chunk:

            def __init__(self, name, tiles, at=None):
                self.k, self.name, self.at = tiles, name, at
                self.xr = self.buffer("xr", E)
                self.h = self.xr
                self.xb = self.buffer("xb", E)
                self.tt = self.buffer("tt", E)
                self.y = self.buffer("y", E)
                self.x1 = self.buffer("x1", E)
                self.x1b = self.buffer("x1b", E)
                self.u = self.buffer("u", HID)
                self.e = self.buffer("e", HID)
                self.stats = self.buffer("stats", 6)
                self.mean = self.buffer("mean", 1)
                self.var = self.buffer("var", 1)
                self.rstd = self.buffer("rstd", 1)
                self.nt = self.buffer("nt", 1)

            def buffer(self, field, n):
                if self.at is None:
                    view = sb(f"{self.name}_{field}", [P, self.k * n])[:]
                else:
                    view = self.at[:, 0:self.k * n]
                    self.at = self.at[:, self.k * n:]
                return view.rearrange("p (k n) -> p k n", k=self.k)

        loop_chunk = Chunk("lc", LOOP_TILES)
        comb_chunk = sb("comb_chunk", [P, LOOP_TILES, E])
        flat_probs = probs[:].rearrange("p a n -> p (a n)")
        CHUNK_SIZE = TAIL_TILES * 8 * E
        tail_chunks = [Chunk(f"tc{c}", TAIL_TILES, flat_probs[:, c * CHUNK_SIZE:(c + 1) * CHUNK_SIZE])
                       for c in range(TAIL_CHUNKS)]
        flat_s = s_t[:].rearrange("p a n -> p (a n)")
        taken = [0]

        def scratch(n):
            taken[0] += n
            return flat_s[:, taken[0] - n:taken[0]]

        MT = M // P
        EC = EXPERTS * HID // P
        moe = Chunk("moe", 2 * MT, scratch(2 * MT * 8 * E))
        ew = scratch(3 * EC * P).rearrange("p (i c d) -> p i c d", i=3, c=EC)
        ew_t = scratch((3 * EC + 1) * P).rearrange("p (c d) -> p c d", d=P)
        eb12 = scratch(2 * EXPERTS * HID).rearrange("p (i n) -> p i n", i=2)
        hx = scratch(2 * MT * EXPERTS * HID).rearrange("p (i j n) -> p i j n", i=2, j=MT)
        zx = scratch(MT * (EC + 1) * P).rearrange("p (j c n) -> p j c n", j=MT, c=EC + 1)
        zx_t = scratch(MT * (EC + 1) * P).rearrange("p (j c n) -> p j c n", j=MT, c=EC + 1)
        G = 1 + EXPERTS
        gate_rows = scratch(P)
        gate_t = scratch(G)
        gate_b = scratch(G + EXPERTS)
        gates = scratch(MT * G).rearrange("p (j g) -> p j g", j=MT)
        biased = scratch(MT * EXPERTS).rearrange("p (j g) -> p j g", j=MT)
        chosen = scratch(MT * EXPERTS).rearrange("p (j g) -> p j g", j=MT)
        best = scratch(MT).rearrange("p (j o) -> p j o", o=1)
        pair = scratch(MT * 2).rearrange("p (j g) -> p j g", j=MT)
        order = sb("order", [P, EXPERTS])
        index = sb("index", [P, 3, MT], I32)

        psum = ctx.enter_context(nc.psum_tensor("psum", [P, 8, S], F32))
        prep = psum[:, 0:4, :]
        o_ps = [psum[:, 4, :], psum[:, 5, :]]
        ot_ps = psum[:, 6, :].rearrange("p (j l) -> p j l", l=L)
        misc = psum[:, 7, :]

        names = ("x_loaded x2_loaded sw3_zeroed w_loaded ffw_loaded pm_loaded xg_loaded masks_zeroed b_zeroed masks_ready low_step xn_stored m_ready "
                 "i_loaded i_ready e_loaded e_zeroed ew_turned ew_ready gathered scattered m_pe m_dve m_act "
                 "c2_step cos_done x_turned x_copied staged proj_done qkv_ready scores_done max_done mrow_done "
                 "qa_ready st_done st_copied exp_done pv_done o_copied ot_done rz_done norm_done comb_done prep_chain chain "
                 "ffw_turned ffw_ready xr_loaded xb_ready cs_ready x1_ready x1_stored y2_ready out_stored "
                 "ff_pe1 ff_pe2 ff_pe3 ff_pe4 ff_pe6 ff_pe7 ff_dve1 ff_dve3 ff_dve4 ff_dve5 ff_dve6 ff_exp "
                 "x1b_ready").split()
        s = {n: sem(n) for n in names}

        x_dram = a["L0_attn_x"].rearrange("b (t p) e -> p (b t) e", p=P)
        out_dram = a["out"].rearrange("b (t p) e -> p (b t) e", p=P)
        x1_dram = a["x1"].rearrange("(j p) e -> p j e", p=P)

        def on_all(ap, n):
            return ap.rearrange("(o n) -> o n", o=1).broadcast_to([P, n])

        def chunk_of(c):
            return tail_chunks[c], LOOP_CHUNKS + c, GT + c * TAIL_TILES

        block = ctx.enter_context(nc.Block())

        @block.sync
        def _(sp):
            sp.dma_start(x_rows[:, 0:GT, :], x_dram[:, 0:GT, :]).then_inc(s["x_loaded"], 16)
            sp.dma_start(x_rows[:, GT:NT, :], x_dram[:, GT:NT, :]).then_inc(s["x2_loaded"], 16)
            for i, name in enumerate(("L0_ffn_index_b", "L0_ffn_index_t")):
                sp.dma_start(index[:, i, :], a[name].rearrange("(j p) -> p j", p=P), allow_slow_non_contiguous=True) \
                    .then_inc(s["i_loaded"], 16)
            sp.wait_ge(s["sw3_zeroed"], 1)
            for dst, name in ((w_o[:], "L0_attn_Wo"), (sw12[0:HID, :], "L0_ffn_sw1"), (sw12[HID:P, :], "L0_ffn_sw2"),
                              (sw3[:, 0, 0, :], "L0_ffn_sw3"), (sw3[:, 1, 1, :], "L0_ffn_sw3")):
                sp.dma_start(dst, a[name]).then_inc(s["ffw_loaded"], 16)
            for i, at, name, n in ((BO, 0, "L0_attn_bo", E), (SB12, 0, "L0_ffn_sb1", HID), (SB12, HID, "L0_ffn_sb2", HID),
                                   (SB3, 0, "L0_ffn_sb3", E), (LN_S, 0, "L0_ffn_s_ln_g", HID), (LN_S, HID, "L0_ffn_s_ln_b", HID),
                                   (LN_X, 0, "L0_ffn_sel_ln_g", HID), (LN_X, HID, "L0_ffn_sel_ln_b", HID)):
                sp.dma_start(rows[:, i, at:at + n], on_all(a[name], n)).then_inc(s["ffw_loaded"], 16)
            sp.wait_ge(s["x_copied"], NT // 4)
            sp.dma_start(a["x_next"], x_next).then_inc(s["xn_stored"], 16)
            sp.wait_ge(s["proj_done"], H)
            sp.wait_ge(s["xn_stored"], 16)
            sp.dma_start(x_group[:], a["x_next"]).then_inc(s["xg_loaded"], 16)
            with sp.Fori(0, LOOP_CHUNKS) as k:
                tile = bass.ds(k * LOOP_TILES, LOOP_TILES)
                sp.dma_start(loop_chunk.xr, x_dram[:, tile, :]).then_inc(s["xr_loaded"], 16)
                sp.wait_ge(s["x1_ready"], k + 1)
                sp.dma_start(x1_dram[:, tile, :], loop_chunk.x1).then_inc(s["x1_stored"], 16)
                sp.wait_ge(s["y2_ready"], k + 2)
                sp.dma_start(out_dram[:, tile, :], loop_chunk.y).then_inc(s["out_stored"], 16)
            sp.wait_ge(s["comb_done"], UNITS)
            for c in range(TAIL_CHUNKS):
                ch, k, t0 = chunk_of(c)
                sp.dma_start(ch.xr, x_dram[:, t0:t0 + ch.k, :]).then_inc(s["xr_loaded"], 16)
            for c in range(TAIL_CHUNKS):
                ch, k, t0 = chunk_of(c)
                sp.wait_ge(s["x1_ready"], k + 1)
                sp.dma_start(x1_dram[:, t0:t0 + ch.k, :], ch.x1).then_inc(s["x1_stored"], 16)
            for c in range(TAIL_CHUNKS):
                ch, k, t0 = chunk_of(c)
                sp.wait_ge(s["y2_ready"], k + 2)
                sp.dma_start(out_dram[:, t0:t0 + ch.k, :], ch.y).then_inc(s["out_stored"], 16)
            sp.wait_ge(s["x1_stored"], 16 * (1 + LOOP_CHUNKS + TAIL_CHUNKS))
            sp.wait_ge(s["out_stored"], 16 * (1 + LOOP_CHUNKS + TAIL_CHUNKS))

        @block.gpsimd
        def _(pool):
            nc.gpsimd.memset(ident[:], 0.0).then_inc(s["masks_zeroed"], 1)
            nc.gpsimd.memset(w_head[:], 0.0).then_inc(s["masks_zeroed"], 1)
            pool.wait_ge(s["masks_zeroed"], 2)
            nc.gpsimd.affine_select(out=ident[:], in_=ident[:], compare_op=ALU.not_equal, fill=1.0, base=0,
                                    pattern=[[-1, P]], channel_multiplier=1).then_inc(s["masks_ready"], 1)

            def stage(n, p):
                h = n % H
                for part in range(3):
                    m = 2 if part else 3
                    nc.gpsimd.tensor_copy(w_head[:, p, 0:m, part * D:(part + 1) * D], w_qkv[:, 0:m, bass.ds(h * D, D)])
                nc.gpsimd.tensor_copy(b_head[:, p, :], b_qkv[:, :, bass.ds(h, 1)])
                nc.gpsimd.tensor_copy(c2_head[:, p, :], c2[:, :, bass.ds(h, 1)]).then_inc(s["staged"], 1)

            def add_rows(ch, k, loaded):
                pool.wait_ge(s["xr_loaded"], loaded)
                nc.gpsimd.tensor_tensor(ch.xb, ch.xr, rows[:, BO:BO + 1, :].broadcast_to([P, ch.k, E]), ALU.add) \
                    .then_inc(s["xb_ready"], 1)

            def add_sb3(ch, k):
                pool.wait_ge(s["x1_ready"], k + 1)
                nc.gpsimd.tensor_tensor(ch.x1b, ch.x1, rows[:, SB3:SB3 + 1, :].broadcast_to([P, ch.k, E]), ALU.add) \
                    .then_inc(s["x1b_ready"], 1)

            pool.wait_ge(s["w_loaded"], 16 * 31)
            pool.wait_ge(s["c2_step"], 7)
            stage(0, 0)
            for g in range(NG):
                if g == 1:
                    pool.wait_ge(s["ffw_loaded"], 16 * 13)
                    pool.wait_ge(s["comb_done"], H)
                with pool.Fori(g * H // 2, (g + 1) * H // 2) as i:
                    for half in range(2):
                        pool.wait_ge(s["exp_done"], (i * 2 + half) * W + 1)
                        if g == 1 and half == 0:
                            k = i - H // 2
                            nc.gpsimd.tensor_copy(comb_chunk[:], comb[:, bass.ds(k * LOOP_TILES, LOOP_TILES), :]) \
                                .then_inc(s["cs_ready"], 1)
                        stage(i * 2 + half + 1, 1 - half)
                        if g == 1 and half == 0:
                            add_rows(loop_chunk, k, k * 16 + 16)
                            add_sb3(loop_chunk, k)
            pool.wait_ge(s["xr_loaded"], 16 * (LOOP_CHUNKS + TAIL_CHUNKS))
            for c in range(TAIL_CHUNKS):
                add_rows(*chunk_of(c)[:2], 16 * (LOOP_CHUNKS + TAIL_CHUNKS))
            for c in range(TAIL_CHUNKS):
                add_sb3(*chunk_of(c)[:2])
            pool.wait_ge(s["i_ready"], 1)
            pool.wait_ge(s["x1_stored"], 16 * (1 + LOOP_CHUNKS + TAIL_CHUNKS))
            for j in range(MT):
                pool.indirect_dma_start(moe.x1[:, j, :], None, a["x1"], bass.IndirectOffsetOnAxis(index[:, 2, j:j + 1], 0)) \
                    .then_inc(s["gathered"], 16)
            pool.wait_ge(s["m_dve"], MOE_DONE)
            pool.wait_ge(s["out_stored"], 16 * (1 + LOOP_CHUNKS + TAIL_CHUNKS))
            for j in range(MT):
                pool.indirect_dma_start(a["out"].rearrange("b t e -> (b t) e"), bass.IndirectOffsetOnAxis(index[:, 2, j:j + 1], 0),
                                        moe.y[:, j, :], None).then_inc(s["scattered"], 16)
            pool.wait_ge(s["scattered"], 16 * MT)

        @block.scalar
        def _(act):
            act.dma_start(pm[:, 0, :], on_all(a["L0_attn_phase_modulators"].rearrange("w h -> (w h)"), W * H)) \
                .then_inc(s["pm_loaded"], 16)
            act.dma_start(iw[:], on_all(a["L0_attn_interference_weights"], W)).then_inc(s["pm_loaded"], 16)
            for i, name in enumerate(("L0_attn_Wq", "L0_attn_Wk", "L0_attn_Wv")):
                act.dma_start(w_qkv[:, i, :], a[name]).then_inc(s["w_loaded"], 16)
            act.wait_ge(s["b_zeroed"], 2)
            for i, name in enumerate(("L0_attn_bq", "L0_attn_bk", "L0_attn_bv")):
                for b in range(NB):
                    for part in range(1 if i == 2 else 3):
                        r0 = L * b + D * part
                        act.dma_start(b_qkv[r0:r0 + D, i, :], a[name].rearrange("(h d) -> d h", d=D),
                                      allow_slow_non_contiguous=True).then_inc(s["w_loaded"], 16)
            act.wait_ge(s["c2_step"], 6)
            nc.scalar.activation(pm[:, 3, :], pm[:, 2, :], ACT.Sin, bias=half_pi[:, 0:1], scale=-1.0).then_inc(s["cos_done"], 1)
            act.preload_act_table(ACT.Exp)

            def exp_of_h(ch, k):
                act.wait_ge(s["ff_dve4"], k + 1)
                nc.scalar.activation(ch.e, ch.h[:, :, 0:HID], ACT.Exp, scale=-1.0).then_inc(s["ff_exp"], 1)

            for g in range(NG):
                with act.Fori(g * H // 2, (g + 1) * H // 2) as i:
                    for p in range(2):
                        u = i * 2 + p
                        act.wait_ge(s["st_copied"], u * T + T)
                        act.wait_ge(s["staged"], u + 1)
                        for w in range(W):
                            if g == 1 and p * W + w == FF_EXP_STEP:
                                exp_of_h(loop_chunk, i - H // 2)
                            act.wait_ge(s["pv_done"], u * W + (w + 1))
                            nc.scalar.activation(probs[:, w % 2, :], s_t[:, p, :], ACT.Exp,
                                                 scale=c2_head[:, p, w:w + 1]).then_inc(s["exp_done"], 1)
            act.wait_ge(s["e_zeroed"], 1)
            for dst, src in ((ew[:, 0, :, :], a["L0_ffn_ew1"].rearrange("(c e) h d -> (e h) c d", c=EC)),
                             (ew[:, 1, :, :], a["L0_ffn_ew2"].rearrange("(c e) h d -> (e h) c d", c=EC)),
                             (ew[:, 2, :, :].rearrange("p c (e h) -> p (c e) h", h=HID), a["L0_ffn_ew3"].rearrange("e d h -> d e h")),
                             (ew_t[0:EXPERTS, 3 * EC, :], a["L0_ffn_eb3"]),
                             (eb12[:, 0, :], on_all(a["L0_ffn_eb1"].rearrange("e h -> (e h)"), EXPERTS * HID)),
                             (eb12[:, 1, :], on_all(a["L0_ffn_eb2"].rearrange("e h -> (e h)"), EXPERTS * HID)),
                             (gate_rows[0:1, :], a["L0_ffn_sg_w"]), (gate_rows[1:G, :], a["L0_ffn_eg_w"]),
                             (gate_b[:, 0:1], on_all(a["L0_ffn_sg_b"], 1)), (gate_b[:, 1:G], on_all(a["L0_ffn_eg_b"], EXPERTS)),
                             (gate_b[:, G:G + EXPERTS], on_all(a["L0_ffn_exp_bias"], EXPERTS))):
                act.dma_start(dst, src).then_inc(s["e_loaded"], 16)
            for c in range(TAIL_CHUNKS):
                exp_of_h(*chunk_of(c)[:2])
            act.wait_ge(s["m_dve"], 2)
            nc.scalar.activation(gates, gates, ACT.Exp, scale=-1.0).then_inc(s["m_act"], 1)
            act.wait_ge(s["m_dve"], 3)
            nc.scalar.activation(moe.e, moe.h[:, :, 0:HID], ACT.Exp, scale=-1.0).then_inc(s["m_act"], 1)
            act.wait_ge(s["m_dve"], 4)
            nc.scalar.activation(pair, pair, ACT.Exp).then_inc(s["m_act"], 1)

        class Linked:

            def __init__(self, dve, chain, base):
                self.dve, self.chain, self.base, self.n = dve, chain, base, 0

            def __call__(self, ins):
                self.n += 1
                ins.then_inc(self.chain, 1)
                self.dve.wait_ge(self.chain, self.base + self.n)

        def in_parts(link, which, done):
            for i, src, dst in which:
                last = nc.vector.tensor_scalar(high[:, i, :].bitcast(I32), src[:].bitcast(I32), HIGH_BITS, None, ALU.bitwise_and)
            link(last)
            for i, src, dst in which:
                last = nc.vector.tensor_scalar(high[:, i, :], high[:, i, :], low_rows[:, i, 1:2], None, ALU.mult)
            link(last)
            for i, src, dst in which:
                last = nc.vector.scalar_tensor_tensor(out=dst[:], in0=src[:], scalar=low_rows[:, i, 0:1], in1=high[:, i, :],
                                                      op0=ALU.mult, op1=ALU.add)
            last.then_inc(done, 1)

        def prep_pe(pe, step, n, p, group, first=False):
            def banks(j):
                return psum[:, 4:8, :] if first and j % 2 else prep

            if step == 1:
                pe.wait_ge(s["staged"], n + 1)
                if not first:
                    pe.wait_ge(s["st_copied"], n * T)
                if not first:
                    pe.wait_ge(s["xg_loaded"], group * 16 + 16)
                for i in range(3):
                    for b in range(NB):
                        last = nc.tensor.matmul(prep[L * b:L * b + L, i, :], w_head[:, p, i, :],
                                                x_group[:, b * S:(b + 1) * S], start=True, stop=True)
                last.then_inc(s["proj_done"], 1)
            if 2 <= step < 2 + T:
                qt = step - 2
                if qt == 0 or (first and qt == 1):
                    pe.wait_ge(s["qkv_ready"], n + 1)
                else:
                    pe.wait_ge(s["max_done"], n * T + (qt - 1 if first else qt))
                for b in range(NB):
                    last = nc.tensor.matmul(banks(qt)[:, b, :], q_s[L * b:L * b + R_S, qt * P:(qt + 1) * P],
                                            k_s[L * b:L * b + R_S, :], start=True, stop=True)
                last.then_inc(s["scores_done"], 1)
            if step == 2 + T:
                pe.wait_ge(s["m_ready"], n + 1)
                for qt in range(T):
                    nc.tensor.transpose(prep[:, 1, qt * P:(qt + 1) * P], v_t[:, qt * P:(qt + 1) * P], ident[:])
                for qt in range(T):
                    last = nc.tensor.transpose(prep[:, 0, qt * P:(qt + 1) * P], m_pad[:, qt, :], ident[:])
                last.then_inc(s["mrow_done"], 1)
            if 4 + T <= step < 4 + 2 * T:
                kt = step - 4 - T
                if kt == 0 or (first and kt == 1):
                    pe.wait_ge(s["qa_ready"], n + 1)
                else:
                    pe.wait_ge(s["st_copied"], n * T + (kt - 1 if first else kt))
                for b in range(NB):
                    last = nc.tensor.matmul(banks(kt)[:, b, :], k_s[L * b:L * b + R_AUG, kt * P:(kt + 1) * P],
                                            q_s[L * b:L * b + R_AUG, :], start=True, stop=True)
                last.then_inc(s["st_done"], 1)

        def prep_dve(dve, step, n, p, first=False):
            def banks(j):
                return psum[:, 4:8, :] if first and j % 2 else prep

            if step == 1:
                dve.wait_ge(s["proj_done"], n + 1)
                link = Linked(dve, s["prep_chain"], n * PREP_LINKS)
                nc.vector.tensor_scalar(v_t[:], prep[:, 2, :], b_head[:, p, 2:3], None, ALU.add)
                nc.vector.tensor_scalar(q_t[:], prep[:, 0, :], b_head[:, p, 0:1], SCALE, ALU.add, ALU.mult)
                link(nc.vector.tensor_scalar(k_t[:], prep[:, 1, :], b_head[:, p, 1:2], None, ALU.add))
                in_parts(link, ((0, q_t, q_s), (1, k_t, k_s)), s["qkv_ready"])
            if 2 <= step < 2 + T:
                qt = step - 2
                dve.wait_ge(s["scores_done"], n * T + (qt + 1))
                nc.vector.tensor_reduce(m_pad[:, qt, :].rearrange("p (b l) -> p b l", l=L)[:, :, R_S:R_S + 1],
                                        banks(qt), AX.X, ALU.max, negate=True).then_inc(s["max_done"], 1)
                if qt == T - 1:
                    dve.wait_ge(s["max_done"], n * T + T)
                    cols = m_pad[:].rearrange("p t (b l) -> p t b l", l=L)
                    nc.vector.tensor_copy(cols[:, :, :, R_S + 1], cols[:, :, :, R_S]).then_inc(s["m_ready"], 1)
            if step == 2 + T:
                dve.wait_ge(s["mrow_done"], n + 1)
                nc.vector.tensor_copy(v_pad[:, p, :, VPAD:VPAD + A].rearrange("p (b t) e -> p t b e", b=NB),
                                      prep[:, 1, :].rearrange("p (t b l) -> p t b l", t=T, b=NB)[:, :, :, 0:A])
                link = Linked(dve, s["prep_chain"], n * PREP_LINKS + PREP_LINKS // 2)
                link(nc.vector.tensor_tensor(q_t[:], prep[:, 0, :], q_t[:], ALU.add))
                in_parts(link, ((0, q_t, q_s),), s["qa_ready"])
            if 4 + T <= step < 4 + 2 * T:
                kt = step - 4 - T
                dve.wait_ge(s["st_done"], n * T + (kt + 1))
                nc.vector.tensor_copy(s_t[:, p, kt * NB * S:(kt + 1) * NB * S],
                                      banks(kt).rearrange("p b q -> p (b q)")).then_inc(s["st_copied"], 1)

        def tile_of(bank, j, n=E):
            return bank[:, j * E:j * E + n]

        def ff_pe(pe, stage, ch, k, bank, source=None):
            if stage == 1:
                for j in range(ch.k):
                    last = nc.tensor.transpose(tile_of(bank, j), source[:, j, :], ident[:])
                last.then_inc(s["ff_pe1"], 1)
            if stage == 2:
                pe.wait_ge(s["ff_dve1"], k + 1)
                for j in range(ch.k):
                    last = nc.tensor.matmul(tile_of(bank, j), ch.tt[:, j, :], w_o[:], start=True, stop=True)
                last.then_inc(s["ff_pe2"], 1)
            if stage == 3:
                pe.wait_ge(s["x1_ready"], k + 1)
                for j in range(ch.k):
                    last = nc.tensor.transpose(tile_of(bank, j), ch.x1[:, j, :], ident[:])
                last.then_inc(s["ff_pe3"], 1)
            if stage == 4:
                pe.wait_ge(s["ff_dve3"], k + 1)
                for j in range(ch.k):
                    last = nc.tensor.matmul(tile_of(bank, j), ch.tt[:, j, :], sw12_t[:], start=True, stop=True)
                last.then_inc(s["ff_pe4"], 1)
            if stage == 6:
                pe.wait_ge(s["ff_dve5"], k + 1)
                for j in range(ch.k // 2):
                    last = nc.tensor.transpose(tile_of(bank, j), ch.u[:, 2 * j:2 * j + 2, :].rearrange("p a h -> p (a h)"),
                                               ident[:])
                last.then_inc(s["ff_pe6"], 1)
            if stage == 7:
                pe.wait_ge(s["ff_dve6"], k + 1)
                for j in range(ch.k):
                    last = nc.tensor.matmul(tile_of(bank, j), ch.tt[:, j // 2, :], sw3_t[:, j % 2, :], start=True, stop=True)
                last.then_inc(s["ff_pe7"], 1)

        def silu_times(link, ch):
            nc.vector.tensor_tensor(ch.u, ch.h[:, :, 0:HID], ch.h[:, :, HID:E], ALU.mult)
            link(nc.vector.tensor_scalar(ch.e, ch.e, 1.0, None, ALU.add))
            link(nc.vector.reciprocal(ch.e, ch.e))
            link(nc.vector.tensor_tensor(ch.u, ch.u, ch.e, ALU.mult))

        def normalised(link, ch, src, n, dst, done=None, tiles=None):
            for j in range(tiles or ch.k):
                last = nc.vector.bn_stats(ch.stats[:, j, :], src[:, j, :])
            link(last)
            var, y, t = ch.var, ch.rstd, ch.nt
            mean_e, sq_e, mean_o, sq_o = (ch.stats[:, :, i:i + 1] for i in (1, 2, 4, 5))
            nc.vector.tensor_tensor(ch.mean, mean_e, mean_o, ALU.add)
            nc.vector.tensor_tensor(t, mean_e, mean_o, ALU.subtract)
            link(nc.vector.tensor_tensor(var, sq_e, sq_o, ALU.add))
            nc.vector.tensor_scalar(ch.mean, ch.mean, 0.5, None, ALU.mult)
            nc.vector.tensor_scalar(var, var, 1.0 / n, EPS, ALU.mult, ALU.add)
            link(nc.vector.scalar_tensor_tensor(out=y, in0=t, scalar=0.25, in1=t, op0=ALU.mult, op1=ALU.mult))
            link(nc.vector.tensor_tensor(var, var, y, ALU.add))
            link(nc.vector.tensor_scalar(t.bitcast(I32), var.bitcast(I32), 1, None, ALU.logical_shift_right))
            link(nc.vector.tensor_scalar(y.bitcast(I32), t.bitcast(I32), -1.0, RSQRT_MAGIC, ALU.mult, ALU.add))
            for _ in range(NEWTON_STEPS):
                link(nc.vector.scalar_tensor_tensor(out=t, in0=y, scalar=-0.5, in1=y, op0=ALU.mult, op1=ALU.mult))
                link(nc.vector.tensor_tensor(t, t, var, ALU.mult))
                link(nc.vector.scalar_tensor_tensor(out=y, in0=t, scalar=1.5, in1=y, op0=ALU.add, op1=ALU.mult))
            for j in range(tiles or ch.k):
                last = nc.vector.tensor_scalar(dst[:, j, :], src[:, j, :], ch.mean[:, j, :], ch.rstd[:, j, :],
                                               ALU.subtract, ALU.mult)
            if done is not None:
                last.then_inc(done, 1)
            else:
                link(last)

        def ff_dve(dve, stage, ch, k, bank, link):
            src = bank[:, 0:ch.k * E].rearrange("p (k e) -> p k e", e=E)
            if stage == 1:
                dve.wait_ge(s["ff_pe1"], k + 1)
                nc.vector.tensor_copy(ch.tt, src).then_inc(s["ff_dve1"], 1)
            if stage == 2:
                dve.wait_ge(s["ff_pe2"], k + 1)
                dve.wait_ge(s["xb_ready"], k + 1)
                if ch is loop_chunk:
                    dve.wait_ge(s["x1_stored"], k * 16 + 16)
                    dve.wait_ge(s["out_stored"], k * 16 + 16)
                link(nc.vector.tensor_tensor(ch.y, src, ch.xb, ALU.add))
                normalised(link, ch, ch.y, E, ch.x1, s["x1_ready"])
            if stage == 3:
                dve.wait_ge(s["ff_pe3"], k + 1)
                nc.vector.tensor_copy(ch.tt, src).then_inc(s["ff_dve3"], 1)
            if stage == 4:
                dve.wait_ge(s["ff_pe4"], k + 1)
                nc.vector.tensor_tensor(ch.h, src, rows[:, SB12:SB12 + 1, :].broadcast_to([P, ch.k, E]), ALU.add) \
                    .then_inc(s["ff_dve4"], 1)
            if stage == 5:
                dve.wait_ge(s["ff_exp"], k + 1)
                silu_times(link, ch)
                normalised(link, ch, ch.u, HID, ch.u)
                link(nc.vector.tensor_tensor(ch.u, ch.u, rows[:, LN_S:LN_S + 1, 0:HID].broadcast_to([P, ch.k, HID]), ALU.mult))
                nc.vector.tensor_tensor(ch.u, ch.u, rows[:, LN_S:LN_S + 1, HID:E].broadcast_to([P, ch.k, HID]), ALU.add) \
                    .then_inc(s["ff_dve5"], 1)
            if stage == 6:
                dve.wait_ge(s["ff_pe6"], k + 1)
                nc.vector.tensor_copy(ch.tt[:, 0:ch.k // 2, :], src[:, 0:ch.k // 2, :]).then_inc(s["ff_dve6"], 1)
            if stage == 7:
                dve.wait_ge(s["ff_pe7"], k + 1)
                dve.wait_ge(s["x1b_ready"], k + 1)
                link(nc.vector.tensor_tensor(ch.xb, src, ch.x1b, ALU.add))
                normalised(link, ch, ch.xb, E, ch.y, s["y2_ready"])

        LINKS_2 = 1 + 6 + 3 * NEWTON_STEPS
        LINKS_5 = 3 + 6 + 3 * NEWTON_STEPS + 1 + 1
        CHUNK_LINKS = 2 * LINKS_2 + LINKS_5
        STAGES = (1, 2, 3, 4, 5, 6, 7)

        def tail_bank(stage, c):
            return psum[:, 4 * (stage % 2) + c, :]

        def experts_weights_pe(pe):
            pe.wait_ge(s["e_loaded"], E_LOADS)
            for i in range(3):
                for c in range(EC):
                    nc.tensor.transpose(tile_of(psum[:, 4 + i, :], c), ew[:, i, c, :], ident[:])
            nc.tensor.transpose(psum[:, 7, 0:G], gate_rows[0:G, :], ident[0:G, 0:G]).then_inc(s["ew_turned"], 1)

        def experts_weights_dve(dve):
            dve.wait_ge(s["ew_turned"], 1)
            for i in range(3):
                nc.vector.tensor_copy(ew_t[:, i * EC:(i + 1) * EC, :].rearrange("p c d -> p (c d)"), psum[:, 4 + i, :])
            nc.vector.tensor_copy(gate_t, psum[:, 7, 0:G]).then_inc(s["ew_ready"], 1)

        def experts_pe(pe):
            pe.wait_ge(s["gathered"], 16 * MT)
            for j in range(MT):
                last = nc.tensor.transpose(tile_of(psum[:, 0, :], j), moe.x1[:, j, :], ident[:])
            last.then_inc(s["m_pe"], 1)
            pe.wait_ge(s["m_dve"], 1)
            for j in range(MT):
                nc.tensor.matmul(psum[:, 1, j * G:(j + 1) * G], moe.tt[:, j, :], gate_t, start=True, stop=True)
            for j in range(MT):
                last = nc.tensor.matmul(tile_of(psum[:, 2, :], j), moe.tt[:, j, :], sw12_t[:], start=True, stop=True)
            last.then_inc(s["m_pe"], 1)
            for i in range(2):
                for j in range(MT):
                    last = nc.tensor.matmul(psum[:, 4 + 2 * i + j, :], moe.tt[:, j, :],
                                            ew_t[:, i * EC:(i + 1) * EC, :].rearrange("p c d -> p (c d)"), start=True, stop=True)
            last.then_inc(s["m_pe"], 1)
            pe.wait_ge(s["m_dve"], 5)
            nc.tensor.transpose(psum[:, 0, 0:P], moe.u[:, 0:MT, :].rearrange("p a h -> p (a h)"), ident[:])
            for j in range(MT):
                for c in range(EC):
                    nc.tensor.transpose(tile_of(psum[:, 1 + j, :], c), zx[:, j, c, :], ident[:])
                last = nc.tensor.transpose(tile_of(psum[:, 3, :], j), zx[:, j, EC, :], ident[:])
            last.then_inc(s["m_pe"], 1)
            pe.wait_ge(s["m_dve"], 6)
            for j in range(MT):
                nc.tensor.matmul(tile_of(psum[:, 4, :], j), moe.tt[:, 0, :], sw3_t[:, j, :], start=True, stop=True)
            for j in range(MT):
                for c in range(EC + 1):
                    last = nc.tensor.matmul(tile_of(psum[:, 5, :], j), zx_t[:, j, c, :], ew_t[:, 2 * EC + c, :],
                                            start=(c == 0), stop=(c == EC))
            last.then_inc(s["m_pe"], 1)

        def experts_dve(dve, link):
            def wide(ap, n):
                return ap.broadcast_to([P, MT, n])

            def two(bank):
                return bank[:, 0:MT * E].rearrange("p (j e) -> p j e", e=E)

            def by_expert(ap):
                return ap.rearrange("p j (e h) -> p j e h", h=HID)

            dve.wait_ge(s["m_pe"], 1)
            nc.vector.tensor_copy(moe.tt[:, 0:MT, :], two(psum[:, 0, :])).then_inc(s["m_dve"], 1)
            dve.wait_ge(s["m_pe"], 2)
            nc.vector.tensor_tensor(gates, psum[:, 1, 0:MT * G].rearrange("p (j g) -> p j g", g=G),
                                    wide(gate_b[:, 0:G].rearrange("p (o g) -> p o g", o=1), G), ALU.add).then_inc(s["m_dve"], 1)
            nc.vector.tensor_tensor(moe.h[:, 0:MT, :], two(psum[:, 2, :]), wide(rows[:, SB12:SB12 + 1, :], E), ALU.add)
            dve.wait_ge(s["m_pe"], 3)
            for i in range(2):
                last = nc.vector.tensor_tensor(hx[:, i, :, :], psum[:, 4 + 2 * i:6 + 2 * i, :],
                                               wide(eb12[:, i:i + 1, :], EXPERTS * HID), ALU.add)
            link(last)
            dve.wait_ge(s["m_act"], 1)
            link(nc.vector.tensor_scalar(gates, gates, 1.0, None, ALU.add))
            link(nc.vector.reciprocal(gates, gates))
            scores = gates[:, :, 1:G]
            link(nc.vector.tensor_tensor(biased, scores, wide(gate_b[:, G:G + EXPERTS].rearrange("p (o g) -> p o g", o=1), EXPERTS),
                                         ALU.add))
            link(nc.vector.tensor_reduce(best, biased, AX.X, ALU.max))
            link(nc.vector.tensor_tensor(chosen, biased, best.broadcast_to([P, MT, EXPERTS]), ALU.is_ge))
            link(nc.vector.tensor_tensor(chosen, chosen, wide(order[:].rearrange("p (o g) -> p o g", o=1), EXPERTS), ALU.mult))
            link(nc.vector.tensor_reduce(best, chosen, AX.X, ALU.max))
            link(nc.vector.tensor_tensor(chosen, chosen, best.broadcast_to([P, MT, EXPERTS]), ALU.is_equal))
            mask = chosen.rearrange("p j (e o) -> p j e o", o=1).broadcast_to([P, MT, EXPERTS, HID])
            for i in range(2):
                last = nc.vector.tensor_tensor(by_expert(hx[:, i, :, :]), by_expert(hx[:, i, :, :]), mask, ALU.mult)
            link(last)
            for i in range(2):
                last = nc.vector.tensor_reduce(moe.h[:, MT:2 * MT, i * HID:(i + 1) * HID],
                                               hx[:, i, :, :].rearrange("p j (e h) -> p j h e", h=HID), AX.X, ALU.add)
            last.then_inc(s["m_dve"], 1)
            link(nc.vector.tensor_tensor(biased, scores, chosen, ALU.mult))
            nc.vector.tensor_copy(pair[:, :, 0:1], gates[:, :, 0:1])
            link(nc.vector.tensor_reduce(pair[:, :, 1:2], biased, AX.X, ALU.add))
            link(nc.vector.tensor_reduce(best, pair, AX.X, ALU.max))
            nc.vector.tensor_tensor(pair, pair, best.broadcast_to([P, MT, 2]), ALU.subtract).then_inc(s["m_dve"], 1)
            dve.wait_ge(s["m_act"], 2)
            silu_times(link, moe)
            normalised(link, moe, moe.u, HID, moe.u)
            for part, gain in ((0, LN_S), (1, LN_X)):
                u = moe.u[:, part * MT:(part + 1) * MT, :]
                last = nc.vector.tensor_tensor(u, u, wide(rows[:, gain:gain + 1, 0:HID], HID), ALU.mult)
            link(last)
            for part, gain in ((0, LN_S), (1, LN_X)):
                u = moe.u[:, part * MT:(part + 1) * MT, :]
                last = nc.vector.tensor_tensor(u, u, wide(rows[:, gain:gain + 1, HID:E], HID), ALU.add)
            link(last)
            for j in range(MT):
                nc.vector.tensor_tensor(zx[:, j, 0:EC, :].rearrange("p c (e h) -> p (c e) h", h=HID), mask[:, j, :, :],
                                        moe.u[:, MT + j:MT + j + 1, :].broadcast_to([P, EXPERTS, HID]), ALU.mult)
            nc.vector.tensor_copy(zx[:, :, EC, 0:EXPERTS], chosen).then_inc(s["m_dve"], 1)
            dve.wait_ge(s["m_act"], 3)
            link(nc.vector.tensor_reduce(best, pair, AX.X, ALU.add))
            link(nc.vector.reciprocal(best, best))
            link(nc.vector.tensor_tensor(pair, pair, best.broadcast_to([P, MT, 2]), ALU.mult))
            dve.wait_ge(s["m_pe"], 4)
            nc.vector.tensor_copy(moe.tt[:, 0, :], psum[:, 0, 0:P])
            for j in range(MT):
                nc.vector.tensor_copy(zx_t[:, j, 0:EC, :].rearrange("p c n -> p (c n)"), psum[:, 1 + j, :])
            nc.vector.tensor_copy(zx_t[:, :, EC, :], two(psum[:, 3, :])).then_inc(s["m_dve"], 1)
            dve.wait_ge(s["m_pe"], 5)
            link(nc.vector.tensor_tensor(moe.xb[:, 0:MT, :], two(psum[:, 4, :]), wide(rows[:, SB3:SB3 + 1, :], E), ALU.add))
            for j in range(MT):
                last = nc.vector.scalar_tensor_tensor(out=moe.xb[:, j, :], in0=moe.xb[:, j, :], scalar=pair[:, j, 0:1],
                                                      in1=moe.x1[:, j, :], op0=ALU.mult, op1=ALU.add)
            link(last)
            for j in range(MT):
                last = nc.vector.scalar_tensor_tensor(out=moe.xb[:, j, :], in0=tile_of(psum[:, 5, :], j), scalar=pair[:, j, 1:2],
                                                      in1=moe.xb[:, j, :], op0=ALU.mult, op1=ALU.add)
            link(last)
            normalised(link, moe, moe.xb, E, moe.y, s["m_dve"], tiles=MT)

        @block.tensor
        def _(pe):
            def turn_x(g):
                pe.wait_ge(s["x_loaded" if g == 0 else "x2_loaded"], 16)
                for q in range(4):
                    n = g * 4 + q
                    if q >= 2:
                        pe.wait_ge(s["x_copied"], n - 1)
                    for j in range(4):
                        last = nc.tensor.transpose(psum[:, 4 + q % 2, j * P:(j + 1) * P], x_rows[:, n * 4 + j, :], ident[:])
                    last.then_inc(s["x_turned"], 1)

            pe.wait_ge(s["masks_ready"], 1)
            turn_x(0)
            pe.wait_ge(s["x_copied"], 4)
            for step in range(W):
                prep_pe(pe, step, 0, 0, 0, first=True)
            pe.wait_ge(s["st_copied"], T)
            turn_x(1)
            pe.wait_ge(s["ffw_loaded"], 16 * 13)
            pe.wait_ge(s["x_copied"], 8)
            nc.tensor.transpose(psum[:, 7, 0:P], sw12[:], ident[:])
            nc.tensor.transpose(psum[:, 7, P:2 * P], sw3[:, 0, :, :].rearrange("p a h -> p (a h)"), ident[:])
            nc.tensor.transpose(psum[:, 7, 2 * P:3 * P], sw3[:, 1, :, :].rearrange("p a h -> p (a h)"), ident[:]) \
                .then_inc(s["ffw_turned"], 1)

            for g in range(NG):
                with pe.Fori(g * H // 2, (g + 1) * H // 2) as i:
                    for p in range(2):
                        u = i * 2 + p

                        def turn_products(wg):
                            n1 = u * NWG + (wg + 1)
                            pe.wait_ge(s["o_copied"], n1 + 2)
                            pe.wait_ge(s["norm_done"], n1)
                            for qt in range(T):
                                last = nc.tensor.transpose(psum[:, 6, qt * P:(qt + 1) * P],
                                                           o_sb[:, wg % 2, qt * P:(qt + 1) * P], ident[:])
                            last.then_inc(s["ot_done"], 1)

                        for w in range(W):
                            pe.wait_ge(s["exp_done"], u * W + (w + 1))
                            if w in FIRST_OF:
                                wg = FIRST_OF[w]
                                pe.wait_ge(s["o_copied"], u * NWG + (wg + 1))
                            c0 = VPAD - A * SLOT_OF[w]
                            for kt in range(T):
                                for b in range(NB):
                                    at = (kt * NB + b) * S
                                    last = nc.tensor.matmul(
                                        o_ps[wg % 2][L * b:L * b + SLOTS * A, :], v_pad[:, p, b * T + kt, c0:c0 + SLOTS * A],
                                        probs[:, w % 2, at:at + S], start=(kt == 0 and w in FIRST_OF),
                                        stop=(kt == T - 1 and w in LAST_OF))
                            last.then_inc(s["pv_done"], 1)
                            prep_pe(pe, w, u + 1, 1 - p, 1 if g == 1 else (i * 2 + p + 1) // H)
                            if g == 1 and p * W + w in FF_STEPS:
                                stage = FF_STEPS[p * W + w]
                                if stage == 1:
                                    pe.wait_ge(s["cs_ready"], i - H // 2 + 1)
                                    pe.wait_ge(s["y2_ready"], i - H // 2 + 1)
                                ff_pe(pe, stage, loop_chunk, i - H // 2, misc, comb_chunk)
                            if w in FIRST_OF and w > 0:
                                turn_products(wg - 1)
                        turn_products(NWG - 1)

            pe.wait_ge(s["comb_done"], UNITS)
            pe.wait_ge(s["y2_ready"], LOOP_CHUNKS + 1)
            for stage in STAGES:
                if stage == 3:
                    experts_weights_pe(pe)
                    pe.wait_ge(s["ew_ready"], 1)
                for c in range(TAIL_CHUNKS):
                    ch, k, t0 = chunk_of(c)
                    ff_pe(pe, stage, ch, k, tail_bank(stage, c), comb[:, t0:t0 + ch.k, :])
            pe.wait_ge(s["y2_ready"], LOOP_CHUNKS + TAIL_CHUNKS + 1)
            experts_pe(pe)

        @block.vector
        def _(dve):
            nc.vector.memset(b_qkv[:, 0, :], 0.0).then_inc(s["b_zeroed"], 1)
            nc.vector.memset(b_qkv[:, 1:3, :], 1.0).then_inc(s["b_zeroed"], 1)
            nc.vector.memset(sw3[:], 0.0).then_inc(s["sw3_zeroed"], 1)
            nc.vector.memset(half_pi[:], float(np.pi / 2))
            nc.vector.memset(m_pad[:], 0.0).then_inc(s["xg_loaded"], 16)
            nc.vector.memset(v_pad[:], 0.0)
            nc.vector.memset(r_z[:], 0.0).then_inc(s["pv_done"], 2)
            nc.vector.memset(o_sb[:, 0, 0:1], 0.0).then_inc(s["norm_done"], 1)
            nc.vector.memset(loop_chunk.nt, 0.0).then_inc(s["y2_ready"], 1)
            nc.vector.memset(loop_chunk.rstd, 0.0).then_inc(s["x1_stored"], 16)
            nc.vector.memset(loop_chunk.mean, 0.0).then_inc(s["out_stored"], 16)
            for e in range(EXPERTS):
                nc.vector.memset(order[:, e:e + 1], float(EXPERTS - e))
            dve.wait_ge(s["i_loaded"], 32)
            nc.vector.scalar_tensor_tensor(out=index[:, 2, :], in0=index[:, 0, :], scalar=float(S), in1=index[:, 1, :],
                                           op0=ALU.mult, op1=ALU.add).then_inc(s["i_ready"], 1)
            dve.wait_ge(s["masks_ready"], 1)
            link = Linked(dve, s["low_step"], 0)
            by_batch = ident[:].rearrange("p (b l) -> p b l", l=L)
            nc.vector.tensor_reduce(low_rows[:, 0, 0:1], by_batch[:, :, 2 * D:3 * D], AX.XY, ALU.add)
            nc.vector.tensor_reduce(low_rows[:, 0, 1:2], by_batch[:, :, R_S + 1:R_S + 2], AX.XY, ALU.add)
            link(nc.vector.tensor_reduce(low_rows[:, 1, 0:1], by_batch[:, :, D:2 * D], AX.XY, ALU.add))
            link(nc.vector.tensor_tensor(low_rows[:, 0, 0:1], low_rows[:, 0, 0:1], low_rows[:, 0, 1:2], ALU.add))
            link(nc.vector.tensor_scalar(low_rows[:, :, 1:2], low_rows[:, :, 0:1], -2.0, 1.0, ALU.mult, ALU.add))
            dve.wait_ge(s["pm_loaded"], 32)
            nc.vector.tensor_scalar(iw[:], iw[:], 1.0 / W, None, ALU.mult)
            nc.vector.tensor_scalar(pm[:, 1, :], pm[:, 0, :], float(1 / (2 * np.pi)), MAGIC, ALU.mult, ALU.add).then_inc(s["c2_step"], 1)
            dve.wait_ge(s["c2_step"], 1)
            nc.vector.tensor_scalar(pm[:, 1, :], pm[:, 1, :], MAGIC, None, ALU.subtract).then_inc(s["c2_step"], 1)
            dve.wait_ge(s["c2_step"], 2)
            for i, part in enumerate(TWO_PI_PARTS):
                nc.vector.scalar_tensor_tensor(out=pm[:, 0, :], in0=pm[:, 1, :], scalar=-part, in1=pm[:, 0, :],
                                               op0=ALU.mult, op1=ALU.add).then_inc(s["c2_step"], 1)
                dve.wait_ge(s["c2_step"], 3 + i)
            nc.vector.scalar_tensor_tensor(out=pm[:, 2, :], in0=pm[:, 0, :], scalar=-1.0, in1=pm[:, 0, :],
                                           op0=ALU.mult, op1=ALU.max).then_inc(s["c2_step"], 1)
            dve.wait_ge(s["cos_done"], 1)
            nc.vector.tensor_tensor(c2[:].rearrange("p w h -> p (w h)"), pm[:, 3, :], pm[:, 3, :], ALU.mult).then_inc(s["c2_step"], 1)

            def copy_x(g):
                for q in range(4):
                    dve.wait_ge(s["x_turned"], g * 4 + q + 1)
                    nc.vector.tensor_copy((x_group[:], x_next)[g][:, q * S:(q + 1) * S], psum[:, 4 + q % 2, :]).then_inc(s["x_copied"], 1)

            copy_x(0)
            for step in range(W):
                prep_dve(dve, step, 0, 0, first=True)
            copy_x(1)
            dve.wait_ge(s["x_copied"], 8)
            nc.vector.memset(psum[:, 4:6, :], 0.0).then_inc(s["o_copied"], 2)
            dve.wait_ge(s["xn_stored"], 16)
            dve.wait_ge(s["ffw_turned"], 1)
            nc.vector.tensor_copy(sw12_t[:], psum[:, 7, 0:P])
            nc.vector.tensor_copy(sw3_t[:].rearrange("p a n -> p (a n)"), psum[:, 7, P:3 * P]).then_inc(s["ffw_ready"], 1)

            for g in range(NG):
                with dve.Fori(g * H // 2, (g + 1) * H // 2) as i:
                    link = Linked(dve, s["chain"], (i - H // 2) * CHUNK_LINKS)
                    for p in range(2):
                        u = i * 2 + p

                        def weigh(wg):
                            w0, n = W_GROUPS[wg]
                            n1 = u * NWG + (wg + 1)
                            dve.wait_ge(s["ot_done"], n1)
                            ot = ot_ps[:, :, 0:n * A].rearrange("p j (r e) -> p j r e", e=A)
                            rz = r_z[:, 0:GT * n].rearrange("p (j r) -> p j r", r=n)
                            nc.vector.reciprocal(rz, ot[:, :, :, D]).then_inc(s["rz_done"], 1)
                            dve.wait_ge(s["rz_done"], n1 * 2 - 1)
                            nc.vector.tensor_tensor(rz, rz, iw[:, w0:w0 + n].rearrange("p (o r) -> p o r", o=1)
                                                    .broadcast_to([P, GT, n]), ALU.mult).then_inc(s["rz_done"], 1)
                            dve.wait_ge(s["rz_done"], n1 * 2)
                            nc.vector.tensor_tensor(
                                weighted[:, w0:w0 + n, :].rearrange("p r (j d) -> p j r d", d=D), ot[:, :, :, 0:D],
                                rz.rearrange("p j (r o) -> p j r o", o=1).broadcast_to([P, GT, n, D]),
                                ALU.mult).then_inc(s["norm_done"], 1)

                        for w in range(W):
                            if w in LAST_OF:
                                wg = LAST_OF[w]
                                dve.wait_ge(s["pv_done"], u * W + (w + 3))
                                nc.vector.tensor_copy(o_sb[:, wg % 2, :], o_ps[wg % 2]).then_inc(s["o_copied"], 1)
                            prep_dve(dve, w, u + 1, 1 - p)
                            if w in FIRST_OF and w > 0:
                                weigh(FIRST_OF[w] - 1)
                            m = p * W + w
                            if g == 1 and m in FF_STEPS:
                                ff_dve(dve, FF_STEPS[m], loop_chunk, i - H // 2, misc, link)
                        weigh(NWG - 1)
                        dve.wait_ge(s["norm_done"], u * NWG + (NWG + 1))
                        nc.vector.tensor_reduce(
                            comb[:, bass.ds(g * GT, GT), bass.ds((u - g * H) * D, D)].rearrange("p (b t) e -> p t b e", b=NB),
                            weighted[:].rearrange("p w (t b d) -> p t b d w", t=T, b=NB), AX.X, ALU.add) \
                            .then_inc(s["comb_done"], 1)
                    if g == 1:
                        assert link.n == CHUNK_LINKS, (link.n, CHUNK_LINKS)
            link = Linked(dve, s["chain"], LOOP_CHUNKS * CHUNK_LINKS)
            nc.vector.memset(zx, 0.0)
            nc.vector.memset(ew_t[:, 3 * EC, :], 0.0).then_inc(s["e_zeroed"], 1)
            for stage in STAGES:
                if stage == 3:
                    experts_weights_dve(dve)
                for c in range(TAIL_CHUNKS):
                    ch, k, t0 = chunk_of(c)
                    ff_dve(dve, stage, ch, k, tail_bank(stage, c), link)
            experts_dve(dve, link)


_INS = ['L0_attn_x', 'L0_attn_Wq', 'L0_attn_bq', 'L0_attn_Wk', 'L0_attn_bk', 'L0_attn_Wv', 'L0_attn_bv', 'L0_attn_Wo',
        'L0_attn_bo', 'L0_attn_phase_modulators', 'L0_attn_interference_weights', 'L0_ffn_index_b', 'L0_ffn_index_t',
        'L0_ffn_sw1', 'L0_ffn_sb1', 'L0_ffn_sw2', 'L0_ffn_sb2', 'L0_ffn_sw3', 'L0_ffn_sb3', 'L0_ffn_s_ln_g',
        'L0_ffn_s_ln_b', 'L0_ffn_sg_w', 'L0_ffn_sg_b', 'L0_ffn_eg_w', 'L0_ffn_eg_b', 'L0_ffn_exp_bias', 'L0_ffn_ew1',
        'L0_ffn_eb1', 'L0_ffn_ew2', 'L0_ffn_eb2', 'L0_ffn_ew3', 'L0_ffn_eb3', 'L0_ffn_sel_ln_g', 'L0_ffn_sel_ln_b']
_OUT = (8, 512, 128)


def kernel(**inputs):
    import numpy as _np
    import concourse.bacc as _bacc
    from concourse import mybir as _mybir
    from concourse.bass_utils import run_bass_kernel_spmd as _run

    nc = _bacc.Bacc("TRN2", target_bir_lowering=False, num_devices=1)
    arrays, args = {}, {}
    for name in _INS:
        x = _np.ascontiguousarray(inputs[name])
        arrays[f"in_{name}_dram"] = x
        args[name] = nc.dram_tensor(f"in_{name}_dram", x.shape, _mybir.dt.from_np(x.dtype), kind="ExternalInput").ap()
    args["x1"] = nc.dram_tensor("x1_dram", (4096, 128), _mybir.dt.float32, kind="Internal").ap()
    args["x_next"] = nc.dram_tensor("x_next_dram", (128, 2048), _mybir.dt.float32, kind="Internal").ap()
    args["out"] = nc.dram_tensor("out_0_dram", _OUT, _mybir.dt.float32, kind="ExternalOutput").ap()
    postln_kernel(nc, args)
    r = _run(nc, [arrays], core_ids=[0])
    return r.results[0]["out_0_dram"]
```

```python
from contextlib import ExitStack

import numpy as np
import concourse.bass as bass
from concourse import mybir

ALU = mybir.AluOpType
ACT = mybir.ActivationFunctionType
AX = mybir.AxisListType
F32 = mybir.dt.float32
F32R = mybir.dt.float32r
I32 = mybir.dt.int32

P = 128
B, S, E = 8, 512, 128
H, D = 16, 8
W = 16
HID = 64
EXPERTS = 8
M = 256
NB = 4
NG = B // NB
T = S // P
GT = NB * T
NT = B * T
UNITS = NG * H
L = 32
SCALE = float(1.0 / np.sqrt(D))
EPS = 1e-5
MAGIC = float(1.5 * 2 ** 23)
TWO_PI_PARTS = (6.28125, 0.0019350051879882812, 3.019916050561733e-07)
RSQRT_MAGIC = float(0x5f3759df)
NEWTON_STEPS = 3

SLOTS = 3
W_GROUPS = [(0, 3), (3, 3), (6, 3), (9, 3), (12, 2), (14, 2)]
NWG = len(W_GROUPS)
FIRST_OF = {w0: g for g, (w0, n) in enumerate(W_GROUPS)}
LAST_OF = {w0 + n - 1: g for g, (w0, n) in enumerate(W_GROUPS)}
SLOT_OF = {w: w - w0 for w0, n in W_GROUPS for w in range(w0, w0 + n)}
R_S = 3 * D
R_AUG = R_S + 2
HIGH_BITS = -4096
PREP_LINKS = 6
A = D + 1
VPAD = (SLOTS - 1) * A

LOOP_TILES, LOOP_CHUNKS = 2, GT // 2
TAIL_TILES, TAIL_CHUNKS = 4, GT // 4
KERR = 2.7e-18 * 1e6
COS_ONE = 2.0 ** -12 / KERR * 0.99
E_LOADS = 16 * 11
MOE_DONE = 7
FF_STEPS = {1: 1, 5: 2, 8: 3, 12: 4, 17: 5, 20: 6, 24: 7}
FF_EXP_STEP = 14


def postln_kernel(nc, a):
    with ExitStack() as ctx:
        def sb(name, shape, dt=F32):
            return ctx.enter_context(nc.sbuf_tensor(name, shape, dt))

        def sem(name):
            return ctx.enter_context(nc.semaphore(name))

        x_group = sb("x_group", [P, NB * S])
        comb = sb("comb", [P, NT, E])
        s_t = sb("s_t", [P, 2, T * NB * S])
        x_rows = s_t[:, 1, 0:NT * E].rearrange("p (j e) -> p j e", e=E)
        probs = sb("probs", [P, 2, T * NB * S])
        weighted = sb("weighted", [P, W, GT * D])
        x_next = weighted[:].rearrange("p w n -> p (w n)")
        o_sb = sb("o_sb", [P, 2, S])
        q_t = sb("q_t", [P, S])
        k_t = sb("k_t", [P, S])
        v_t = sb("v_t", [P, S])
        q_s = sb("q_s", [P, S], F32R)
        k_s = sb("k_s", [P, S], F32R)
        high = sb("high", [P, 2, S])
        low_rows = sb("low_rows", [P, 2, 2])
        m_pad = sb("m_pad", [P, T, P])
        v_pad = sb("v_pad", [P, 2, GT, A + 2 * VPAD])
        r_z = sb("r_z", [P, GT * SLOTS])
        ident = sb("ident", [P, P])
        w_qkv = sb("w_qkv", [P, 3, E])
        b_qkv = sb("b_qkv", [P, 3, H])
        w_head = sb("w_head", [P, 2, 3, L])
        b_head = sb("b_head", [P, 2, 3])
        c2 = sb("c2", [P, W, H])
        c2_head = sb("c2_head", [P, 2, W])
        iw = sb("iw", [P, W])
        half_pi = sb("half_pi", [P, 1])
        pm = probs[:, 1, 0:4 * W * H].rearrange("p (k n) -> p k n", k=4)

        w_o = sb("w_o", [P, E])
        sw12 = sb("sw12", [P, E])
        sw12_t = sb("sw12_t", [P, 2 * HID])
        sw3 = sb("sw3", [P, 2, 2, HID])
        sw3_t = sb("sw3_t", [P, 2, P])
        rows = sb("rows", [P, 5, E])
        BO, SB12, SB3, LN_S, LN_X = range(5)

        class Chunk:

            def __init__(self, name, tiles, at=None):
                self.k, self.name, self.at = tiles, name, at
                self.xr = self.buffer("xr", E)
                self.h = self.xr
                self.xb = self.buffer("xb", E)
                self.tt = self.buffer("tt", E)
                self.y = self.buffer("y", E)
                self.x1 = self.buffer("x1", E)
                self.x1b = self.buffer("x1b", E)
                self.u = self.buffer("u", HID)
                self.e = self.buffer("e", HID)
                self.stats = self.buffer("stats", 6)
                self.mean = self.buffer("mean", 1)
                self.var = self.buffer("var", 1)
                self.rstd = self.buffer("rstd", 1)
                self.nt = self.buffer("nt", 1)

            def buffer(self, field, n):
                if self.at is None:
                    view = sb(f"{self.name}_{field}", [P, self.k * n])[:]
                else:
                    view = self.at[:, 0:self.k * n]
                    self.at = self.at[:, self.k * n:]
                return view.rearrange("p (k n) -> p k n", k=self.k)

        loop_chunk = Chunk("lc", LOOP_TILES)
        comb_chunk = sb("comb_chunk", [P, LOOP_TILES, E])
        flat_probs = probs[:].rearrange("p a n -> p (a n)")
        CHUNK_SIZE = TAIL_TILES * 8 * E
        tail_chunks = [Chunk(f"tc{c}", TAIL_TILES, flat_probs[:, c * CHUNK_SIZE:(c + 1) * CHUNK_SIZE])
                       for c in range(TAIL_CHUNKS)]
        flat_s = s_t[:].rearrange("p a n -> p (a n)")
        taken = [0]

        def scratch(n):
            taken[0] += n
            return flat_s[:, taken[0] - n:taken[0]]

        MT = M // P
        EC = EXPERTS * HID // P
        moe = Chunk("moe", 2 * MT, scratch(2 * MT * 8 * E))
        ew = scratch(3 * EC * P).rearrange("p (i c d) -> p i c d", i=3, c=EC)
        ew_t = scratch((3 * EC + 1) * P).rearrange("p (c d) -> p c d", d=P)
        eb12 = scratch(2 * EXPERTS * HID).rearrange("p (i n) -> p i n", i=2)
        hx = scratch(2 * MT * EXPERTS * HID).rearrange("p (i j n) -> p i j n", i=2, j=MT)
        zx = scratch(MT * (EC + 1) * P).rearrange("p (j c n) -> p j c n", j=MT, c=EC + 1)
        zx_t = scratch(MT * (EC + 1) * P).rearrange("p (j c n) -> p j c n", j=MT, c=EC + 1)
        G = 1 + EXPERTS
        gate_rows = scratch(P)
        gate_t = scratch(G)
        gate_b = scratch(G + EXPERTS)
        gates = scratch(MT * G).rearrange("p (j g) -> p j g", j=MT)
        biased = scratch(MT * EXPERTS).rearrange("p (j g) -> p j g", j=MT)
        chosen = scratch(MT * EXPERTS).rearrange("p (j g) -> p j g", j=MT)
        best = scratch(MT).rearrange("p (j o) -> p j o", o=1)
        pair = scratch(MT * 2).rearrange("p (j g) -> p j g", j=MT)
        order = sb("order", [P, EXPERTS])
        index = sb("index", [P, 3, MT], I32)

        flag = sb("flag", [P, 1], I32)
        x_sq = sb("x_sq", [P, NT + 1])
        bound = probs[:, 1, 4 * W * H:]
        ones = bound[:, 0:P]
        w_sq = bound[:, P:3 * P]
        b_rows = bound[:, 3 * P:5 * P].rearrange("p (i e) -> p i e", i=2)
        by_head = bound[:, 5 * P:5 * P + 2 * H].rearrange("p (i h) -> p i h", i=2)
        x_squares = probs[:, 0, 0:NT * E].rearrange("p (j e) -> p j e", e=E)

        wave = [probs[:, i // 4, (i % 4) * NB * S:(i % 4 + 1) * NB * S].rearrange("p (b k) -> p b k", b=NB) for i in range(8)]
        cos_small = sb("cos_small", [P, 3, NB])

        psum = ctx.enter_context(nc.psum_tensor("psum", [P, 8, S], F32))
        prep = psum[:, 0:4, :]
        o_ps = [psum[:, 4, :], psum[:, 5, :]]
        ot_ps = psum[:, 6, :].rearrange("p (j l) -> p j l", l=L)
        misc = psum[:, 7, :]

        names = ("x_loaded x2_loaded sw3_zeroed w_loaded ffw_loaded pm_loaded xg_loaded masks_zeroed b_zeroed masks_ready low_step xn_stored m_ready "
                 "i_loaded i_ready e_loaded e_zeroed ew_turned ew_ready gathered scattered m_pe m_dve m_act "
                 "b2_loaded x_squared r_ready r_max ones_ready w_summed bound_chain flag_ready "
                 "c_free c_staged c_proj c_qkv c_vturned c_v c_scores c_angle c_cos c_max c_exp c_sum c_turned "
                 "c_copied c_out c_tile c_chain "
                 "c2_step cos_done x_turned x_copied staged proj_done qkv_ready scores_done max_done mrow_done "
                 "qa_ready st_done st_copied exp_done pv_done o_copied ot_done rz_done norm_done comb_done prep_chain chain "
                 "ffw_turned ffw_ready xr_loaded xb_ready cs_ready x1_ready x1_stored y2_ready out_stored "
                 "ff_pe1 ff_pe2 ff_pe3 ff_pe4 ff_pe6 ff_pe7 ff_dve1 ff_dve3 ff_dve4 ff_dve5 ff_dve6 ff_exp "
                 "x1b_ready").split()
        s = {n: sem(n) for n in names}

        x_dram = a["L0_attn_x"].rearrange("b (t p) e -> p (b t) e", p=P)
        out_dram = a["out"].rearrange("b (t p) e -> p (b t) e", p=P)
        x1_dram = a["x1"].rearrange("(j p) e -> p j e", p=P)

        def on_all(ap, n):
            return ap.rearrange("(o n) -> o n", o=1).broadcast_to([P, n])

        def chunk_of(c):
            return tail_chunks[c], LOOP_CHUNKS + c, GT + c * TAIL_TILES

        def one_way(eng):
            eng.wait_ge(s["flag_ready"], 1)
            return eng.value_load(flag[0:1, 0:1], min_val=0, max_val=1)

        class Linked:

            def __init__(self, dve, chain, base):
                self.dve, self.chain, self.base, self.n = dve, chain, base, 0

            def __call__(self, ins):
                self.n += 1
                ins.then_inc(self.chain, 1)
                self.dve.wait_ge(self.chain, self.base + self.n)

        C_WAVE = 12
        C_TILE = W * C_WAVE
        C_UNIT = T * C_TILE

        def cos_pe(pe):
            with pe.Fori(0, UNITS) as u:
                pe.wait_ge(s["c_staged"], u + 1)
                pe.wait_ge(s["c_free"], u + 1)
                pe.wait_ge(s["xg_loaded"], u // H * 16 + 16)
                for i in range(3):
                    for b in range(NB):
                        last = nc.tensor.matmul(prep[L * b:L * b + L, i, :], w_head[:, 0, i, :],
                                                x_group[:, b * S:(b + 1) * S], start=True, stop=True)
                last.then_inc(s["c_proj"], 1)
                pe.wait_ge(s["c_qkv"], u + 1)
                for qt in range(T):
                    last = nc.tensor.transpose(prep[:, 3, qt * P:(qt + 1) * P], v_t[:, qt * P:(qt + 1) * P], ident[:])
                last.then_inc(s["c_vturned"], 1)
                pe.wait_ge(s["c_v"], u + 1)
                for qt in range(T):
                    n1 = u * T + (qt + 1)
                    for b in range(NB):
                        last = nc.tensor.matmul(prep[:, b, :], q_t[L * b:L * b + D, qt * P:(qt + 1) * P],
                                                k_t[L * b:L * b + D, :], start=True, stop=True)
                    last.then_inc(s["c_scores"], 1)
                    pe.wait_ge(s["c_sum"], n1)
                    for b in range(NB):
                        for kt in range(T):
                            last = nc.tensor.transpose(psum[:, 4 + b, kt * P:(kt + 1) * P],
                                                       wave[4][:, b, kt * P:(kt + 1) * P], ident[:])
                    last.then_inc(s["c_turned"], 1)
                    pe.wait_ge(s["c_copied"], n1)
                    for b in range(NB):
                        for kt in range(T):
                            last = nc.tensor.matmul(prep[:, 0, b * D:(b + 1) * D], wave[5][:, b, kt * P:(kt + 1) * P],
                                                    v_pad[:, 0, b * T + kt, VPAD:VPAD + D], start=(kt == 0), stop=(kt == T - 1))
                    last.then_inc(s["c_out"], 1)
                    pe.wait_ge(s["c_tile"], n1)

        def cos_act(act):
            with act.Fori(0, UNITS) as u:
                for qt in range(T):
                    with act.Fori(0, W) as w:
                        t1 = (u * T + qt) * W + w + 1
                        act.wait_ge(s["c_angle"], t1)
                        nc.scalar.activation(wave[2], wave[1], ACT.Sin, bias=half_pi[:, 0:1], scale=-1.0).then_inc(s["c_cos"], 1)
                        act.wait_ge(s["c_max"], t1)
                        for b in range(NB):
                            last = nc.scalar.activation(wave[3][:, b, :], wave[2][:, b, :], ACT.Exp, bias=cos_small[:, 0, b:b + 1],
                                                        accum_out=cos_small[:, 1, b:b + 1])
                        last.then_inc(s["c_exp"], 1)

        def cos_dve(dve):
            with dve.Fori(0, UNITS) as u:
                dve.wait_ge(s["c_proj"], u + 1)
                nc.vector.tensor_scalar(v_t[:], prep[:, 2, :], b_head[:, 0, 2:3], None, ALU.add)
                nc.vector.tensor_scalar(q_t[:], prep[:, 0, :], b_head[:, 0, 0:1], SCALE, ALU.add, ALU.mult)
                nc.vector.tensor_scalar(k_t[:], prep[:, 1, :], b_head[:, 0, 1:2], None, ALU.add).then_inc(s["c_qkv"], 1)
                dve.wait_ge(s["c_vturned"], u + 1)
                nc.vector.tensor_copy(v_pad[:, 0, :, VPAD:VPAD + A].rearrange("p (b t) e -> p t b e", b=NB),
                                      prep[:, 3, :].rearrange("p (t b l) -> p t b l", t=T, b=NB)[:, :, :, 0:A]).then_inc(s["c_v"], 1)
                for qt in range(T):
                    n1 = u * T + (qt + 1)
                    base = u * C_UNIT + qt * C_TILE
                    dve.wait_ge(s["c_scores"], n1)
                    nc.vector.memset(wave[4], 0.0)
                    with dve.Fori(0, W) as w:
                        link = Linked(dve, s["c_chain"], base + w * C_WAVE)
                        t1 = (u * T + qt) * W + w + 1
                        link(nc.vector.tensor_scalar(wave[0], prep, c2_head[:, 0, bass.ds(w, 1)], None, ALU.mult))
                        link(nc.vector.scalar_tensor_tensor(out=wave[1], in0=wave[0], scalar=KERR, in1=wave[0],
                                                            op0=ALU.mult, op1=ALU.mult))
                        link(nc.vector.tensor_scalar(wave[2], wave[1], float(1 / (2 * np.pi)), MAGIC, ALU.mult, ALU.add))
                        link(nc.vector.tensor_scalar(wave[2], wave[2], MAGIC, None, ALU.subtract))
                        for part in TWO_PI_PARTS:
                            link(nc.vector.scalar_tensor_tensor(out=wave[1], in0=wave[2], scalar=-part, in1=wave[1],
                                                                op0=ALU.mult, op1=ALU.add))
                        link(nc.vector.scalar_tensor_tensor(out=wave[1], in0=wave[1], scalar=-1.0, in1=wave[1],
                                                            op0=ALU.mult, op1=ALU.max))
                        nc.vector.tensor_scalar(wave[1], wave[1], float(np.pi), None, ALU.min).then_inc(s["c_angle"], 1)
                        dve.wait_ge(s["c_cos"], t1)
                        link(nc.vector.tensor_tensor(wave[2], wave[2], wave[0], ALU.mult))
                        nc.vector.tensor_reduce(cos_small[:, 0, :], wave[2], AX.X, ALU.max, negate=True).then_inc(s["c_max"], 1)
                        dve.wait_ge(s["c_exp"], t1)
                        link(nc.vector.reciprocal(cos_small[:, 2, :], cos_small[:, 1, :]))
                        link(nc.vector.tensor_scalar(cos_small[:, 2, :], cos_small[:, 2, :], iw[:, bass.ds(w, 1)], None, ALU.mult))
                        for b in range(NB):
                            last = nc.vector.scalar_tensor_tensor(out=wave[4][:, b, :], in0=wave[3][:, b, :],
                                                                  scalar=cos_small[:, 2, b:b + 1], in1=wave[4][:, b, :],
                                                                  op0=ALU.mult, op1=ALU.add)
                        link(last)
                        assert link.n == C_WAVE, link.n
                    nc.vector.tensor_copy(cos_small[:, 2, 0:1], cos_small[:, 1, 0:1]).then_inc(s["c_sum"], 1)
                    dve.wait_ge(s["c_turned"], n1)
                    nc.vector.tensor_copy(wave[5], psum[:, 4:8, :]).then_inc(s["c_copied"], 1)
                    dve.wait_ge(s["c_out"], n1)
                    g, h = u // H, u % H
                    nc.vector.tensor_copy(
                        comb[:, bass.ds(g * GT + qt, NB, T), bass.ds(h * D, D)],
                        prep[:, 0, 0:NB * D].rearrange("p (b d) -> p b d", d=D)).then_inc(s["c_tile"], 1)
                dve.wait_ge(s["c_tile"], u * T + T)
                nc.vector.tensor_copy(cos_small[:, 2, 0:1], cos_small[:, 1, 0:1]).then_inc(s["comb_done"], 1)
                nc.vector.tensor_copy(cos_small[:, 2, 1:2], cos_small[:, 1, 1:2]).then_inc(s["c_free"], 1)

        block = ctx.enter_context(nc.Block())

        @block.sync
        def _(sp):
            sp.dma_start(x_rows[:, 0:GT, :], x_dram[:, 0:GT, :]).then_inc(s["x_loaded"], 16)
            sp.dma_start(x_rows[:, GT:NT, :], x_dram[:, GT:NT, :]).then_inc(s["x2_loaded"], 16)
            for i, name in enumerate(("L0_attn_bq", "L0_attn_bk")):
                sp.dma_start(b_rows[:, i, :], on_all(a[name], E)).then_inc(s["b2_loaded"], 16)
            for i, name in enumerate(("L0_ffn_index_b", "L0_ffn_index_t")):
                sp.dma_start(index[:, i, :], a[name].rearrange("(j p) -> p j", p=P), allow_slow_non_contiguous=True) \
                    .then_inc(s["i_loaded"], 16)
            sp.wait_ge(s["sw3_zeroed"], 1)
            for dst, name in ((w_o[:], "L0_attn_Wo"), (sw12[0:HID, :], "L0_ffn_sw1"), (sw12[HID:P, :], "L0_ffn_sw2"),
                              (sw3[:, 0, 0, :], "L0_ffn_sw3"), (sw3[:, 1, 1, :], "L0_ffn_sw3")):
                sp.dma_start(dst, a[name]).then_inc(s["ffw_loaded"], 16)
            for i, at, name, n in ((BO, 0, "L0_attn_bo", E), (SB12, 0, "L0_ffn_sb1", HID), (SB12, HID, "L0_ffn_sb2", HID),
                                   (SB3, 0, "L0_ffn_sb3", E), (LN_S, 0, "L0_ffn_s_ln_g", HID), (LN_S, HID, "L0_ffn_s_ln_b", HID),
                                   (LN_X, 0, "L0_ffn_sel_ln_g", HID), (LN_X, HID, "L0_ffn_sel_ln_b", HID)):
                sp.dma_start(rows[:, i, at:at + n], on_all(a[name], n)).then_inc(s["ffw_loaded"], 16)
            sp.wait_ge(s["x_copied"], NT // 4)
            sp.dma_start(a["x_next"], x_next).then_inc(s["xn_stored"], 16)
            sp.wait_ge(s["xn_stored"], 16)
            fast = one_way(sp)
            with sp.If(fast == 1):
                sp.wait_ge(s["proj_done"], H)
                sp.dma_start(x_group[:], a["x_next"]).then_inc(s["xg_loaded"], 16)
            with sp.Else():
                sp.wait_ge(s["c_proj"], H)
                sp.dma_start(x_group[:], a["x_next"]).then_inc(s["xg_loaded"], 16)
            with sp.Fori(0, LOOP_CHUNKS) as k:
                tile = bass.ds(k * LOOP_TILES, LOOP_TILES)
                sp.dma_start(loop_chunk.xr, x_dram[:, tile, :]).then_inc(s["xr_loaded"], 16)
                sp.wait_ge(s["x1_ready"], k + 1)
                sp.dma_start(x1_dram[:, tile, :], loop_chunk.x1).then_inc(s["x1_stored"], 16)
                sp.wait_ge(s["y2_ready"], k + 2)
                sp.dma_start(out_dram[:, tile, :], loop_chunk.y).then_inc(s["out_stored"], 16)
            sp.wait_ge(s["comb_done"], UNITS)
            for c in range(TAIL_CHUNKS):
                ch, k, t0 = chunk_of(c)
                sp.dma_start(ch.xr, x_dram[:, t0:t0 + ch.k, :]).then_inc(s["xr_loaded"], 16)
            for c in range(TAIL_CHUNKS):
                ch, k, t0 = chunk_of(c)
                sp.wait_ge(s["x1_ready"], k + 1)
                sp.dma_start(x1_dram[:, t0:t0 + ch.k, :], ch.x1).then_inc(s["x1_stored"], 16)
            for c in range(TAIL_CHUNKS):
                ch, k, t0 = chunk_of(c)
                sp.wait_ge(s["y2_ready"], k + 2)
                sp.dma_start(out_dram[:, t0:t0 + ch.k, :], ch.y).then_inc(s["out_stored"], 16)
            sp.wait_ge(s["x1_stored"], 16 * (1 + LOOP_CHUNKS + TAIL_CHUNKS))
            sp.wait_ge(s["out_stored"], 16 * (1 + LOOP_CHUNKS + TAIL_CHUNKS))

        @block.gpsimd
        def _(pool):
            nc.gpsimd.memset(ident[:], 0.0).then_inc(s["masks_zeroed"], 1)
            nc.gpsimd.memset(w_head[:], 0.0).then_inc(s["masks_zeroed"], 1)
            pool.wait_ge(s["masks_zeroed"], 2)
            nc.gpsimd.affine_select(out=ident[:], in_=ident[:], compare_op=ALU.not_equal, fill=1.0, base=0,
                                    pattern=[[-1, P]], channel_multiplier=1).then_inc(s["masks_ready"], 1)

            def stage(n, p, done=s["staged"]):
                h = n % H
                for part in range(3):
                    m = 2 if part else 3
                    nc.gpsimd.tensor_copy(w_head[:, p, 0:m, part * D:(part + 1) * D], w_qkv[:, 0:m, bass.ds(h * D, D)])
                nc.gpsimd.tensor_copy(b_head[:, p, :], b_qkv[:, :, bass.ds(h, 1)])
                nc.gpsimd.tensor_copy(c2_head[:, p, :], c2[:, :, bass.ds(h, 1)]).then_inc(done, 1)

            def add_rows(ch, k, loaded):
                pool.wait_ge(s["xr_loaded"], loaded)
                nc.gpsimd.tensor_tensor(ch.xb, ch.xr, rows[:, BO:BO + 1, :].broadcast_to([P, ch.k, E]), ALU.add) \
                    .then_inc(s["xb_ready"], 1)

            def add_sb3(ch, k):
                pool.wait_ge(s["x1_ready"], k + 1)
                nc.gpsimd.tensor_tensor(ch.x1b, ch.x1, rows[:, SB3:SB3 + 1, :].broadcast_to([P, ch.k, E]), ALU.add) \
                    .then_inc(s["x1b_ready"], 1)

            pool.wait_ge(s["w_loaded"], 16 * 31)
            pool.wait_ge(s["c2_step"], 7)
            stage(0, 0)
            pool.wait_ge(s["r_ready"], 1)
            nc.gpsimd.partition_all_reduce(x_sq[:, NT:NT + 1], x_sq[:, NT:NT + 1], P, bass.bass_isa.ReduceOp.max) \
                .then_inc(s["r_max"], 1)
            fast = one_way(pool)
            with pool.If(fast == 1):
                for g in range(NG):
                    if g == 1:
                        pool.wait_ge(s["ffw_loaded"], 16 * 13)
                        pool.wait_ge(s["comb_done"], H)
                    with pool.Fori(g * H // 2, (g + 1) * H // 2) as i:
                        for half in range(2):
                            pool.wait_ge(s["exp_done"], (i * 2 + half) * W + 1)
                            if g == 1 and half == 0:
                                k = i - H // 2
                                nc.gpsimd.tensor_copy(comb_chunk[:], comb[:, bass.ds(k * LOOP_TILES, LOOP_TILES), :]) \
                                    .then_inc(s["cs_ready"], 1)
                            stage(i * 2 + half + 1, 1 - half)
                            if g == 1 and half == 0:
                                add_rows(loop_chunk, k, k * 16 + 16)
                                add_sb3(loop_chunk, k)
            with pool.Else():
                pool.wait_ge(s["st_copied"], T)
                with pool.Fori(0, UNITS) as u:
                    pool.wait_ge(s["c_free"], u + 1)
                    stage(u, 0, s["c_staged"])
                pool.wait_ge(s["ffw_loaded"], 16 * 13)
                with pool.Fori(0, LOOP_CHUNKS) as k:
                    pool.wait_ge(s["c_free"], UNITS + 1)
                    pool.wait_ge(s["y2_ready"], k + 1)
                    nc.gpsimd.tensor_copy(comb_chunk[:], comb[:, bass.ds(k * LOOP_TILES, LOOP_TILES), :]) \
                        .then_inc(s["cs_ready"], 1)
                    add_rows(loop_chunk, k, k * 16 + 16)
                    add_sb3(loop_chunk, k)
            pool.wait_ge(s["xr_loaded"], 16 * (LOOP_CHUNKS + TAIL_CHUNKS))
            for c in range(TAIL_CHUNKS):
                add_rows(*chunk_of(c)[:2], 16 * (LOOP_CHUNKS + TAIL_CHUNKS))
            for c in range(TAIL_CHUNKS):
                add_sb3(*chunk_of(c)[:2])
            pool.wait_ge(s["i_ready"], 1)
            pool.wait_ge(s["x1_stored"], 16 * (1 + LOOP_CHUNKS + TAIL_CHUNKS))
            for j in range(MT):
                pool.indirect_dma_start(moe.x1[:, j, :], None, a["x1"], bass.IndirectOffsetOnAxis(index[:, 2, j:j + 1], 0)) \
                    .then_inc(s["gathered"], 16)
            pool.wait_ge(s["m_dve"], MOE_DONE)
            pool.wait_ge(s["out_stored"], 16 * (1 + LOOP_CHUNKS + TAIL_CHUNKS))
            for j in range(MT):
                pool.indirect_dma_start(a["out"].rearrange("b t e -> (b t) e"), bass.IndirectOffsetOnAxis(index[:, 2, j:j + 1], 0),
                                        moe.y[:, j, :], None).then_inc(s["scattered"], 16)
            pool.wait_ge(s["scattered"], 16 * MT)

        @block.scalar
        def _(act):
            act.dma_start(pm[:, 0, :], on_all(a["L0_attn_phase_modulators"].rearrange("w h -> (w h)"), W * H)) \
                .then_inc(s["pm_loaded"], 16)
            act.dma_start(iw[:], on_all(a["L0_attn_interference_weights"], W)).then_inc(s["pm_loaded"], 16)
            for i, name in enumerate(("L0_attn_Wq", "L0_attn_Wk", "L0_attn_Wv")):
                act.dma_start(w_qkv[:, i, :], a[name]).then_inc(s["w_loaded"], 16)
            act.wait_ge(s["b_zeroed"], 2)
            for i, name in enumerate(("L0_attn_bq", "L0_attn_bk", "L0_attn_bv")):
                for b in range(NB):
                    for part in range(1 if i == 2 else 3):
                        r0 = L * b + D * part
                        act.dma_start(b_qkv[r0:r0 + D, i, :], a[name].rearrange("(h d) -> d h", d=D),
                                      allow_slow_non_contiguous=True).then_inc(s["w_loaded"], 16)
            act.wait_ge(s["c2_step"], 6)
            nc.scalar.activation(pm[:, 3, :], pm[:, 2, :], ACT.Sin, bias=half_pi[:, 0:1], scale=-1.0).then_inc(s["cos_done"], 1)
            act.preload_act_table(ACT.Exp)
            act.wait_ge(s["x_loaded"], 16)
            act.wait_ge(s["x2_loaded"], 16)
            for j in range(NT):
                last = nc.scalar.activation(x_squares[:, j, :], x_rows[:, j, :], ACT.Square, accum_out=x_sq[:, j:j + 1])
            last.then_inc(s["x_squared"], 1)
            act.wait_ge(s["x_squared"], 1)

            def exp_of_h(ch, k):
                act.wait_ge(s["ff_dve4"], k + 1)
                nc.scalar.activation(ch.e, ch.h[:, :, 0:HID], ACT.Exp, scale=-1.0).then_inc(s["ff_exp"], 1)

            fast = one_way(act)
            with act.If(fast == 1):
                for g in range(NG):
                    with act.Fori(g * H // 2, (g + 1) * H // 2) as i:
                        for p in range(2):
                            u = i * 2 + p
                            act.wait_ge(s["st_copied"], u * T + T)
                            act.wait_ge(s["staged"], u + 1)
                            for w in range(W):
                                if g == 1 and p * W + w == FF_EXP_STEP:
                                    exp_of_h(loop_chunk, i - H // 2)
                                act.wait_ge(s["pv_done"], u * W + (w + 1))
                                nc.scalar.activation(probs[:, w % 2, :], s_t[:, p, :], ACT.Exp,
                                                     scale=c2_head[:, p, w:w + 1]).then_inc(s["exp_done"], 1)
            with act.Else():
                cos_act(act)
                with act.Fori(0, LOOP_CHUNKS) as k:
                    exp_of_h(loop_chunk, k)
            act.wait_ge(s["e_zeroed"], 1)
            for dst, src in ((ew[:, 0, :, :], a["L0_ffn_ew1"].rearrange("(c e) h d -> (e h) c d", c=EC)),
                             (ew[:, 1, :, :], a["L0_ffn_ew2"].rearrange("(c e) h d -> (e h) c d", c=EC)),
                             (ew[:, 2, :, :].rearrange("p c (e h) -> p (c e) h", h=HID), a["L0_ffn_ew3"].rearrange("e d h -> d e h")),
                             (ew_t[0:EXPERTS, 3 * EC, :], a["L0_ffn_eb3"]),
                             (eb12[:, 0, :], on_all(a["L0_ffn_eb1"].rearrange("e h -> (e h)"), EXPERTS * HID)),
                             (eb12[:, 1, :], on_all(a["L0_ffn_eb2"].rearrange("e h -> (e h)"), EXPERTS * HID)),
                             (gate_rows[0:1, :], a["L0_ffn_sg_w"]), (gate_rows[1:G, :], a["L0_ffn_eg_w"]),
                             (gate_b[:, 0:1], on_all(a["L0_ffn_sg_b"], 1)), (gate_b[:, 1:G], on_all(a["L0_ffn_eg_b"], EXPERTS)),
                             (gate_b[:, G:G + EXPERTS], on_all(a["L0_ffn_exp_bias"], EXPERTS))):
                act.dma_start(dst, src).then_inc(s["e_loaded"], 16)
            for c in range(TAIL_CHUNKS):
                exp_of_h(*chunk_of(c)[:2])
            act.wait_ge(s["m_dve"], 2)
            nc.scalar.activation(gates, gates, ACT.Exp, scale=-1.0).then_inc(s["m_act"], 1)
            act.wait_ge(s["m_dve"], 3)
            nc.scalar.activation(moe.e, moe.h[:, :, 0:HID], ACT.Exp, scale=-1.0).then_inc(s["m_act"], 1)
            act.wait_ge(s["m_dve"], 4)
            nc.scalar.activation(pair, pair, ACT.Exp).then_inc(s["m_act"], 1)

        def in_parts(link, which, done):
            for i, src, dst in which:
                last = nc.vector.tensor_scalar(high[:, i, :].bitcast(I32), src[:].bitcast(I32), HIGH_BITS, None, ALU.bitwise_and)
            link(last)
            for i, src, dst in which:
                last = nc.vector.tensor_scalar(high[:, i, :], high[:, i, :], low_rows[:, i, 1:2], None, ALU.mult)
            link(last)
            for i, src, dst in which:
                last = nc.vector.scalar_tensor_tensor(out=dst[:], in0=src[:], scalar=low_rows[:, i, 0:1], in1=high[:, i, :],
                                                      op0=ALU.mult, op1=ALU.add)
            last.then_inc(done, 1)

        def prep_pe(pe, step, n, p, group, first=False):
            def banks(j):
                return psum[:, 4:8, :] if first and j % 2 else prep

            if step == 1:
                pe.wait_ge(s["staged"], n + 1)
                if not first:
                    pe.wait_ge(s["st_copied"], n * T)
                if not first:
                    pe.wait_ge(s["xg_loaded"], group * 16 + 16)
                for i in range(3):
                    for b in range(NB):
                        last = nc.tensor.matmul(prep[L * b:L * b + L, i, :], w_head[:, p, i, :],
                                                x_group[:, b * S:(b + 1) * S], start=True, stop=True)
                last.then_inc(s["proj_done"], 1)
            if 2 <= step < 2 + T:
                qt = step - 2
                if qt == 0 or (first and qt == 1):
                    pe.wait_ge(s["qkv_ready"], n + 1)
                else:
                    pe.wait_ge(s["max_done"], n * T + (qt - 1 if first else qt))
                for b in range(NB):
                    last = nc.tensor.matmul(banks(qt)[:, b, :], q_s[L * b:L * b + R_S, qt * P:(qt + 1) * P],
                                            k_s[L * b:L * b + R_S, :], start=True, stop=True)
                last.then_inc(s["scores_done"], 1)
            if step == 2 + T:
                pe.wait_ge(s["m_ready"], n + 1)
                for qt in range(T):
                    nc.tensor.transpose(prep[:, 1, qt * P:(qt + 1) * P], v_t[:, qt * P:(qt + 1) * P], ident[:])
                for qt in range(T):
                    last = nc.tensor.transpose(prep[:, 0, qt * P:(qt + 1) * P], m_pad[:, qt, :], ident[:])
                last.then_inc(s["mrow_done"], 1)
            if 4 + T <= step < 4 + 2 * T:
                kt = step - 4 - T
                if kt == 0 or (first and kt == 1):
                    pe.wait_ge(s["qa_ready"], n + 1)
                else:
                    pe.wait_ge(s["st_copied"], n * T + (kt - 1 if first else kt))
                for b in range(NB):
                    last = nc.tensor.matmul(banks(kt)[:, b, :], k_s[L * b:L * b + R_AUG, kt * P:(kt + 1) * P],
                                            q_s[L * b:L * b + R_AUG, :], start=True, stop=True)
                last.then_inc(s["st_done"], 1)

        def prep_dve(dve, step, n, p, first=False):
            def banks(j):
                return psum[:, 4:8, :] if first and j % 2 else prep

            if step == 1:
                dve.wait_ge(s["proj_done"], n + 1)
                link = Linked(dve, s["prep_chain"], n * PREP_LINKS)
                nc.vector.tensor_scalar(v_t[:], prep[:, 2, :], b_head[:, p, 2:3], None, ALU.add)
                nc.vector.tensor_scalar(q_t[:], prep[:, 0, :], b_head[:, p, 0:1], SCALE, ALU.add, ALU.mult)
                link(nc.vector.tensor_scalar(k_t[:], prep[:, 1, :], b_head[:, p, 1:2], None, ALU.add))
                in_parts(link, ((0, q_t, q_s), (1, k_t, k_s)), s["qkv_ready"])
            if 2 <= step < 2 + T:
                qt = step - 2
                dve.wait_ge(s["scores_done"], n * T + (qt + 1))
                nc.vector.tensor_reduce(m_pad[:, qt, :].rearrange("p (b l) -> p b l", l=L)[:, :, R_S:R_S + 1],
                                        banks(qt), AX.X, ALU.max, negate=True).then_inc(s["max_done"], 1)
                if qt == T - 1:
                    dve.wait_ge(s["max_done"], n * T + T)
                    cols = m_pad[:].rearrange("p t (b l) -> p t b l", l=L)
                    nc.vector.tensor_copy(cols[:, :, :, R_S + 1], cols[:, :, :, R_S]).then_inc(s["m_ready"], 1)
            if step == 2 + T:
                dve.wait_ge(s["mrow_done"], n + 1)
                nc.vector.tensor_copy(v_pad[:, p, :, VPAD:VPAD + A].rearrange("p (b t) e -> p t b e", b=NB),
                                      prep[:, 1, :].rearrange("p (t b l) -> p t b l", t=T, b=NB)[:, :, :, 0:A])
                link = Linked(dve, s["prep_chain"], n * PREP_LINKS + PREP_LINKS // 2)
                link(nc.vector.tensor_tensor(q_t[:], prep[:, 0, :], q_t[:], ALU.add))
                in_parts(link, ((0, q_t, q_s),), s["qa_ready"])
            if 4 + T <= step < 4 + 2 * T:
                kt = step - 4 - T
                dve.wait_ge(s["st_done"], n * T + (kt + 1))
                nc.vector.tensor_copy(s_t[:, p, kt * NB * S:(kt + 1) * NB * S],
                                      banks(kt).rearrange("p b q -> p (b q)")).then_inc(s["st_copied"], 1)

        def tile_of(bank, j, n=E):
            return bank[:, j * E:j * E + n]

        def ff_pe(pe, stage, ch, k, bank, source=None):
            if stage == 1:
                for j in range(ch.k):
                    last = nc.tensor.transpose(tile_of(bank, j), source[:, j, :], ident[:])
                last.then_inc(s["ff_pe1"], 1)
            if stage == 2:
                pe.wait_ge(s["ff_dve1"], k + 1)
                for j in range(ch.k):
                    last = nc.tensor.matmul(tile_of(bank, j), ch.tt[:, j, :], w_o[:], start=True, stop=True)
                last.then_inc(s["ff_pe2"], 1)
            if stage == 3:
                pe.wait_ge(s["x1_ready"], k + 1)
                for j in range(ch.k):
                    last = nc.tensor.transpose(tile_of(bank, j), ch.x1[:, j, :], ident[:])
                last.then_inc(s["ff_pe3"], 1)
            if stage == 4:
                pe.wait_ge(s["ff_dve3"], k + 1)
                for j in range(ch.k):
                    last = nc.tensor.matmul(tile_of(bank, j), ch.tt[:, j, :], sw12_t[:], start=True, stop=True)
                last.then_inc(s["ff_pe4"], 1)
            if stage == 6:
                pe.wait_ge(s["ff_dve5"], k + 1)
                for j in range(ch.k // 2):
                    last = nc.tensor.transpose(tile_of(bank, j), ch.u[:, 2 * j:2 * j + 2, :].rearrange("p a h -> p (a h)"),
                                               ident[:])
                last.then_inc(s["ff_pe6"], 1)
            if stage == 7:
                pe.wait_ge(s["ff_dve6"], k + 1)
                for j in range(ch.k):
                    last = nc.tensor.matmul(tile_of(bank, j), ch.tt[:, j // 2, :], sw3_t[:, j % 2, :], start=True, stop=True)
                last.then_inc(s["ff_pe7"], 1)

        def silu_times(link, ch):
            nc.vector.tensor_tensor(ch.u, ch.h[:, :, 0:HID], ch.h[:, :, HID:E], ALU.mult)
            link(nc.vector.tensor_scalar(ch.e, ch.e, 1.0, None, ALU.add))
            link(nc.vector.reciprocal(ch.e, ch.e))
            link(nc.vector.tensor_tensor(ch.u, ch.u, ch.e, ALU.mult))

        def normalised(link, ch, src, n, dst, done=None, tiles=None):
            for j in range(tiles or ch.k):
                last = nc.vector.bn_stats(ch.stats[:, j, :], src[:, j, :])
            link(last)
            var, y, t = ch.var, ch.rstd, ch.nt
            mean_e, sq_e, mean_o, sq_o = (ch.stats[:, :, i:i + 1] for i in (1, 2, 4, 5))
            nc.vector.tensor_tensor(ch.mean, mean_e, mean_o, ALU.add)
            nc.vector.tensor_tensor(t, mean_e, mean_o, ALU.subtract)
            link(nc.vector.tensor_tensor(var, sq_e, sq_o, ALU.add))
            nc.vector.tensor_scalar(ch.mean, ch.mean, 0.5, None, ALU.mult)
            nc.vector.tensor_scalar(var, var, 1.0 / n, EPS, ALU.mult, ALU.add)
            link(nc.vector.scalar_tensor_tensor(out=y, in0=t, scalar=0.25, in1=t, op0=ALU.mult, op1=ALU.mult))
            link(nc.vector.tensor_tensor(var, var, y, ALU.add))
            link(nc.vector.tensor_scalar(t.bitcast(I32), var.bitcast(I32), 1, None, ALU.logical_shift_right))
            link(nc.vector.tensor_scalar(y.bitcast(I32), t.bitcast(I32), -1.0, RSQRT_MAGIC, ALU.mult, ALU.add))
            for _ in range(NEWTON_STEPS):
                link(nc.vector.scalar_tensor_tensor(out=t, in0=y, scalar=-0.5, in1=y, op0=ALU.mult, op1=ALU.mult))
                link(nc.vector.tensor_tensor(t, t, var, ALU.mult))
                link(nc.vector.scalar_tensor_tensor(out=y, in0=t, scalar=1.5, in1=y, op0=ALU.add, op1=ALU.mult))
            for j in range(tiles or ch.k):
                last = nc.vector.tensor_scalar(dst[:, j, :], src[:, j, :], ch.mean[:, j, :], ch.rstd[:, j, :],
                                               ALU.subtract, ALU.mult)
            if done is not None:
                last.then_inc(done, 1)
            else:
                link(last)

        def ff_dve(dve, stage, ch, k, bank, link):
            src = bank[:, 0:ch.k * E].rearrange("p (k e) -> p k e", e=E)
            if stage == 1:
                dve.wait_ge(s["ff_pe1"], k + 1)
                nc.vector.tensor_copy(ch.tt, src).then_inc(s["ff_dve1"], 1)
            if stage == 2:
                dve.wait_ge(s["ff_pe2"], k + 1)
                dve.wait_ge(s["xb_ready"], k + 1)
                if ch is loop_chunk:
                    dve.wait_ge(s["x1_stored"], k * 16 + 16)
                    dve.wait_ge(s["out_stored"], k * 16 + 16)
                link(nc.vector.tensor_tensor(ch.y, src, ch.xb, ALU.add))
                normalised(link, ch, ch.y, E, ch.x1, s["x1_ready"])
            if stage == 3:
                dve.wait_ge(s["ff_pe3"], k + 1)
                nc.vector.tensor_copy(ch.tt, src).then_inc(s["ff_dve3"], 1)
            if stage == 4:
                dve.wait_ge(s["ff_pe4"], k + 1)
                nc.vector.tensor_tensor(ch.h, src, rows[:, SB12:SB12 + 1, :].broadcast_to([P, ch.k, E]), ALU.add) \
                    .then_inc(s["ff_dve4"], 1)
            if stage == 5:
                dve.wait_ge(s["ff_exp"], k + 1)
                silu_times(link, ch)
                normalised(link, ch, ch.u, HID, ch.u)
                link(nc.vector.tensor_tensor(ch.u, ch.u, rows[:, LN_S:LN_S + 1, 0:HID].broadcast_to([P, ch.k, HID]), ALU.mult))
                nc.vector.tensor_tensor(ch.u, ch.u, rows[:, LN_S:LN_S + 1, HID:E].broadcast_to([P, ch.k, HID]), ALU.add) \
                    .then_inc(s["ff_dve5"], 1)
            if stage == 6:
                dve.wait_ge(s["ff_pe6"], k + 1)
                nc.vector.tensor_copy(ch.tt[:, 0:ch.k // 2, :], src[:, 0:ch.k // 2, :]).then_inc(s["ff_dve6"], 1)
            if stage == 7:
                dve.wait_ge(s["ff_pe7"], k + 1)
                dve.wait_ge(s["x1b_ready"], k + 1)
                link(nc.vector.tensor_tensor(ch.xb, src, ch.x1b, ALU.add))
                normalised(link, ch, ch.xb, E, ch.y, s["y2_ready"])

        LINKS_2 = 1 + 6 + 3 * NEWTON_STEPS
        LINKS_5 = 3 + 6 + 3 * NEWTON_STEPS + 1 + 1
        CHUNK_LINKS = 2 * LINKS_2 + LINKS_5
        STAGES = (1, 2, 3, 4, 5, 6, 7)

        def tail_bank(stage, c):
            return psum[:, 4 * (stage % 2) + c, :]

        def experts_weights_pe(pe):
            pe.wait_ge(s["e_loaded"], E_LOADS)
            for i in range(3):
                for c in range(EC):
                    nc.tensor.transpose(tile_of(psum[:, 4 + i, :], c), ew[:, i, c, :], ident[:])
            nc.tensor.transpose(psum[:, 7, 0:G], gate_rows[0:G, :], ident[0:G, 0:G]).then_inc(s["ew_turned"], 1)

        def experts_weights_dve(dve):
            dve.wait_ge(s["ew_turned"], 1)
            for i in range(3):
                nc.vector.tensor_copy(ew_t[:, i * EC:(i + 1) * EC, :].rearrange("p c d -> p (c d)"), psum[:, 4 + i, :])
            nc.vector.tensor_copy(gate_t, psum[:, 7, 0:G]).then_inc(s["ew_ready"], 1)

        def experts_pe(pe):
            pe.wait_ge(s["gathered"], 16 * MT)
            for j in range(MT):
                last = nc.tensor.transpose(tile_of(psum[:, 0, :], j), moe.x1[:, j, :], ident[:])
            last.then_inc(s["m_pe"], 1)
            pe.wait_ge(s["m_dve"], 1)
            for j in range(MT):
                nc.tensor.matmul(psum[:, 1, j * G:(j + 1) * G], moe.tt[:, j, :], gate_t, start=True, stop=True)
            for j in range(MT):
                last = nc.tensor.matmul(tile_of(psum[:, 2, :], j), moe.tt[:, j, :], sw12_t[:], start=True, stop=True)
            last.then_inc(s["m_pe"], 1)
            for i in range(2):
                for j in range(MT):
                    last = nc.tensor.matmul(psum[:, 4 + 2 * i + j, :], moe.tt[:, j, :],
                                            ew_t[:, i * EC:(i + 1) * EC, :].rearrange("p c d -> p (c d)"), start=True, stop=True)
            last.then_inc(s["m_pe"], 1)
            pe.wait_ge(s["m_dve"], 5)
            nc.tensor.transpose(psum[:, 0, 0:P], moe.u[:, 0:MT, :].rearrange("p a h -> p (a h)"), ident[:])
            for j in range(MT):
                for c in range(EC):
                    nc.tensor.transpose(tile_of(psum[:, 1 + j, :], c), zx[:, j, c, :], ident[:])
                last = nc.tensor.transpose(tile_of(psum[:, 3, :], j), zx[:, j, EC, :], ident[:])
            last.then_inc(s["m_pe"], 1)
            pe.wait_ge(s["m_dve"], 6)
            for j in range(MT):
                nc.tensor.matmul(tile_of(psum[:, 4, :], j), moe.tt[:, 0, :], sw3_t[:, j, :], start=True, stop=True)
            for j in range(MT):
                for c in range(EC + 1):
                    last = nc.tensor.matmul(tile_of(psum[:, 5, :], j), zx_t[:, j, c, :], ew_t[:, 2 * EC + c, :],
                                            start=(c == 0), stop=(c == EC))
            last.then_inc(s["m_pe"], 1)

        def experts_dve(dve, link):
            def wide(ap, n):
                return ap.broadcast_to([P, MT, n])

            def two(bank):
                return bank[:, 0:MT * E].rearrange("p (j e) -> p j e", e=E)

            def by_expert(ap):
                return ap.rearrange("p j (e h) -> p j e h", h=HID)

            dve.wait_ge(s["m_pe"], 1)
            nc.vector.tensor_copy(moe.tt[:, 0:MT, :], two(psum[:, 0, :])).then_inc(s["m_dve"], 1)
            dve.wait_ge(s["m_pe"], 2)
            nc.vector.tensor_tensor(gates, psum[:, 1, 0:MT * G].rearrange("p (j g) -> p j g", g=G),
                                    wide(gate_b[:, 0:G].rearrange("p (o g) -> p o g", o=1), G), ALU.add).then_inc(s["m_dve"], 1)
            nc.vector.tensor_tensor(moe.h[:, 0:MT, :], two(psum[:, 2, :]), wide(rows[:, SB12:SB12 + 1, :], E), ALU.add)
            dve.wait_ge(s["m_pe"], 3)
            for i in range(2):
                last = nc.vector.tensor_tensor(hx[:, i, :, :], psum[:, 4 + 2 * i:6 + 2 * i, :],
                                               wide(eb12[:, i:i + 1, :], EXPERTS * HID), ALU.add)
            link(last)
            dve.wait_ge(s["m_act"], 1)
            link(nc.vector.tensor_scalar(gates, gates, 1.0, None, ALU.add))
            link(nc.vector.reciprocal(gates, gates))
            scores = gates[:, :, 1:G]
            link(nc.vector.tensor_tensor(biased, scores, wide(gate_b[:, G:G + EXPERTS].rearrange("p (o g) -> p o g", o=1), EXPERTS),
                                         ALU.add))
            link(nc.vector.tensor_reduce(best, biased, AX.X, ALU.max))
            link(nc.vector.tensor_tensor(chosen, biased, best.broadcast_to([P, MT, EXPERTS]), ALU.is_ge))
            link(nc.vector.tensor_tensor(chosen, chosen, wide(order[:].rearrange("p (o g) -> p o g", o=1), EXPERTS), ALU.mult))
            link(nc.vector.tensor_reduce(best, chosen, AX.X, ALU.max))
            link(nc.vector.tensor_tensor(chosen, chosen, best.broadcast_to([P, MT, EXPERTS]), ALU.is_equal))
            mask = chosen.rearrange("p j (e o) -> p j e o", o=1).broadcast_to([P, MT, EXPERTS, HID])
            for i in range(2):
                last = nc.vector.tensor_tensor(by_expert(hx[:, i, :, :]), by_expert(hx[:, i, :, :]), mask, ALU.mult)
            link(last)
            for i in range(2):
                last = nc.vector.tensor_reduce(moe.h[:, MT:2 * MT, i * HID:(i + 1) * HID],
                                               hx[:, i, :, :].rearrange("p j (e h) -> p j h e", h=HID), AX.X, ALU.add)
            last.then_inc(s["m_dve"], 1)
            link(nc.vector.tensor_tensor(biased, scores, chosen, ALU.mult))
            nc.vector.tensor_copy(pair[:, :, 0:1], gates[:, :, 0:1])
            link(nc.vector.tensor_reduce(pair[:, :, 1:2], biased, AX.X, ALU.add))
            link(nc.vector.tensor_reduce(best, pair, AX.X, ALU.max))
            nc.vector.tensor_tensor(pair, pair, best.broadcast_to([P, MT, 2]), ALU.subtract).then_inc(s["m_dve"], 1)
            dve.wait_ge(s["m_act"], 2)
            silu_times(link, moe)
            normalised(link, moe, moe.u, HID, moe.u)
            for part, gain in ((0, LN_S), (1, LN_X)):
                u = moe.u[:, part * MT:(part + 1) * MT, :]
                last = nc.vector.tensor_tensor(u, u, wide(rows[:, gain:gain + 1, 0:HID], HID), ALU.mult)
            link(last)
            for part, gain in ((0, LN_S), (1, LN_X)):
                u = moe.u[:, part * MT:(part + 1) * MT, :]
                last = nc.vector.tensor_tensor(u, u, wide(rows[:, gain:gain + 1, HID:E], HID), ALU.add)
            link(last)
            for j in range(MT):
                nc.vector.tensor_tensor(zx[:, j, 0:EC, :].rearrange("p c (e h) -> p (c e) h", h=HID), mask[:, j, :, :],
                                        moe.u[:, MT + j:MT + j + 1, :].broadcast_to([P, EXPERTS, HID]), ALU.mult)
            nc.vector.tensor_copy(zx[:, :, EC, 0:EXPERTS], chosen).then_inc(s["m_dve"], 1)
            dve.wait_ge(s["m_act"], 3)
            link(nc.vector.tensor_reduce(best, pair, AX.X, ALU.add))
            link(nc.vector.reciprocal(best, best))
            link(nc.vector.tensor_tensor(pair, pair, best.broadcast_to([P, MT, 2]), ALU.mult))
            dve.wait_ge(s["m_pe"], 4)
            nc.vector.tensor_copy(moe.tt[:, 0, :], psum[:, 0, 0:P])
            for j in range(MT):
                nc.vector.tensor_copy(zx_t[:, j, 0:EC, :].rearrange("p c n -> p (c n)"), psum[:, 1 + j, :])
            nc.vector.tensor_copy(zx_t[:, :, EC, :], two(psum[:, 3, :])).then_inc(s["m_dve"], 1)
            dve.wait_ge(s["m_pe"], 5)
            link(nc.vector.tensor_tensor(moe.xb[:, 0:MT, :], two(psum[:, 4, :]), wide(rows[:, SB3:SB3 + 1, :], E), ALU.add))
            for j in range(MT):
                last = nc.vector.scalar_tensor_tensor(out=moe.xb[:, j, :], in0=moe.xb[:, j, :], scalar=pair[:, j, 0:1],
                                                      in1=moe.x1[:, j, :], op0=ALU.mult, op1=ALU.add)
            link(last)
            for j in range(MT):
                last = nc.vector.scalar_tensor_tensor(out=moe.xb[:, j, :], in0=tile_of(psum[:, 5, :], j), scalar=pair[:, j, 1:2],
                                                      in1=moe.xb[:, j, :], op0=ALU.mult, op1=ALU.add)
            link(last)
            normalised(link, moe, moe.xb, E, moe.y, s["m_dve"], tiles=MT)

        @block.tensor
        def _(pe):
            def turn_x(g):
                pe.wait_ge(s["x_loaded" if g == 0 else "x2_loaded"], 16)
                for q in range(4):
                    n = g * 4 + q
                    if q >= 2:
                        pe.wait_ge(s["x_copied"], n - 1)
                    for j in range(4):
                        last = nc.tensor.transpose(psum[:, 4 + q % 2, j * P:(j + 1) * P], x_rows[:, n * 4 + j, :], ident[:])
                    last.then_inc(s["x_turned"], 1)

            pe.wait_ge(s["masks_ready"], 1)
            turn_x(0)
            pe.wait_ge(s["ones_ready"], 1)
            nc.tensor.matmul(psum[:, 7, 0:2 * E], ones, w_sq, start=True, stop=True).then_inc(s["w_summed"], 1)
            pe.wait_ge(s["x_copied"], 4)
            for step in range(W):
                prep_pe(pe, step, 0, 0, 0, first=True)
            pe.wait_ge(s["st_copied"], T)
            turn_x(1)
            pe.wait_ge(s["ffw_loaded"], 16 * 13)
            pe.wait_ge(s["x_copied"], 8)
            nc.tensor.transpose(psum[:, 7, 0:P], sw12[:], ident[:])
            nc.tensor.transpose(psum[:, 7, P:2 * P], sw3[:, 0, :, :].rearrange("p a h -> p (a h)"), ident[:])
            nc.tensor.transpose(psum[:, 7, 2 * P:3 * P], sw3[:, 1, :, :].rearrange("p a h -> p (a h)"), ident[:]) \
                .then_inc(s["ffw_turned"], 1)

            fast = one_way(pe)
            with pe.If(fast == 1):
                for g in range(NG):
                    with pe.Fori(g * H // 2, (g + 1) * H // 2) as i:
                        for p in range(2):
                            u = i * 2 + p

                            def turn_products(wg):
                                n1 = u * NWG + (wg + 1)
                                pe.wait_ge(s["o_copied"], n1 + 2)
                                pe.wait_ge(s["norm_done"], n1)
                                for qt in range(T):
                                    last = nc.tensor.transpose(psum[:, 6, qt * P:(qt + 1) * P],
                                                               o_sb[:, wg % 2, qt * P:(qt + 1) * P], ident[:])
                                last.then_inc(s["ot_done"], 1)

                            for w in range(W):
                                pe.wait_ge(s["exp_done"], u * W + (w + 1))
                                if w in FIRST_OF:
                                    wg = FIRST_OF[w]
                                    pe.wait_ge(s["o_copied"], u * NWG + (wg + 1))
                                c0 = VPAD - A * SLOT_OF[w]
                                for kt in range(T):
                                    for b in range(NB):
                                        at = (kt * NB + b) * S
                                        last = nc.tensor.matmul(
                                            o_ps[wg % 2][L * b:L * b + SLOTS * A, :], v_pad[:, p, b * T + kt, c0:c0 + SLOTS * A],
                                            probs[:, w % 2, at:at + S], start=(kt == 0 and w in FIRST_OF),
                                            stop=(kt == T - 1 and w in LAST_OF))
                                last.then_inc(s["pv_done"], 1)
                                prep_pe(pe, w, u + 1, 1 - p, 1 if g == 1 else (i * 2 + p + 1) // H)
                                if g == 1 and p * W + w in FF_STEPS:
                                    stage = FF_STEPS[p * W + w]
                                    if stage == 1:
                                        pe.wait_ge(s["cs_ready"], i - H // 2 + 1)
                                        pe.wait_ge(s["y2_ready"], i - H // 2 + 1)
                                    ff_pe(pe, stage, loop_chunk, i - H // 2, misc, comb_chunk)
                                if w in FIRST_OF and w > 0:
                                    turn_products(wg - 1)
                            turn_products(NWG - 1)
            with pe.Else():
                cos_pe(pe)
                with pe.Fori(0, LOOP_CHUNKS) as k:
                    pe.wait_ge(s["cs_ready"], k + 1)
                    for stage in STAGES:
                        ff_pe(pe, stage, loop_chunk, k, misc, comb_chunk)
            pe.wait_ge(s["comb_done"], UNITS)
            pe.wait_ge(s["y2_ready"], LOOP_CHUNKS + 1)
            for stage in STAGES:
                if stage == 3:
                    experts_weights_pe(pe)
                    pe.wait_ge(s["ew_ready"], 1)
                for c in range(TAIL_CHUNKS):
                    ch, k, t0 = chunk_of(c)
                    ff_pe(pe, stage, ch, k, tail_bank(stage, c), comb[:, t0:t0 + ch.k, :])
            pe.wait_ge(s["y2_ready"], LOOP_CHUNKS + TAIL_CHUNKS + 1)
            experts_pe(pe)

        @block.vector
        def _(dve):
            nc.vector.memset(b_qkv[:, 0, :], 0.0).then_inc(s["b_zeroed"], 1)
            nc.vector.memset(b_qkv[:, 1:3, :], 1.0).then_inc(s["b_zeroed"], 1)
            nc.vector.memset(sw3[:], 0.0).then_inc(s["sw3_zeroed"], 1)
            nc.vector.memset(half_pi[:], float(np.pi / 2))
            nc.vector.memset(m_pad[:], 0.0).then_inc(s["xg_loaded"], 16)
            nc.vector.memset(v_pad[:], 0.0)
            nc.vector.memset(r_z[:], 0.0).then_inc(s["pv_done"], 2)
            nc.vector.memset(o_sb[:, 0, 0:1], 0.0).then_inc(s["norm_done"], 1)
            nc.vector.memset(loop_chunk.nt, 0.0).then_inc(s["y2_ready"], 1)
            nc.vector.memset(cos_small[:], 0.0).then_inc(s["c_free"], 1)
            nc.vector.memset(loop_chunk.rstd, 0.0).then_inc(s["x1_stored"], 16)
            nc.vector.memset(loop_chunk.mean, 0.0).then_inc(s["out_stored"], 16)
            for e in range(EXPERTS):
                nc.vector.memset(order[:, e:e + 1], float(EXPERTS - e))
            dve.wait_ge(s["i_loaded"], 32)
            nc.vector.scalar_tensor_tensor(out=index[:, 2, :], in0=index[:, 0, :], scalar=float(S), in1=index[:, 1, :],
                                           op0=ALU.mult, op1=ALU.add).then_inc(s["i_ready"], 1)
            dve.wait_ge(s["masks_ready"], 1)
            link = Linked(dve, s["low_step"], 0)
            by_batch = ident[:].rearrange("p (b l) -> p b l", l=L)
            nc.vector.tensor_reduce(low_rows[:, 0, 0:1], by_batch[:, :, 2 * D:3 * D], AX.XY, ALU.add)
            nc.vector.tensor_reduce(low_rows[:, 0, 1:2], by_batch[:, :, R_S + 1:R_S + 2], AX.XY, ALU.add)
            link(nc.vector.tensor_reduce(low_rows[:, 1, 0:1], by_batch[:, :, D:2 * D], AX.XY, ALU.add))
            link(nc.vector.tensor_tensor(low_rows[:, 0, 0:1], low_rows[:, 0, 0:1], low_rows[:, 0, 1:2], ALU.add))
            link(nc.vector.tensor_scalar(low_rows[:, :, 1:2], low_rows[:, :, 0:1], -2.0, 1.0, ALU.mult, ALU.add))
            dve.wait_ge(s["pm_loaded"], 32)
            nc.vector.tensor_scalar(iw[:], iw[:], 1.0 / W, None, ALU.mult)
            nc.vector.tensor_scalar(pm[:, 1, :], pm[:, 0, :], float(1 / (2 * np.pi)), MAGIC, ALU.mult, ALU.add).then_inc(s["c2_step"], 1)
            dve.wait_ge(s["c2_step"], 1)
            nc.vector.tensor_scalar(pm[:, 1, :], pm[:, 1, :], MAGIC, None, ALU.subtract).then_inc(s["c2_step"], 1)
            dve.wait_ge(s["c2_step"], 2)
            for i, part in enumerate(TWO_PI_PARTS):
                nc.vector.scalar_tensor_tensor(out=pm[:, 0, :], in0=pm[:, 1, :], scalar=-part, in1=pm[:, 0, :],
                                               op0=ALU.mult, op1=ALU.add).then_inc(s["c2_step"], 1)
                dve.wait_ge(s["c2_step"], 3 + i)
            nc.vector.scalar_tensor_tensor(out=pm[:, 2, :], in0=pm[:, 0, :], scalar=-1.0, in1=pm[:, 0, :],
                                           op0=ALU.mult, op1=ALU.max).then_inc(s["c2_step"], 1)
            dve.wait_ge(s["cos_done"], 1)
            nc.vector.tensor_tensor(c2[:].rearrange("p w h -> p (w h)"), pm[:, 3, :], pm[:, 3, :], ALU.mult).then_inc(s["c2_step"], 1)

            def copy_x(g):
                for q in range(4):
                    dve.wait_ge(s["x_turned"], g * 4 + q + 1)
                    nc.vector.tensor_copy((x_group[:], x_next)[g][:, q * S:(q + 1) * S], psum[:, 4 + q % 2, :]).then_inc(s["x_copied"], 1)

            link = Linked(dve, s["bound_chain"], 0)
            nc.vector.memset(ones, 1.0)
            dve.wait_ge(s["w_loaded"], 16 * 31)
            w_qk = w_qkv[:, 0:2, :].rearrange("p i e -> p (i e)")
            nc.vector.tensor_tensor(w_sq, w_qk, w_qk, ALU.mult).then_inc(s["ones_ready"], 1)
            copy_x(0)
            dve.wait_ge(s["x_squared"], 1)
            nc.vector.tensor_reduce(x_sq[:, NT:NT + 1], x_sq[:, 0:NT], AX.X, ALU.max).then_inc(s["r_ready"], 1)
            dve.wait_ge(s["b2_loaded"], 32)
            link(nc.vector.tensor_tensor(b_rows, b_rows, b_rows, ALU.mult))
            dve.wait_ge(s["r_max"], 1)
            dve.wait_ge(s["w_summed"], 1)
            link(nc.vector.scalar_tensor_tensor(out=w_sq.rearrange("p (i e) -> p i e", i=2),
                                                in0=psum[:, 7, 0:2 * E].rearrange("p (i e) -> p i e", i=2),
                                                scalar=x_sq[:, NT:NT + 1], in1=b_rows, op0=ALU.mult, op1=ALU.add))
            link(nc.vector.tensor_reduce(by_head, w_sq.rearrange("p (i h d) -> p i h d", i=2, d=D), AX.X, ALU.add))
            link(nc.vector.tensor_tensor(by_head[:, 0, :], by_head[:, 0, :], by_head[:, 1, :], ALU.mult))
            link(nc.vector.tensor_reduce(by_head[:, 1, 0:1], by_head[:, 0, :], AX.X, ALU.max))
            nc.vector.tensor_scalar(flag[:], by_head[:, 1, 0:1], COS_ONE / (4 * SCALE * SCALE), None, ALU.is_le) \
                .then_inc(s["flag_ready"], 1)
            for step in range(W):
                prep_dve(dve, step, 0, 0, first=True)
            copy_x(1)
            dve.wait_ge(s["x_copied"], 8)
            nc.vector.memset(psum[:, 4:6, :], 0.0).then_inc(s["o_copied"], 2)
            dve.wait_ge(s["xn_stored"], 16)
            dve.wait_ge(s["ffw_turned"], 1)
            nc.vector.tensor_copy(sw12_t[:], psum[:, 7, 0:P])
            nc.vector.tensor_copy(sw3_t[:].rearrange("p a n -> p (a n)"), psum[:, 7, P:3 * P]).then_inc(s["ffw_ready"], 1)

            fast = one_way(dve)
            with dve.If(fast == 1):
                for g in range(NG):
                    with dve.Fori(g * H // 2, (g + 1) * H // 2) as i:
                        link = Linked(dve, s["chain"], (i - H // 2) * CHUNK_LINKS)
                        for p in range(2):
                            u = i * 2 + p

                            def weigh(wg):
                                w0, n = W_GROUPS[wg]
                                n1 = u * NWG + (wg + 1)
                                dve.wait_ge(s["ot_done"], n1)
                                ot = ot_ps[:, :, 0:n * A].rearrange("p j (r e) -> p j r e", e=A)
                                rz = r_z[:, 0:GT * n].rearrange("p (j r) -> p j r", r=n)
                                nc.vector.reciprocal(rz, ot[:, :, :, D]).then_inc(s["rz_done"], 1)
                                dve.wait_ge(s["rz_done"], n1 * 2 - 1)
                                nc.vector.tensor_tensor(rz, rz, iw[:, w0:w0 + n].rearrange("p (o r) -> p o r", o=1)
                                                        .broadcast_to([P, GT, n]), ALU.mult).then_inc(s["rz_done"], 1)
                                dve.wait_ge(s["rz_done"], n1 * 2)
                                nc.vector.tensor_tensor(
                                    weighted[:, w0:w0 + n, :].rearrange("p r (j d) -> p j r d", d=D), ot[:, :, :, 0:D],
                                    rz.rearrange("p j (r o) -> p j r o", o=1).broadcast_to([P, GT, n, D]),
                                    ALU.mult).then_inc(s["norm_done"], 1)

                            for w in range(W):
                                if w in LAST_OF:
                                    wg = LAST_OF[w]
                                    dve.wait_ge(s["pv_done"], u * W + (w + 3))
                                    nc.vector.tensor_copy(o_sb[:, wg % 2, :], o_ps[wg % 2]).then_inc(s["o_copied"], 1)
                                prep_dve(dve, w, u + 1, 1 - p)
                                if w in FIRST_OF and w > 0:
                                    weigh(FIRST_OF[w] - 1)
                                m = p * W + w
                                if g == 1 and m in FF_STEPS:
                                    ff_dve(dve, FF_STEPS[m], loop_chunk, i - H // 2, misc, link)
                            weigh(NWG - 1)
                            dve.wait_ge(s["norm_done"], u * NWG + (NWG + 1))
                            nc.vector.tensor_reduce(
                                comb[:, bass.ds(g * GT, GT), bass.ds((u - g * H) * D, D)].rearrange("p (b t) e -> p t b e", b=NB),
                                weighted[:].rearrange("p w (t b d) -> p t b d w", t=T, b=NB), AX.X, ALU.add) \
                                .then_inc(s["comb_done"], 1)
                        if g == 1:
                            assert link.n == CHUNK_LINKS, (link.n, CHUNK_LINKS)
            with dve.Else():
                cos_dve(dve)
                with dve.Fori(0, LOOP_CHUNKS) as k:
                    link = Linked(dve, s["chain"], k * CHUNK_LINKS)
                    for stage in STAGES:
                        ff_dve(dve, stage, loop_chunk, k, misc, link)
            link = Linked(dve, s["chain"], LOOP_CHUNKS * CHUNK_LINKS)
            nc.vector.memset(zx, 0.0)
            nc.vector.memset(ew_t[:, 3 * EC, :], 0.0).then_inc(s["e_zeroed"], 1)
            for stage in STAGES:
                if stage == 3:
                    experts_weights_dve(dve)
                for c in range(TAIL_CHUNKS):
                    ch, k, t0 = chunk_of(c)
                    ff_dve(dve, stage, ch, k, tail_bank(stage, c), link)
            experts_dve(dve, link)


_INS = ['L0_attn_x', 'L0_attn_Wq', 'L0_attn_bq', 'L0_attn_Wk', 'L0_attn_bk', 'L0_attn_Wv', 'L0_attn_bv', 'L0_attn_Wo',
        'L0_attn_bo', 'L0_attn_phase_modulators', 'L0_attn_interference_weights', 'L0_ffn_index_b', 'L0_ffn_index_t',
        'L0_ffn_sw1', 'L0_ffn_sb1', 'L0_ffn_sw2', 'L0_ffn_sb2', 'L0_ffn_sw3', 'L0_ffn_sb3', 'L0_ffn_s_ln_g',
        'L0_ffn_s_ln_b', 'L0_ffn_sg_w', 'L0_ffn_sg_b', 'L0_ffn_eg_w', 'L0_ffn_eg_b', 'L0_ffn_exp_bias', 'L0_ffn_ew1',
        'L0_ffn_eb1', 'L0_ffn_ew2', 'L0_ffn_eb2', 'L0_ffn_ew3', 'L0_ffn_eb3', 'L0_ffn_sel_ln_g', 'L0_ffn_sel_ln_b']
_OUT = (8, 512, 128)


def kernel(**inputs):
    import numpy as _np
    import concourse.bacc as _bacc
    from concourse import mybir as _mybir
    from concourse.bass_utils import run_bass_kernel_spmd as _run

    nc = _bacc.Bacc("TRN2", target_bir_lowering=False, num_devices=1)
    arrays, args = {}, {}
    for name in _INS:
        x = _np.ascontiguousarray(inputs[name])
        arrays[f"in_{name}_dram"] = x
        args[name] = nc.dram_tensor(f"in_{name}_dram", x.shape, _mybir.dt.from_np(x.dtype), kind="ExternalInput").ap()
    args["x1"] = nc.dram_tensor("x1_dram", (4096, 128), _mybir.dt.float32, kind="Internal").ap()
    args["x_next"] = nc.dram_tensor("x_next_dram", (128, 2048), _mybir.dt.float32, kind="Internal").ap()
    args["out"] = nc.dram_tensor("out_0_dram", _OUT, _mybir.dt.float32, kind="ExternalOutput").ap()
    postln_kernel(nc, args)
    r = _run(nc, [arrays], core_ids=[0])
    return r.results[0]["out_0_dram"]
```

```python
from contextlib import ExitStack

import numpy as np
import concourse.bass as bass
from concourse import mybir

ALU = mybir.AluOpType
ACT = mybir.ActivationFunctionType
AX = mybir.AxisListType
F32 = mybir.dt.float32
F32R = mybir.dt.float32r
I32 = mybir.dt.int32
I16 = mybir.dt.int16
BF16 = mybir.dt.bfloat16

P = 128
B, S, E = 8, 512, 128
H, D = 16, 8
W = 16
HID = 64
EXPERTS = 8
M = 256
NB = 4
NG = B // NB
T = S // P
GT = NB * T
NT = B * T
UNITS = NG * H
L = 32
SCALE = float(1.0 / np.sqrt(D))
EPS = 1e-5
MAGIC = float(1.5 * 2 ** 23)
TWO_PI_PARTS = (6.28125, 0.0019350051879882812, 3.019916050561733e-07)
RSQRT_MAGIC = float(0x5f3759df)
NEWTON_STEPS = 3

SLOTS = 3
W_GROUPS = [(0, 3), (3, 3), (6, 3), (9, 3), (12, 3), (15, 1)]
DVE_KT = 2
X_BATCHES = 2
X_COLS = X_BATCHES * S
PIECES = DVE_KT * NB // X_BATCHES
LOG2_E = float(np.log2(np.e))
BIASED_MAGIC = float(1.5 * 2 ** 23 + 127)
LOWEST_Y = -126.0
EXP2 = (1.0000000005541674, 0.6931472057372656, 0.24022646890630472, 0.05550328776967869, 0.009618488957523083,
        0.00133999312182961, 0.00015345811891707452)
PART_LINKS = (0, 4, 7, 9)
PIECE_STEPS = {0: (0, 0), 2: (0, 1), 3: (0, 2), 4: (1, 0), 5: (1, 1), 7: (1, 2), 8: (2, 0), 9: (2, 1), 10: (2, 2),
               11: (3, 0), 12: (3, 1), 13: (3, 2)}
PRODUCT_STEPS = {4: 0, 8: 1, 11: 2, 15: 3}
NWG = len(W_GROUPS)
FIRST_OF = {w0: g for g, (w0, n) in enumerate(W_GROUPS)}
LAST_OF = {w0 + n - 1: g for g, (w0, n) in enumerate(W_GROUPS)}
SLOT_OF = {w: w - w0 for w0, n in W_GROUPS for w in range(w0, w0 + n)}
R_S = 3 * D
R_AUG = R_S + 2
HIGH_BITS = -4096
PREP_LINKS = 6
A = D + 1
VPAD = (SLOTS - 1) * A

LOOP_TILES, LOOP_CHUNKS = 2, GT // 2
TAIL_TILES, TAIL_CHUNKS = 4, GT // 4
HALF = TAIL_CHUNKS // 2
KERR = 2.7e-18 * 1e6
COS_ONE = 2.0 ** -12 / KERR * 0.99
B_LINKS = 5
E_LOADS = 16 * 11
ALL_STORED = 16 * (1 + LOOP_CHUNKS + 2)
MOE_DONE = 7
FF_STEPS = {12: 1, 13: 2, 15: 3, 16: 4, 23: 5, 27: 5.5, 28: 6, 29: 7}
FF_EXP_STEP = 20


def postln_kernel(nc, a):
    with ExitStack() as ctx:
        def sb(name, shape, dt=F32):
            return ctx.enter_context(nc.sbuf_tensor(name, shape, dt))

        def sem(name):
            return ctx.enter_context(nc.semaphore(name))

        x_group = sb("x_group", [P, NB * S])
        comb = sb("comb", [P, NT, E])
        s_t = sb("s_t", [P, 2, T * NB * S])
        x_rows = s_t[:, 1, 0:NT * E].rearrange("p (j e) -> p j e", e=E)
        probs = sb("probs", [P, 2, T * NB * S])
        weighted = sb("weighted", [P, W, GT * D])
        x_next = weighted[:].rearrange("p w n -> p (w n)")
        o_sb = sb("o_sb", [P, 2, S])
        q_t = sb("q_t", [P, S])
        k_t = sb("k_t", [P, S])
        v_t = sb("v_t", [P, S])
        q_s = sb("q_s", [P, S], F32R)
        k_s = sb("k_s", [P, S], F32R)
        low_rows = sb("low_rows", [P, 2, 2])
        m_pad = sb("m_pad", [P, T, P])
        v_pad = sb("v_pad", [P, 2, GT, A + 2 * VPAD])
        r_z = sb("r_z", [P, GT * SLOTS])
        x_y = sb("x_y", [P, X_COLS])
        x_p = sb("x_p", [P, X_COLS])
        x_2k = sb("x_2k", [P, X_COLS], BF16)
        c2_last = sb("c2_last", [P, H])
        high = o_sb
        ident = sb("ident", [P, P])
        w_qkv = sb("w_qkv", [P, 3, E])
        b_qkv = sb("b_qkv", [P, 3, H])
        w_head = sb("w_head", [P, 2, 3, L])
        b_head = sb("b_head", [P, 2, 3])
        c2 = sb("c2", [P, W, H])
        c2_head = sb("c2_head", [P, 2, W])
        iw = sb("iw", [P, W])
        half_pi = sb("half_pi", [P, 1])
        pm = probs[:, 1, 0:4 * W * H].rearrange("p (k n) -> p k n", k=4)

        w_o = sb("w_o", [P, E])
        sw12 = comb[:, NT - 1, :]
        sw12_t = sb("sw12_t", [P, 2 * HID])
        sw3 = comb[:, NT - 3:NT - 1, :].rearrange("p a (c h) -> p a c h", h=HID)
        sw3_t = sb("sw3_t", [P, 2, P])
        rows = sb("rows", [P, 5, E])
        BO, SB12, SB3, LN_S, LN_X = range(5)

        class Chunk:
            WIDTHS = (E, E, E, E, E, HID, HID, 6, 1, 1, 1, 1, 1)

            def __init__(self, k, buffers):
                self.k, self.buffers = k, buffers
                (self.xr, self.xb, self.tt, self.y, self.x1, self.u, self.e,
                 self.stats, self.mean, self.var, self.rstd, self.nt, self.shift) = buffers
                self.h, self.x1b = self.xr, self.y

            def part(self, t0, k):
                return Chunk(k, [b[:, t0:t0 + k, :] for b in self.buffers])

        def new_chunk(k, take):
            return Chunk(k, [take(k * n).rearrange("p (k n) -> p k n", k=k) for n in Chunk.WIDTHS])

        loop_memory = sb("loop_memory", [P, LOOP_TILES * sum(Chunk.WIDTHS)])
        loop_taken = [0]

        def from_loop_memory(n):
            loop_taken[0] += n
            return loop_memory[:, loop_taken[0] - n:loop_taken[0]]

        loop_chunk = new_chunk(LOOP_TILES, from_loop_memory)
        comb_chunk = loop_chunk.tt
        x_bo = x_group[:].rearrange("p (k e) -> p k e", e=E)
        flat_probs = probs[:].rearrange("p a n -> p (a n)")
        flat_s = s_t[:].rearrange("p a n -> p (a n)")
        taken = [0]

        def scratch(n):
            taken[0] += n
            return flat_s[:, taken[0] - n:taken[0]]

        MT = M // P
        EC = EXPERTS * HID // P
        tail_taken = [0]

        def from_tail_memory(n):
            if tail_taken[0] + n > 2 * T * NB * S:
                return scratch(n)
            tail_taken[0] += n
            return flat_probs[:, tail_taken[0] - n:tail_taken[0]]

        tail = new_chunk(GT + 2 * MT, from_tail_memory)
        rest, moe = tail.part(0, GT), tail.part(GT, 2 * MT)
        ew = scratch(3 * EC * P).rearrange("p (i c d) -> p i c d", i=3, c=EC)
        ew_t = scratch((3 * EC + 1) * P).rearrange("p (c d) -> p c d", d=P)
        eb12 = scratch(2 * EXPERTS * HID).rearrange("p (i n) -> p i n", i=2)
        hx = scratch(2 * MT * EXPERTS * HID).rearrange("p (i j n) -> p i j n", i=2, j=MT)
        zx = scratch(MT * (EC + 1) * P).rearrange("p (j c n) -> p j c n", j=MT, c=EC + 1)
        zx_t = scratch(MT * (EC + 1) * P).rearrange("p (j c n) -> p j c n", j=MT, c=EC + 1)
        G = 1 + EXPERTS
        gate_rows = scratch(P)
        gate_t = scratch(G)
        gate_b = scratch(G + EXPERTS)
        gates = scratch(MT * G).rearrange("p (j g) -> p j g", j=MT)
        biased = scratch(MT * EXPERTS).rearrange("p (j g) -> p j g", j=MT)
        chosen = scratch(MT * EXPERTS).rearrange("p (j g) -> p j g", j=MT)
        best = scratch(MT).rearrange("p (j o) -> p j o", o=1)
        pair = scratch(MT * 2).rearrange("p (j g) -> p j g", j=MT)
        order = sb("order", [P, EXPERTS])
        index = sb("index", [P, 3, MT], I32)

        flag = sb("flag", [P, 1], I32)
        x_sq = sb("x_sq", [P, NT + 1])
        bound = probs[:, 1, 4 * W * H:]
        ones = bound[:, 0:P]
        w_sq = bound[:, P:3 * P]
        b_sq = bound[:, 3 * P:5 * P].rearrange("p (i e) -> p i e", i=2)
        by_head = bound[:, 5 * P:5 * P + 2 * H].rearrange("p (i h) -> p i h", i=2)
        w_sums = bound[:, 6 * P:8 * P]
        b_rows = bound[:, 8 * P:11 * P].rearrange("p (i e) -> p i e", i=3)
        b_own = bound[:, 11 * P:14 * P].rearrange("p (i e) -> p i e", i=3)
        row_dim = bound[:, 14 * P:14 * P + 3 * D].rearrange("p (i d) -> p i d", i=3)
        no_dim = bound[:, 15 * P:15 * P + 2].rearrange("p (i o) -> p i o", o=1)
        x_squares = probs[:, 0, 0:NT * E].rearrange("p (j e) -> p j e", e=E)

        wave = [probs[:, i // 4, (i % 4) * NB * S:(i % 4 + 1) * NB * S].rearrange("p (b k) -> p b k", b=NB) for i in range(8)]
        cos_small = sb("cos_small", [P, 3, NB])

        psum = ctx.enter_context(nc.psum_tensor("psum", [P, 8, S], F32))
        prep = psum[:, 0:4, :]
        o_ps = [psum[:, 4, :], psum[:, 5, :]]
        ot_ps = psum[:, 6, :].rearrange("p (j l) -> p j l", l=L)
        ff_bank = psum[:, 3, :]

        def products_of(wg):
            return psum[:, 7, :] if wg == NWG - 1 else o_ps[wg % 2]


        names = ("x_loaded x2_loaded sw3_zeroed w_loaded ffw_loaded pm_loaded xg_loaded masks_zeroed b_loaded masks_ready low_step xn_stored m_ready "
                 "i_loaded i_ready e_loaded e_zeroed ew_turned ew_ready gathered scattered m_pe m_dve m_act "
                 "x_squared b_step st_shared  r_ready r_max ones_ready w_summed bound_chain flag_ready "
                 "c_free c_staged c_proj c_qkv c_vturned c_v c_scores c_angle c_cos c_max c_exp c_sum c_turned "
                 "c_copied c_out c_tile c_chain "
                 "c2_step cos_done x_turned x_copied staged proj_done qkv_ready scores_done max_done mrow_done "
                 "qa_ready st_done st_copied exp_done pv_done o_copied ot_done rz_done norm_done comb_done prep_chain chain "
                 "ffw_turned ffw_ready xr_loaded xb_ready cs_ready x1_ready x1_stored y2_ready out_stored "
                 "ff_pe1 ff_pe2 ff_pe3 ff_pe4 ff_pe6 ff_pe7 ff_dve1 ff_dve3 ff_dve4 ff_dve5 ff_dve6 ff_exp "
                 "x1b_ready ln_ready x1_act tt_act piece_ready piece_used piece_chain u_act y2_act").split()
        s = {n: sem(n) for n in names}

        x_dram = a["L0_attn_x"].rearrange("b (t p) e -> p (b t) e", p=P)
        out_dram = a["out"].rearrange("b (t p) e -> p (b t) e", p=P)
        x1_dram = a["x1"].rearrange("(j p) e -> p j e", p=P)

        def on_all(ap, n):
            return ap.rearrange("(o n) -> o n", o=1).broadcast_to([P, n])

        def chunk_of(c):
            return tail.part(c * TAIL_TILES, TAIL_TILES), LOOP_CHUNKS + c, GT + c * TAIL_TILES

        def tail_bank(stage, c):
            return psum[:, {1: (0, 1, 2, 3), 2: (4, 5, 6, 7), 3: (0, 1, 2, 3), 4: (4, 5, 6, 7), 6: (0, 1, 2, 3), 7: (7, 0, 1, 2)}[stage][c], :]

        def one_way(eng):
            eng.wait_ge(s["flag_ready"], 1)
            return eng.value_load(flag[0:1, 0:1], min_val=0, max_val=1)

        class Linked:

            def __init__(self, dve, chain, base):
                self.dve, self.chain, self.base, self.n = dve, chain, base, 0

            def __call__(self, ins):
                self.n += 1
                ins.then_inc(self.chain, 1)
                self.dve.wait_ge(self.chain, self.base + self.n)

        C_WAVE = 12
        C_TILE = W * C_WAVE
        C_UNIT = T * C_TILE

        def cos_pe(pe):
            with pe.Fori(0, UNITS) as u:
                pe.wait_ge(s["c_staged"], u + 1)
                pe.wait_ge(s["c_free"], u + 1)
                pe.wait_ge(s["xg_loaded"], u // H * 16 + 16)
                for i in range(3):
                    for b in range(NB):
                        last = nc.tensor.matmul(prep[L * b:L * b + L, i, :], w_head[:, 0, i, :],
                                                x_group[:, b * S:(b + 1) * S], start=True, stop=True)
                last.then_inc(s["c_proj"], 1)
                pe.wait_ge(s["c_qkv"], u + 1)
                for qt in range(T):
                    last = nc.tensor.transpose(prep[:, 3, qt * P:(qt + 1) * P], v_t[:, qt * P:(qt + 1) * P], ident[:])
                last.then_inc(s["c_vturned"], 1)
                pe.wait_ge(s["c_v"], u + 1)
                for qt in range(T):
                    n1 = u * T + (qt + 1)
                    for b in range(NB):
                        last = nc.tensor.matmul(prep[:, b, :], q_t[L * b:L * b + D, qt * P:(qt + 1) * P],
                                                k_t[L * b:L * b + D, :], start=True, stop=True)
                    last.then_inc(s["c_scores"], 1)
                    pe.wait_ge(s["c_sum"], n1)
                    for b in range(NB):
                        for kt in range(T):
                            last = nc.tensor.transpose(psum[:, 4 + b, kt * P:(kt + 1) * P],
                                                       wave[4][:, b, kt * P:(kt + 1) * P], ident[:])
                    last.then_inc(s["c_turned"], 1)
                    pe.wait_ge(s["c_copied"], n1)
                    for b in range(NB):
                        for kt in range(T):
                            last = nc.tensor.matmul(prep[:, 0, b * D:(b + 1) * D], wave[5][:, b, kt * P:(kt + 1) * P],
                                                    v_pad[:, 0, b * T + kt, VPAD:VPAD + D], start=(kt == 0), stop=(kt == T - 1))
                    last.then_inc(s["c_out"], 1)
                    pe.wait_ge(s["c_tile"], n1)

        def cos_act(act):
            with act.Fori(0, UNITS) as u:
                for qt in range(T):
                    with act.Fori(0, W) as w:
                        t1 = (u * T + qt) * W + w + 1
                        act.wait_ge(s["c_angle"], t1)
                        nc.scalar.activation(wave[2], wave[1], ACT.Sin, bias=half_pi[:, 0:1], scale=-1.0).then_inc(s["c_cos"], 1)
                        act.wait_ge(s["c_max"], t1)
                        for b in range(NB):
                            last = nc.scalar.activation(wave[3][:, b, :], wave[2][:, b, :], ACT.Exp, bias=cos_small[:, 0, b:b + 1],
                                                        accum_out=cos_small[:, 1, b:b + 1])
                        last.then_inc(s["c_exp"], 1)

        def cos_dve(dve):
            with dve.Fori(0, UNITS) as u:
                dve.wait_ge(s["c_proj"], u + 1)
                nc.vector.tensor_scalar(v_t[:], prep[:, 2, :], b_head[:, 0, 2:3], None, ALU.add)
                nc.vector.tensor_scalar(q_t[:], prep[:, 0, :], b_head[:, 0, 0:1], SCALE, ALU.add, ALU.mult)
                nc.vector.tensor_scalar(k_t[:], prep[:, 1, :], b_head[:, 0, 1:2], None, ALU.add).then_inc(s["c_qkv"], 1)
                dve.wait_ge(s["c_vturned"], u + 1)
                nc.vector.tensor_copy(v_pad[:, 0, :, VPAD:VPAD + A].rearrange("p (b t) e -> p t b e", b=NB),
                                      prep[:, 3, :].rearrange("p (t b l) -> p t b l", t=T, b=NB)[:, :, :, 0:A]).then_inc(s["c_v"], 1)
                for qt in range(T):
                    n1 = u * T + (qt + 1)
                    base = u * C_UNIT + qt * C_TILE
                    dve.wait_ge(s["c_scores"], n1)
                    nc.vector.memset(wave[4], 0.0)
                    with dve.Fori(0, W) as w:
                        link = Linked(dve, s["c_chain"], base + w * C_WAVE)
                        t1 = (u * T + qt) * W + w + 1
                        link(nc.vector.tensor_scalar(wave[0], prep, c2_head[:, 0, bass.ds(w, 1)], None, ALU.mult))
                        link(nc.vector.scalar_tensor_tensor(out=wave[1], in0=wave[0], scalar=KERR, in1=wave[0],
                                                            op0=ALU.mult, op1=ALU.mult))
                        link(nc.vector.tensor_scalar(wave[2], wave[1], float(1 / (2 * np.pi)), MAGIC, ALU.mult, ALU.add))
                        link(nc.vector.tensor_scalar(wave[2], wave[2], MAGIC, None, ALU.subtract))
                        for part in TWO_PI_PARTS:
                            link(nc.vector.scalar_tensor_tensor(out=wave[1], in0=wave[2], scalar=-part, in1=wave[1],
                                                                op0=ALU.mult, op1=ALU.add))
                        link(nc.vector.scalar_tensor_tensor(out=wave[1], in0=wave[1], scalar=-1.0, in1=wave[1],
                                                            op0=ALU.mult, op1=ALU.max))
                        nc.vector.tensor_scalar(wave[1], wave[1], float(np.pi), None, ALU.min).then_inc(s["c_angle"], 1)
                        dve.wait_ge(s["c_cos"], t1)
                        link(nc.vector.tensor_tensor(wave[2], wave[2], wave[0], ALU.mult))
                        nc.vector.tensor_reduce(cos_small[:, 0, :], wave[2], AX.X, ALU.max, negate=True).then_inc(s["c_max"], 1)
                        dve.wait_ge(s["c_exp"], t1)
                        link(nc.vector.reciprocal(cos_small[:, 2, :], cos_small[:, 1, :]))
                        link(nc.vector.tensor_scalar(cos_small[:, 2, :], cos_small[:, 2, :], iw[:, bass.ds(w, 1)], None, ALU.mult))
                        for b in range(NB):
                            last = nc.vector.scalar_tensor_tensor(out=wave[4][:, b, :], in0=wave[3][:, b, :],
                                                                  scalar=cos_small[:, 2, b:b + 1], in1=wave[4][:, b, :],
                                                                  op0=ALU.mult, op1=ALU.add)
                        link(last)
                        assert link.n == C_WAVE, link.n
                    nc.vector.tensor_copy(cos_small[:, 2, 0:1], cos_small[:, 1, 0:1]).then_inc(s["c_sum"], 1)
                    dve.wait_ge(s["c_turned"], n1)
                    nc.vector.tensor_copy(wave[5], psum[:, 4:8, :]).then_inc(s["c_copied"], 1)
                    dve.wait_ge(s["c_out"], n1)
                    g, h = u // H, u % H
                    nc.vector.tensor_copy(
                        comb[:, bass.ds(g * GT + qt, NB, T), bass.ds(h * D, D)],
                        prep[:, 0, 0:NB * D].rearrange("p (b d) -> p b d", d=D)).then_inc(s["c_tile"], 1)
                dve.wait_ge(s["c_tile"], u * T + T)
                nc.vector.tensor_copy(cos_small[:, 2, 0:1], cos_small[:, 1, 0:1]).then_inc(s["comb_done"], 1)
                nc.vector.tensor_copy(cos_small[:, 2, 1:2], cos_small[:, 1, 1:2]).then_inc(s["c_free"], 1)

        block = ctx.enter_context(nc.Block())

        @block.sync
        def _(sp):
            sp.dma_start(x_rows[:, 0:GT, :], x_dram[:, 0:GT, :]).then_inc(s["x_loaded"], 16)
            for i, name in enumerate(("L0_attn_bq", "L0_attn_bk", "L0_attn_bv")):
                sp.dma_start(b_rows[:, i, :], on_all(a[name], E)).then_inc(s["b_loaded"], 16)
            sp.dma_start(x_rows[:, GT:NT, :], x_dram[:, GT:NT, :]).then_inc(s["x2_loaded"], 16)
            for i, name in enumerate(("L0_ffn_index_b", "L0_ffn_index_t")):
                sp.dma_start(index[:, i, :], a[name].rearrange("(j p) -> p j", p=P), allow_slow_non_contiguous=True) \
                    .then_inc(s["i_loaded"], 16)
            sp.wait_ge(s["sw3_zeroed"], 1)
            for dst, name in ((w_o[:], "L0_attn_Wo"), (sw12[0:HID, :], "L0_ffn_sw1"), (sw12[HID:P, :], "L0_ffn_sw2"),
                              (sw3[:, 0, 0, :], "L0_ffn_sw3"), (sw3[:, 1, 1, :], "L0_ffn_sw3")):
                sp.dma_start(dst, a[name]).then_inc(s["ffw_loaded"], 16)
            for i, at, name, n in ((BO, 0, "L0_attn_bo", E), (SB12, 0, "L0_ffn_sb1", HID), (SB12, HID, "L0_ffn_sb2", HID),
                                   (SB3, 0, "L0_ffn_sb3", E), (LN_S, 0, "L0_ffn_s_ln_g", HID), (LN_S, HID, "L0_ffn_s_ln_b", HID),
                                   (LN_X, 0, "L0_ffn_sel_ln_g", HID), (LN_X, HID, "L0_ffn_sel_ln_b", HID)):
                sp.dma_start(rows[:, i, at:at + n], on_all(a[name], n)).then_inc(s["ffw_loaded"], 16)
            sp.wait_ge(s["x_copied"], NT // 4)
            sp.dma_start(a["x_next"], x_next).then_inc(s["xn_stored"], 16)
            sp.wait_ge(s["xn_stored"], 16)
            fast = one_way(sp)
            with sp.If(fast == 1):
                sp.wait_ge(s["proj_done"], H)
                sp.dma_start(x_group[:], a["x_next"]).then_inc(s["xg_loaded"], 16)
            with sp.Else():
                sp.wait_ge(s["c_proj"], H)
                sp.dma_start(x_group[:], a["x_next"]).then_inc(s["xg_loaded"], 16)
            with sp.Fori(0, LOOP_CHUNKS) as k:
                tile = bass.ds(k * LOOP_TILES, LOOP_TILES)
                sp.dma_start(loop_chunk.xr, x_dram[:, tile, :]).then_inc(s["xr_loaded"], 16)
                sp.wait_ge(s["x1_ready"], k + 1)
                sp.dma_start(x1_dram[:, tile, :], loop_chunk.x1).then_inc(s["x1_stored"], 16)
                sp.wait_ge(s["y2_ready"], k + 2)
                sp.dma_start(out_dram[:, tile, :], loop_chunk.y).then_inc(s["out_stored"], 16)
            with sp.If(fast == 1):
                sp.wait_ge(s["proj_done"], UNITS + 1)
                sp.dma_start(x_bo, x_dram[:, GT:NT, :]).then_inc(s["xr_loaded"], 16)
            with sp.Else():
                sp.wait_ge(s["c_proj"], UNITS)
                sp.dma_start(x_bo, x_dram[:, GT:NT, :]).then_inc(s["xr_loaded"], 16)
            sp.wait_ge(s["e_zeroed"], 1)
            for dst, src in ((ew[:, 0, :, :], a["L0_ffn_ew1"].rearrange("(c e) h d -> (e h) c d", c=EC)),
                             (ew[:, 1, :, :], a["L0_ffn_ew2"].rearrange("(c e) h d -> (e h) c d", c=EC)),
                             (ew[:, 2, :, :].rearrange("p c (e h) -> p (c e) h", h=HID), a["L0_ffn_ew3"].rearrange("e d h -> d e h")),
                             (gate_rows[0:1, :], a["L0_ffn_sg_w"]), (gate_rows[1:G, :], a["L0_ffn_eg_w"]),
                             (ew_t[0:EXPERTS, 3 * EC, :], a["L0_ffn_eb3"]),
                             (gate_b[:, 0:1], on_all(a["L0_ffn_sg_b"], 1)), (gate_b[:, 1:G], on_all(a["L0_ffn_eg_b"], EXPERTS)),
                             (gate_b[:, G:G + EXPERTS], on_all(a["L0_ffn_exp_bias"], EXPERTS)),
                             (eb12[:, 0, :], on_all(a["L0_ffn_eb1"].rearrange("e h -> (e h)"), EXPERTS * HID)),
                             (eb12[:, 1, :], on_all(a["L0_ffn_eb2"].rearrange("e h -> (e h)"), EXPERTS * HID))):
                sp.dma_start(dst, src).then_inc(s["e_loaded"], 16)
            for ready, act_ready, dram, src, stored in (("x1_ready", "x1_act", x1_dram, rest.x1, "x1_stored"),
                                                        ("y2_ready", "y2_act", out_dram, rest.y, "out_stored")):
                n = HALF * TAIL_TILES
                sp.wait_ge(s[ready], LOOP_CHUNKS + HALF + (1 if ready == "y2_ready" else 0))
                sp.dma_start(dram[:, GT:GT + n, :], src[:, 0:n, :]).then_inc(s[stored], 16)
                sp.wait_ge(s[act_ready], TAIL_CHUNKS - HALF)
                sp.dma_start(dram[:, GT + n:NT, :], src[:, n:GT, :]).then_inc(s[stored], 16)
            sp.wait_ge(s["x1_stored"], ALL_STORED)
            sp.wait_ge(s["out_stored"], ALL_STORED)

        @block.gpsimd
        def _(pool):
            nc.gpsimd.memset(ident[:], 0.0).then_inc(s["masks_zeroed"], 1)
            nc.gpsimd.memset(w_head[:], 0.0).then_inc(s["masks_zeroed"], 1)
            pool.wait_ge(s["masks_zeroed"], 2)
            nc.gpsimd.affine_select(out=ident[:], in_=ident[:], compare_op=ALU.not_equal, fill=1.0, base=0,
                                    pattern=[[-1, P]], channel_multiplier=1).then_inc(s["masks_ready"], 1)

            def stage(n, p, done=s["staged"]):
                h = n % H
                for part in range(3):
                    m = 2 if part else 3
                    nc.gpsimd.tensor_copy(w_head[:, p, 0:m, part * D:(part + 1) * D], w_qkv[:, 0:m, bass.ds(h * D, D)])
                nc.gpsimd.tensor_copy(b_head[:, p, :], b_qkv[:, :, bass.ds(h, 1)])
                nc.gpsimd.tensor_copy(c2_head[:, p, :], c2[:, :, bass.ds(h, 1)]).then_inc(done, 1)

            def add_rows(ch, k, loaded):
                pool.wait_ge(s["xr_loaded"], loaded)
                nc.gpsimd.tensor_tensor(ch.xb, ch.xr, rows[:, BO:BO + 1, :].broadcast_to([P, ch.k, E]), ALU.add) \
                    .then_inc(s["xb_ready"], 1)

            def add_sb3(ch, k, ready=None):
                pool.wait_ge(*(ready or (s["x1_ready"], k + 1)))
                nc.gpsimd.tensor_tensor(ch.x1b, ch.x1, rows[:, SB3:SB3 + 1, :].broadcast_to([P, ch.k, E]), ALU.add) \
                    .then_inc(s["x1b_ready"], 1)

            pool.wait_ge(s["w_loaded"], 16 * 3)
            pool.wait_ge(s["b_step"], B_LINKS)
            pool.wait_ge(s["c2_step"], 7)
            stage(0, 0)
            pool.wait_ge(s["r_ready"], 1)
            nc.gpsimd.partition_all_reduce(x_sq[:, NT:NT + 1], x_sq[:, NT:NT + 1], P, bass.bass_isa.ReduceOp.max) \
                .then_inc(s["r_max"], 1)
            fast = one_way(pool)
            with pool.If(fast == 1):
                for g in range(NG):
                    if g == 1:
                        pool.wait_ge(s["ffw_loaded"], 16 * 13)
                        pool.wait_ge(s["comb_done"], H)
                    with pool.Fori(g * H // 2, (g + 1) * H // 2) as i:
                        for half in range(2):
                            pool.wait_ge(s["exp_done"], (i * 2 + half) * W + 1)
                            stage(i * 2 + half + 1, 1 - half)
                            if g == 1 and half == 0:
                                k = i - H // 2
                                pool.wait_ge(s["y2_ready"], k + 1)
                                nc.gpsimd.tensor_copy(comb_chunk, comb[:, bass.ds(k * LOOP_TILES, LOOP_TILES), :]) \
                                    .then_inc(s["cs_ready"], 1)
                                add_rows(loop_chunk, k, k * 16 + 16)
                                add_sb3(loop_chunk, k)
            with pool.Else():
                pool.wait_ge(s["st_copied"], T)
                pool.wait_ge(s["st_shared"], T // 2)
                with pool.Fori(0, UNITS) as u:
                    pool.wait_ge(s["c_free"], u + 1)
                    stage(u, 0, s["c_staged"])
                pool.wait_ge(s["ffw_loaded"], 16 * 13)
                with pool.Fori(0, LOOP_CHUNKS) as k:
                    pool.wait_ge(s["c_free"], UNITS + 1)
                    pool.wait_ge(s["y2_ready"], k + 1)
                    nc.gpsimd.tensor_copy(comb_chunk, comb[:, bass.ds(k * LOOP_TILES, LOOP_TILES), :]) \
                        .then_inc(s["cs_ready"], 1)
                    add_rows(loop_chunk, k, k * 16 + 16)
                    add_sb3(loop_chunk, k)
            pool.wait_ge(s["xr_loaded"], 16 * (LOOP_CHUNKS + 1))
            nc.gpsimd.tensor_tensor(x_bo, x_bo, rows[:, BO:BO + 1, :].broadcast_to([P, GT, E]), ALU.add).then_inc(s["xb_ready"], 1)
            pool.wait_ge(s["i_ready"], 1)
            pool.wait_ge(s["x1_stored"], ALL_STORED)
            for j in range(MT):
                pool.indirect_dma_start(moe.x1[:, j, :], None, a["x1"], bass.IndirectOffsetOnAxis(index[:, 2, j:j + 1], 0)) \
                    .then_inc(s["gathered"], 16)
            for c in range(TAIL_CHUNKS):
                add_sb3(*chunk_of(c)[:2], (s["x1_act"], c - HALF + 1) if c >= HALF else None)
            pool.wait_ge(s["m_dve"], MOE_DONE)
            pool.wait_ge(s["out_stored"], ALL_STORED)
            for j in range(MT):
                pool.indirect_dma_start(a["out"].rearrange("b t e -> (b t) e"), bass.IndirectOffsetOnAxis(index[:, 2, j:j + 1], 0),
                                        moe.y[:, j, :], None).then_inc(s["scattered"], 16)
            pool.wait_ge(s["scattered"], 16 * MT)

        @block.scalar
        def _(act):
            act.dma_start(pm[:, 0, :], on_all(a["L0_attn_phase_modulators"].rearrange("w h -> (w h)"), W * H)) \
                .then_inc(s["pm_loaded"], 16)
            act.dma_start(iw[:], on_all(a["L0_attn_interference_weights"], W)).then_inc(s["pm_loaded"], 16)
            for i, name in enumerate(("L0_attn_Wq", "L0_attn_Wk", "L0_attn_Wv")):
                act.dma_start(w_qkv[:, i, :], a[name]).then_inc(s["w_loaded"], 16)
            act.wait_ge(s["c2_step"], 6)
            nc.scalar.activation(pm[:, 3, :], pm[:, 2, :], ACT.Sin, bias=half_pi[:, 0:1], scale=-1.0).then_inc(s["cos_done"], 1)
            act.preload_act_table(ACT.Exp)
            act.wait_ge(s["x_loaded"], 16)
            act.wait_ge(s["x2_loaded"], 16)
            for j in range(NT):
                last = nc.scalar.activation(x_squares[:, j, :], x_rows[:, j, :], ACT.Square, accum_out=x_sq[:, j:j + 1])
            last.then_inc(s["x_squared"], 1)
            for kt in range(1, T, 2):
                act.wait_ge(s["st_done"], kt + 1)
                nc.scalar.activation(s_t[:, 0, kt * NB * S:(kt + 1) * NB * S], psum[:, 4:8, :].rearrange("p b q -> p (b q)"),
                                     ACT.Copy).then_inc(s["st_shared"], 1)
            act.wait_ge(s["st_shared"], T // 2)

            def exp_of_h(ch, k):
                act.wait_ge(s["ff_dve4"], k + 1)
                nc.scalar.activation(ch.e, ch.h[:, :, 0:HID], ACT.Exp, scale=-1.0).then_inc(s["ff_exp"], 1)

            fast = one_way(act)
            with act.If(fast == 1):
                for g in range(NG):
                    with act.Fori(g * H // 2, (g + 1) * H // 2) as i:
                        for p in range(2):
                            u = i * 2 + p
                            act.wait_ge(s["st_copied"], u * T + T)
                            act.wait_ge(s["staged"], u + 1)
                            for w in range(W):
                                if g == 1 and p * W + w == FF_EXP_STEP:
                                    exp_of_h(loop_chunk, i - H // 2)
                                act.wait_ge(s["pv_done"], u * W + (w + 1))
                                n0 = DVE_KT * NB * S if w == W - 1 else 0
                                nc.scalar.activation(probs[:, w % 2, n0:], s_t[:, p, n0:], ACT.Exp,
                                                     scale=c2_head[:, p, w:w + 1]).then_inc(s["exp_done"], 1)
            with act.Else():
                cos_act(act)
                with act.Fori(0, LOOP_CHUNKS) as k:
                    exp_of_h(loop_chunk, k)
            def copy_tile(stage, c, done, n=TAIL_TILES):
                ch, k, t0 = chunk_of(c)
                act.wait_ge(s[f"ff_pe{stage}"], k + 1)
                nc.scalar.activation(ch.tt[:, 0:n, :].rearrange("p k e -> p (k e)"), tail_bank(stage, c)[:, 0:n * E], ACT.Copy) \
                    .then_inc(s[done], 1)

            def scale_tiles(src, dst, chunks, done):
                for c in chunks:
                    for j in range(c * TAIL_TILES, (c + 1) * TAIL_TILES):
                        last = nc.scalar.activation(dst[:, j, :], src[:, j, :], ACT.Identity, bias=tail.shift[:, j, :],
                                                    scale=tail.rstd[:, j, :])
                    last.then_inc(s[done], 1)

            for c in range(TAIL_CHUNKS):
                copy_tile(1, c, "ff_dve1")
            act.wait_ge(s["ew_turned"], 1)
            for i in range(3):
                nc.scalar.activation(ew_t[:, i * EC:(i + 1) * EC, :].rearrange("p c d -> p (c d)"), psum[:, i, :], ACT.Copy)
            nc.scalar.activation(gate_t, psum[:, 3, 0:G], ACT.Copy).then_inc(s["ew_ready"], 1)
            act.wait_ge(s["ln_ready"], 1)
            scale_tiles(tail.y, tail.x1, range(HALF, TAIL_CHUNKS), "x1_act")
            for c in range(HALF, TAIL_CHUNKS):
                copy_tile(3, c, "tt_act")
            for c in range(TAIL_CHUNKS):
                exp_of_h(*chunk_of(c)[:2])
            act.wait_ge(s["m_dve"], 2)
            nc.scalar.activation(gates, gates, ACT.Exp, scale=-1.0).then_inc(s["m_act"], 1)
            act.wait_ge(s["m_dve"], 3)
            nc.scalar.activation(moe.e, moe.h[:, :, 0:HID], ACT.Exp, scale=-1.0).then_inc(s["m_act"], 1)
            act.wait_ge(s["m_dve"], 4)
            nc.scalar.activation(pair, pair, ACT.Exp).then_inc(s["m_act"], 1)
            act.wait_ge(s["ln_ready"], 2)
            scale_tiles(tail.u, tail.u, range(0, HALF), "u_act")
            for c in range(TAIL_CHUNKS):
                copy_tile(6, c, "ff_dve6", TAIL_TILES // 2)
            act.wait_ge(s["ln_ready"], 3)
            scale_tiles(tail.xb, tail.y, range(HALF, TAIL_CHUNKS), "y2_act")

        def in_parts(link, which, done):
            for i, src, dst in which:
                last = nc.vector.tensor_scalar(high[:, i, :].bitcast(I32), src[:].bitcast(I32), HIGH_BITS, None, ALU.bitwise_and)
            link(last)
            for i, src, dst in which:
                last = nc.vector.tensor_scalar(high[:, i, :], high[:, i, :], low_rows[:, i, 1:2], None, ALU.mult)
            link(last)
            for i, src, dst in which:
                last = nc.vector.scalar_tensor_tensor(out=dst[:], in0=src[:], scalar=low_rows[:, i, 0:1], in1=high[:, i, :],
                                                      op0=ALU.mult, op1=ALU.add)
            last.then_inc(done, 1)

        def piece_dve(dve, piece, part, u, p, h):
            n = u * PIECES + piece
            link = Linked(dve, s["piece_chain"], n * PART_LINKS[3] + PART_LINKS[part])
            a = [c * (-1) ** i for i, c in enumerate(EXP2)]

            def horner(*coefficients):
                for c in coefficients:
                    link(nc.vector.scalar_tensor_tensor(out=x_p[:], in0=x_p[:], scalar=c, in1=x_y[:], op0=ALU.add, op1=ALU.mult))

            if part == 0:
                scores = s_t[:, p, piece * X_COLS:(piece + 1) * X_COLS]
                link(nc.vector.tensor_scalar(x_y[:], scores, c2_last[:, bass.ds(h, 1)], LOWEST_Y, ALU.mult, ALU.max))
                dve.wait_ge(s["piece_used"], n + 1)
                link(nc.vector.tensor_scalar(x_p[:], x_y[:], BIASED_MAGIC, None, ALU.add))
                low_halves = x_p[:].bitcast(I16).rearrange("p (n o) -> p n o", o=2)[:, :, 0:1]
                nc.vector.tensor_scalar(x_2k[:].bitcast(I16).rearrange("p (n o) -> p n o", o=1), low_halves, 7, None,
                                        ALU.logical_shift_left)
                link(nc.vector.scalar_tensor_tensor(out=x_y[:], in0=x_p[:], scalar=BIASED_MAGIC, in1=x_y[:],
                                                    op0=ALU.subtract, op1=ALU.subtract))
                link(nc.vector.tensor_scalar(x_p[:], x_y[:], a[6], None, ALU.mult))
            if part == 1:
                horner(a[5], a[4], a[3])
            if part == 2:
                horner(a[2], a[1])
                nc.vector.scalar_tensor_tensor(out=x_p[:], in0=x_p[:], scalar=a[0], in1=x_2k[:],
                                               op0=ALU.add, op1=ALU.mult).then_inc(s["piece_ready"], 1)
            assert PART_LINKS[part] + link.n == PART_LINKS[part + 1]

        def piece_pe(pe, piece, u, p):
            pe.wait_ge(s["piece_ready"], u * PIECES + (piece + 1))
            if piece == 0:
                pe.wait_ge(s["o_copied"], u * NWG + 2)
            kt, b0 = piece * X_BATCHES // NB, piece * X_BATCHES % NB
            for i in range(X_BATCHES):
                b = b0 + i
                last = nc.tensor.matmul(products_of(NWG - 1)[L * b:L * b + SLOTS * A, :], v_pad[:, p, b * T + kt, VPAD:VPAD + SLOTS * A],
                                        x_p[:, i * S:(i + 1) * S], start=(kt == 0), stop=False)
            last.then_inc(s["piece_used"], 1)

        def prep_pe(pe, step, n, p, group, first=False):
            def banks(j):
                return psum[:, 4:8, :] if first and j % 2 else prep

            if step == 1:
                pe.wait_ge(s["staged"], n + 1)
                if not first:
                    pe.wait_ge(s["st_copied"], n * T)
                if not first:
                    pe.wait_ge(s["xg_loaded"], group * 16 + 16)
                for i in range(3):
                    for b in range(NB):
                        last = nc.tensor.matmul(prep[L * b:L * b + L, i, :], w_head[:, p, i, :],
                                                x_group[:, b * S:(b + 1) * S], start=True, stop=True)
                last.then_inc(s["proj_done"], 1)
            if 2 <= step < 2 + T:
                qt = step - 2
                if qt == 0 or (first and qt == 1):
                    pe.wait_ge(s["qkv_ready"], n + 1)
                else:
                    pe.wait_ge(s["max_done"], n * T + (qt - 1 if first else qt))
                for b in range(NB):
                    last = nc.tensor.matmul(banks(qt)[:, b, :], q_s[L * b:L * b + R_S, qt * P:(qt + 1) * P],
                                            k_s[L * b:L * b + R_S, :], start=True, stop=True)
                last.then_inc(s["scores_done"], 1)
            if step == 2 + T:
                pe.wait_ge(s["m_ready"], n + 1)
                for qt in range(T):
                    nc.tensor.transpose(prep[:, 1, qt * P:(qt + 1) * P], v_t[:, qt * P:(qt + 1) * P], ident[:])
                for qt in range(T):
                    last = nc.tensor.transpose(prep[:, 0, qt * P:(qt + 1) * P], m_pad[:, qt, :], ident[:])
                last.then_inc(s["mrow_done"], 1)
            if 4 + T <= step < 4 + 2 * T:
                kt = step - 4 - T
                if kt == 0 or (first and kt == 1):
                    pe.wait_ge(s["qa_ready"], n + 1)
                elif first:
                    pe.wait_ge(s["st_shared" if kt % 2 else "st_copied"], kt // 2)
                else:
                    pe.wait_ge(s["st_copied"], n * T + kt)
                for b in range(NB):
                    last = nc.tensor.matmul(banks(kt)[:, b, :], k_s[L * b:L * b + R_AUG, kt * P:(kt + 1) * P],
                                            q_s[L * b:L * b + R_AUG, :], start=True, stop=True)
                last.then_inc(s["st_done"], 1)

        def prep_dve(dve, step, n, p, first=False):
            def banks(j):
                return psum[:, 4:8, :] if first and j % 2 else prep

            if step == 1:
                dve.wait_ge(s["proj_done"], n + 1)
                link = Linked(dve, s["prep_chain"], n * PREP_LINKS)
                nc.vector.tensor_scalar(v_t[:], prep[:, 2, :], b_head[:, p, 2:3], None, ALU.add)
                nc.vector.tensor_scalar(q_t[:], prep[:, 0, :], b_head[:, p, 0:1], SCALE, ALU.add, ALU.mult)
                link(nc.vector.tensor_scalar(k_t[:], prep[:, 1, :], b_head[:, p, 1:2], None, ALU.add))
                in_parts(link, ((0, q_t, q_s), (1, k_t, k_s)), s["qkv_ready"])
                dve.wait_ge(s["qkv_ready"], n + 1)
            if 2 <= step < 2 + T:
                qt = step - 2
                dve.wait_ge(s["scores_done"], n * T + (qt + 1))
                nc.vector.tensor_reduce(m_pad[:, qt, :].rearrange("p (b l) -> p b l", l=L)[:, :, R_S:R_S + 1],
                                        banks(qt), AX.X, ALU.max, negate=True).then_inc(s["max_done"], 1)
                if qt == T - 1:
                    dve.wait_ge(s["max_done"], n * T + T)
                    cols = m_pad[:].rearrange("p t (b l) -> p t b l", l=L)
                    nc.vector.tensor_copy(cols[:, :, :, R_S + 1], cols[:, :, :, R_S]).then_inc(s["m_ready"], 1)
            if step == 2 + T:
                dve.wait_ge(s["mrow_done"], n + 1)
                nc.vector.tensor_copy(v_pad[:, p, :, VPAD:VPAD + A].rearrange("p (b t) e -> p t b e", b=NB),
                                      prep[:, 1, :].rearrange("p (t b l) -> p t b l", t=T, b=NB)[:, :, :, 0:A])
                link = Linked(dve, s["prep_chain"], n * PREP_LINKS + PREP_LINKS // 2)
                link(nc.vector.tensor_tensor(q_t[:], prep[:, 0, :], q_t[:], ALU.add))
                in_parts(link, ((0, q_t, q_s),), s["qa_ready"])
                dve.wait_ge(s["qa_ready"], n + 1)
            if 4 + T <= step < 4 + 2 * T:
                kt = step - 4 - T
                if not (first and kt % 2):
                    dve.wait_ge(s["st_done"], n * T + (kt + 1))
                    nc.vector.tensor_copy(s_t[:, p, kt * NB * S:(kt + 1) * NB * S],
                                          banks(kt).rearrange("p b q -> p (b q)")) \
                        .then_inc(s["st_copied"], 1 + T // 2 if first and kt == T - 2 else 1)

        def tile_of(bank, j, n=E):
            return bank[:, j * E:j * E + n]

        def ff_pe(pe, stage, ch, k, bank, source=None, ready=None):
            if stage == 1:
                for j in range(ch.k):
                    last = nc.tensor.transpose(tile_of(bank, j), source[:, j, :], ident[:])
                last.then_inc(s["ff_pe1"], 1)
            if stage == 2:
                pe.wait_ge(s["ff_dve1"], k + 1)
                for j in range(ch.k):
                    last = nc.tensor.matmul(tile_of(bank, j), ch.tt[:, j, :], w_o[:], start=True, stop=True)
                last.then_inc(s["ff_pe2"], 1)
            if stage == 3:
                pe.wait_ge(*(ready or (s["x1_ready"], k + 1)))
                for j in range(ch.k):
                    last = nc.tensor.transpose(tile_of(bank, j), ch.x1[:, j, :], ident[:])
                last.then_inc(s["ff_pe3"], 1)
            if stage == 4:
                pe.wait_ge(*(ready or (s["ff_dve3"], k + 1)))
                for j in range(ch.k):
                    last = nc.tensor.matmul(tile_of(bank, j), ch.tt[:, j, :], sw12_t[:], start=True, stop=True)
                last.then_inc(s["ff_pe4"], 1)
            if stage == 6:
                pe.wait_ge(s["ff_dve5"], k + 1)
                for j in range(ch.k // 2):
                    last = nc.tensor.transpose(tile_of(bank, j), ch.u[:, 2 * j:2 * j + 2, :].rearrange("p a h -> p (a h)"),
                                               ident[:])
                last.then_inc(s["ff_pe6"], 1)
            if stage == 7:
                pe.wait_ge(s["ff_dve6"], k + 1)
                for j in range(ch.k):
                    last = nc.tensor.matmul(tile_of(bank, j), ch.tt[:, j // 2, :], sw3_t[:, j % 2, :], start=True, stop=True)
                last.then_inc(s["ff_pe7"], 1)

        def silu_times(link, ch):
            nc.vector.tensor_tensor(ch.u, ch.h[:, :, 0:HID], ch.h[:, :, HID:E], ALU.mult)
            link(nc.vector.tensor_scalar(ch.e, ch.e, 1.0, None, ALU.add))
            link(nc.vector.reciprocal(ch.e, ch.e))
            link(nc.vector.tensor_tensor(ch.u, ch.u, ch.e, ALU.mult))

        def tile_stats(ch, src):
            for j in range(ch.k):
                last = nc.vector.bn_stats(ch.stats[:, j, :], src[:, j, :])
            return last

        def rstd_of(link, ch, n):
            var, y, t = ch.var, ch.rstd, ch.nt
            mean_e, sq_e, mean_o, sq_o = (ch.stats[:, :, i:i + 1] for i in (1, 2, 4, 5))
            nc.vector.tensor_tensor(ch.mean, mean_e, mean_o, ALU.add)
            nc.vector.tensor_tensor(t, mean_e, mean_o, ALU.subtract)
            link(nc.vector.tensor_tensor(var, sq_e, sq_o, ALU.add))
            nc.vector.tensor_scalar(ch.mean, ch.mean, 0.5, None, ALU.mult)
            nc.vector.tensor_scalar(var, var, 1.0 / n, EPS, ALU.mult, ALU.add)
            link(nc.vector.scalar_tensor_tensor(out=y, in0=t, scalar=0.25, in1=t, op0=ALU.mult, op1=ALU.mult))
            link(nc.vector.tensor_tensor(var, var, y, ALU.add))
            link(nc.vector.tensor_scalar(t.bitcast(I32), var.bitcast(I32), 1, None, ALU.logical_shift_right))
            link(nc.vector.tensor_scalar(y.bitcast(I32), t.bitcast(I32), -1.0, RSQRT_MAGIC, ALU.mult, ALU.add))
            for _ in range(NEWTON_STEPS):
                link(nc.vector.scalar_tensor_tensor(out=t, in0=y, scalar=-0.5, in1=y, op0=ALU.mult, op1=ALU.mult))
                link(nc.vector.tensor_tensor(t, t, var, ALU.mult))
                link(nc.vector.scalar_tensor_tensor(out=y, in0=t, scalar=1.5, in1=y, op0=ALU.add, op1=ALU.mult))

        def scaled(ch, src, dst):
            for j in range(ch.k):
                last = nc.vector.tensor_scalar(dst[:, j, :], src[:, j, :], ch.mean[:, j, :], ch.rstd[:, j, :],
                                               ALU.subtract, ALU.mult)
            return last

        def normalised(link, ch, src, n, dst, done=None):
            link(tile_stats(ch, src))
            rstd_of(link, ch, n)
            last = scaled(ch, src, dst)
            if done is not None:
                last.then_inc(done, 1)
            else:
                link(last)

        def ff_dve(dve, stage, ch, k, bank, link):
            src = bank[:, 0:ch.k * E].rearrange("p (k e) -> p k e", e=E)
            if stage == 1:
                dve.wait_ge(s["ff_pe1"], k + 1)
                nc.vector.tensor_copy(ch.tt, src).then_inc(s["ff_dve1"], 1)
            if stage == 2:
                dve.wait_ge(s["ff_pe2"], k + 1)
                dve.wait_ge(s["xb_ready"], k + 1)
                dve.wait_ge(s["x1_stored"], k * 16 + 16)
                dve.wait_ge(s["out_stored"], k * 16 + 16)
                link(nc.vector.tensor_tensor(ch.y, src, ch.xb, ALU.add))
                normalised(link, ch, ch.y, E, ch.x1, s["x1_ready"])
            if stage == 3:
                dve.wait_ge(s["ff_pe3"], k + 1)
                nc.vector.tensor_copy(ch.tt, src).then_inc(s["ff_dve3"], 1)
            if stage == 4:
                dve.wait_ge(s["ff_pe4"], k + 1)
                nc.vector.tensor_tensor(ch.h, src, rows[:, SB12:SB12 + 1, :].broadcast_to([P, ch.k, E]), ALU.add) \
                    .then_inc(s["ff_dve4"], 1)
            if stage == 5:
                dve.wait_ge(s["ff_exp"], k + 1)
                silu_times(link, ch)
            if stage == 5.5:
                normalised(link, ch, ch.u, HID, ch.u)
                link(nc.vector.tensor_tensor(ch.u, ch.u, rows[:, LN_S:LN_S + 1, 0:HID].broadcast_to([P, ch.k, HID]), ALU.mult))
                nc.vector.tensor_tensor(ch.u, ch.u, rows[:, LN_S:LN_S + 1, HID:E].broadcast_to([P, ch.k, HID]), ALU.add) \
                    .then_inc(s["ff_dve5"], 1)
            if stage == 6:
                dve.wait_ge(s["ff_pe6"], k + 1)
                nc.vector.tensor_copy(ch.tt[:, 0:ch.k // 2, :], src[:, 0:ch.k // 2, :]).then_inc(s["ff_dve6"], 1)
            if stage == 7:
                dve.wait_ge(s["ff_pe7"], k + 1)
                dve.wait_ge(s["x1b_ready"], k + 1)
                link(nc.vector.tensor_tensor(ch.xb, src, ch.x1b, ALU.add))
                normalised(link, ch, ch.xb, E, ch.y, s["y2_ready"])

        LINKS_2 = 1 + 6 + 3 * NEWTON_STEPS
        LINKS_5 = 3 + 6 + 3 * NEWTON_STEPS + 1 + 1
        CHUNK_LINKS = 2 * LINKS_2 + LINKS_5
        STAGES = (1, 2, 3, 4, 5, 5.5, 6, 7)

        def experts_weights_pe(pe):
            pe.wait_ge(s["e_loaded"], E_LOADS)
            for i in range(3):
                for c in range(EC):
                    nc.tensor.transpose(tile_of(psum[:, i, :], c), ew[:, i, c, :], ident[:])
            nc.tensor.transpose(psum[:, 3, 0:G], gate_rows[0:G, :], ident[0:G, 0:G]).then_inc(s["ew_turned"], 1)

        def experts_hidden_pe(pe):
            pe.wait_ge(s["gathered"], 16 * MT)
            for j in range(MT):
                last = nc.tensor.transpose(tile_of(psum[:, 0, :], j), moe.x1[:, j, :], ident[:])
            last.then_inc(s["m_pe"], 1)
            pe.wait_ge(s["m_dve"], 1)
            for j in range(MT):
                nc.tensor.matmul(psum[:, 1, j * G:(j + 1) * G], moe.tt[:, j, :], gate_t, start=True, stop=True)
            for j in range(MT):
                last = nc.tensor.matmul(tile_of(psum[:, 2, :], j), moe.tt[:, j, :], sw12_t[:], start=True, stop=True)
            last.then_inc(s["m_pe"], 1)
            pe.wait_ge(s["ff_dve4"], LOOP_CHUNKS + TAIL_CHUNKS)
            for i in range(2):
                for j in range(MT):
                    last = nc.tensor.matmul(psum[:, 4 + 2 * i + j, :], moe.tt[:, j, :],
                                            ew_t[:, i * EC:(i + 1) * EC, :].rearrange("p c d -> p (c d)"), start=True, stop=True)
            last.then_inc(s["m_pe"], 1)

        def experts_turn_pe(pe):
            pe.wait_ge(s["m_dve"], 5)
            nc.tensor.transpose(tile_of(psum[:, 6, :], 0), moe.u[:, 0:MT, :].rearrange("p a h -> p (a h)"), ident[:])
            for j in range(MT):
                for c in range(EC):
                    nc.tensor.transpose(tile_of(psum[:, 4 + j, :], c), zx[:, j, c, :], ident[:])
                last = nc.tensor.transpose(tile_of(psum[:, 6, :], 1 + j), zx[:, j, EC, :], ident[:])
            last.then_inc(s["m_pe"], 1)

        def experts_down_pe(pe):
            pe.wait_ge(s["m_dve"], 6)
            for j in range(MT):
                nc.tensor.matmul(tile_of(psum[:, 3, :], j), moe.tt[:, 0, :], sw3_t[:, j, :], start=True, stop=True)
            for j in range(MT):
                for c in range(EC + 1):
                    last = nc.tensor.matmul(tile_of(psum[:, 3, :], MT + j), zx_t[:, j, c, :], ew_t[:, 2 * EC + c, :],
                                            start=(c == 0), stop=(c == EC))
            last.then_inc(s["m_pe"], 1)

        def wide(ap, n):
            return ap.broadcast_to([P, MT, n])

        def two(bank):
            return bank[:, 0:MT * E].rearrange("p (j e) -> p j e", e=E)

        mask = chosen.rearrange("p j (e o) -> p j e o", o=1).broadcast_to([P, MT, EXPERTS, HID])

        def experts_hidden_dve(dve, link):
            def by_expert(ap):
                return ap.rearrange("p j (e h) -> p j e h", h=HID)

            dve.wait_ge(s["m_pe"], 2)
            nc.vector.tensor_tensor(gates, psum[:, 1, 0:MT * G].rearrange("p (j g) -> p j g", g=G),
                                    wide(gate_b[:, 0:G].rearrange("p (o g) -> p o g", o=1), G), ALU.add).then_inc(s["m_dve"], 1)
            nc.vector.tensor_tensor(moe.h[:, 0:MT, :], two(psum[:, 2, :]), wide(rows[:, SB12:SB12 + 1, :], E), ALU.add)
            dve.wait_ge(s["m_pe"], 3)
            for i in range(2):
                last = nc.vector.tensor_tensor(hx[:, i, :, :], psum[:, 4 + 2 * i:6 + 2 * i, :],
                                               wide(eb12[:, i:i + 1, :], EXPERTS * HID), ALU.add)
            link(last)
            dve.wait_ge(s["m_act"], 1)
            link(nc.vector.tensor_scalar(gates, gates, 1.0, None, ALU.add))
            link(nc.vector.reciprocal(gates, gates))
            scores = gates[:, :, 1:G]
            link(nc.vector.tensor_tensor(biased, scores, wide(gate_b[:, G:G + EXPERTS].rearrange("p (o g) -> p o g", o=1), EXPERTS),
                                         ALU.add))
            link(nc.vector.tensor_reduce(best, biased, AX.X, ALU.max))
            link(nc.vector.tensor_tensor(chosen, biased, best.broadcast_to([P, MT, EXPERTS]), ALU.is_ge))
            link(nc.vector.tensor_tensor(chosen, chosen, wide(order[:].rearrange("p (o g) -> p o g", o=1), EXPERTS), ALU.mult))
            link(nc.vector.tensor_reduce(best, chosen, AX.X, ALU.max))
            link(nc.vector.tensor_tensor(chosen, chosen, best.broadcast_to([P, MT, EXPERTS]), ALU.is_equal))
            for i in range(2):
                last = nc.vector.tensor_tensor(by_expert(hx[:, i, :, :]), by_expert(hx[:, i, :, :]), mask, ALU.mult)
            link(last)
            for i in range(2):
                last = nc.vector.tensor_reduce(moe.h[:, MT:2 * MT, i * HID:(i + 1) * HID],
                                               hx[:, i, :, :].rearrange("p j (e h) -> p j h e", h=HID), AX.X, ALU.add)
            last.then_inc(s["m_dve"], 1)
            link(nc.vector.tensor_tensor(biased, scores, chosen, ALU.mult))
            nc.vector.tensor_copy(pair[:, :, 0:1], gates[:, :, 0:1])
            link(nc.vector.tensor_reduce(pair[:, :, 1:2], biased, AX.X, ALU.add))
            link(nc.vector.tensor_reduce(best, pair, AX.X, ALU.max))
            nc.vector.tensor_tensor(pair, pair, best.broadcast_to([P, MT, 2]), ALU.subtract).then_inc(s["m_dve"], 1)
            dve.wait_ge(s["m_act"], 2)
            silu_times(link, moe)

        def experts_down_dve(dve, link):
            for j in range(MT):
                nc.vector.tensor_tensor(zx[:, j, 0:EC, :].rearrange("p c (e h) -> p (c e) h", h=HID), mask[:, j, :, :],
                                        moe.u[:, MT + j:MT + j + 1, :].broadcast_to([P, EXPERTS, HID]), ALU.mult)
            nc.vector.tensor_copy(zx[:, :, EC, 0:EXPERTS], chosen).then_inc(s["m_dve"], 1)
            dve.wait_ge(s["m_act"], 3)
            link(nc.vector.tensor_reduce(best, pair, AX.X, ALU.add))
            link(nc.vector.reciprocal(best, best))
            link(nc.vector.tensor_tensor(pair, pair, best.broadcast_to([P, MT, 2]), ALU.mult))
            dve.wait_ge(s["m_pe"], 4)
            nc.vector.tensor_copy(moe.tt[:, 0, :], psum[:, 6, 0:P])
            nc.vector.tensor_copy(zx_t[:, :, EC, :], psum[:, 6, P:(1 + MT) * P].rearrange("p (j e) -> p j e", e=P))
            for j in range(MT):
                last = nc.vector.tensor_copy(zx_t[:, j, 0:EC, :].rearrange("p c n -> p (c n)"), psum[:, 4 + j, :])
            last.then_inc(s["m_dve"], 1)

        def experts_sum_dve(dve, link):
            dve.wait_ge(s["m_pe"], 5)
            link(nc.vector.tensor_tensor(moe.xb[:, 0:MT, :], two(psum[:, 3, :]), wide(rows[:, SB3:SB3 + 1, :], E), ALU.add))
            for j in range(MT):
                last = nc.vector.scalar_tensor_tensor(out=moe.xb[:, j, :], in0=moe.xb[:, j, :], scalar=pair[:, j, 0:1],
                                                      in1=moe.x1[:, j, :], op0=ALU.mult, op1=ALU.add)
            link(last)
            for j in range(MT):
                last = nc.vector.scalar_tensor_tensor(out=moe.xb[:, j, :], in0=tile_of(psum[:, 3, :], MT + j), scalar=pair[:, j, 1:2],
                                                      in1=moe.xb[:, j, :], op0=ALU.mult, op1=ALU.add)
            link(last)

        def tail_dve(dve):
            link = Linked(dve, s["chain"], LOOP_CHUNKS * CHUNK_LINKS)
            chunks = [chunk_of(c)[:2] for c in range(TAIL_CHUNKS)]

            def src(stage, c):
                return tail_bank(stage, c).rearrange("p (k e) -> p k e", e=E)

            def shifts(ch):
                nc.vector.scalar_tensor_tensor(out=ch.shift, in0=ch.mean, scalar=-1.0, in1=ch.rstd,
                                               op0=ALU.mult, op1=ALU.mult).then_inc(s["ln_ready"], 1)

            nc.vector.memset(ew_t[:, 3 * EC, :], 0.0).then_inc(s["e_zeroed"], 1)
            nc.vector.memset(zx, 0.0)
            dve.wait_ge(s["xb_ready"], LOOP_CHUNKS + 1)
            for c, (ch, k) in enumerate(chunks):
                dve.wait_ge(s["ff_pe2"], k + 1)
                last = nc.vector.tensor_tensor(ch.y, src(2, c), x_bo[:, c * TAIL_TILES:(c + 1) * TAIL_TILES, :], ALU.add)
            link(last)
            link(tile_stats(rest, rest.y))
            rstd_of(link, rest, E)
            shifts(rest)
            for ch, k in chunks[:HALF]:
                scaled(ch, ch.y, ch.x1).then_inc(s["x1_ready"], 1)
            for c, (ch, k) in enumerate(chunks[:HALF]):
                dve.wait_ge(s["ff_pe3"], k + 1)
                nc.vector.tensor_copy(ch.tt, src(3, c)).then_inc(s["ff_dve3"], 1)
            for c, (ch, k) in enumerate(chunks):
                dve.wait_ge(s["ff_pe4"], k + 1)
                nc.vector.tensor_tensor(ch.h, src(4, c), rows[:, SB12:SB12 + 1, :].broadcast_to([P, ch.k, E]), ALU.add) \
                    .then_inc(s["ff_dve4"], 1)
            dve.wait_ge(s["ff_exp"], LOOP_CHUNKS + TAIL_CHUNKS)
            nc.vector.tensor_tensor(rest.u, rest.h[:, :, 0:HID], rest.h[:, :, HID:E], ALU.mult)
            link(nc.vector.tensor_scalar(rest.e, rest.e, 1.0, None, ALU.add))
            dve.wait_ge(s["m_pe"], 1)
            nc.vector.tensor_copy(moe.tt[:, 0:MT, :], two(psum[:, 0, :])).then_inc(s["m_dve"], 1)
            link(nc.vector.reciprocal(rest.e, rest.e))
            link(nc.vector.tensor_tensor(rest.u, rest.u, rest.e, ALU.mult))
            link(tile_stats(rest, rest.u))
            experts_hidden_dve(dve, link)
            link(tile_stats(moe, moe.u))
            rstd_of(link, tail, HID)
            shifts(tail)
            own = tail.part(HALF * TAIL_TILES, GT - HALF * TAIL_TILES + 2 * MT)
            link(scaled(own, own.u, own.u))
            dve.wait_ge(s["u_act"], HALF)
            shared, expert = tail.part(0, GT + MT), tail.part(GT + MT, MT)
            for at, op, done in ((0, ALU.mult, None), (HID, ALU.add, s["ff_dve5"])):
                last = nc.vector.tensor_tensor(expert.u, expert.u, wide(rows[:, LN_X:LN_X + 1, at:at + HID], HID), op)
                last = nc.vector.tensor_tensor(shared.u, shared.u, rows[:, LN_S:LN_S + 1, at:at + HID].broadcast_to([P, GT + MT, HID]), op)
                if done is None:
                    link(last)
                else:
                    last.then_inc(done, TAIL_CHUNKS)
                    dve.wait_ge(done, LOOP_CHUNKS + TAIL_CHUNKS)
            experts_down_dve(dve, link)
            for c, (ch, k) in enumerate(chunks):
                dve.wait_ge(s["ff_pe7"], k + 1)
                dve.wait_ge(s["x1b_ready"], k + 1)
                nc.vector.tensor_tensor(ch.xb, src(7, c), ch.x1b, ALU.add)
            experts_sum_dve(dve, link)
            done = tail.part(0, GT + MT)
            link(tile_stats(done, done.xb))
            rstd_of(link, done, E)
            shifts(done)
            for ch, k in chunks[:HALF]:
                scaled(ch, ch.xb, ch.y).then_inc(s["y2_ready"], 1)
            experts = tail.part(GT, MT)
            scaled(experts, experts.xb, experts.y).then_inc(s["m_dve"], 1)

        @block.tensor
        def _(pe):
            def turn_x(g):
                pe.wait_ge(s["x_loaded" if g == 0 else "x2_loaded"], 16)
                for q in range(4):
                    n = g * 4 + q
                    if q >= 2:
                        pe.wait_ge(s["x_copied"], n - 1)
                    for j in range(4):
                        last = nc.tensor.transpose(psum[:, 4 + q % 2, j * P:(j + 1) * P], x_rows[:, n * 4 + j, :], ident[:])
                    last.then_inc(s["x_turned"], 1)

            pe.wait_ge(s["masks_ready"], 1)
            turn_x(0)
            pe.wait_ge(s["ones_ready"], 1)
            nc.tensor.matmul(psum[:, 7, 0:2 * E], ones, w_sq, start=True, stop=True).then_inc(s["w_summed"], 1)
            pe.wait_ge(s["x_copied"], 4)
            for step in range(W):
                prep_pe(pe, step, 0, 0, 0, first=True)
            pe.wait_ge(s["st_shared"], T // 2)
            turn_x(1)
            pe.wait_ge(s["ffw_loaded"], 16 * 13)
            pe.wait_ge(s["x_copied"], 8)
            nc.tensor.transpose(psum[:, 7, 0:P], sw12, ident[:])
            nc.tensor.transpose(psum[:, 7, P:2 * P], sw3[:, 0, :, :].rearrange("p a h -> p (a h)"), ident[:])
            nc.tensor.transpose(psum[:, 7, 2 * P:3 * P], sw3[:, 1, :, :].rearrange("p a h -> p (a h)"), ident[:]) \
                .then_inc(s["ffw_turned"], 1)

            fast = one_way(pe)
            with pe.If(fast == 1):
                for g in range(NG):
                    with pe.Fori(g * H // 2, (g + 1) * H // 2) as i:
                        for p in range(2):
                            u = i * 2 + p

                            def turn_products(wg):
                                n1 = u * NWG + (wg + 1)
                                pe.wait_ge(s["o_copied"], n1 + 2)
                                pe.wait_ge(s["norm_done"], n1)
                                for qt in range(T):
                                    last = nc.tensor.transpose(psum[:, 6, qt * P:(qt + 1) * P],
                                                               o_sb[:, wg % 2, qt * P:(qt + 1) * P], ident[:])
                                last.then_inc(s["ot_done"], 1)

                            for w in range(W):
                                if w in PRODUCT_STEPS:
                                    piece_pe(pe, PRODUCT_STEPS[w], u, p)
                                pe.wait_ge(s["exp_done"], u * W + (w + 1))
                                if w in FIRST_OF:
                                    wg = FIRST_OF[w]
                                    pe.wait_ge(s["o_copied"], u * NWG + (wg + 1))
                                c0 = VPAD - A * SLOT_OF[w]
                                for kt in range(DVE_KT if w == W - 1 else 0, T):
                                    for b in range(NB):
                                        at = (kt * NB + b) * S
                                        last = nc.tensor.matmul(
                                            products_of(wg)[L * b:L * b + SLOTS * A, :], v_pad[:, p, b * T + kt, c0:c0 + SLOTS * A],
                                            probs[:, w % 2, at:at + S], start=(kt == 0 and w in FIRST_OF),
                                            stop=(kt == T - 1 and w in LAST_OF))
                                last.then_inc(s["pv_done"], 1)
                                prep_pe(pe, w, u + 1, 1 - p, 1 if g == 1 else (i * 2 + p + 1) // H)
                                if g == 1 and p * W + w in FF_STEPS:
                                    stage = FF_STEPS[p * W + w]
                                    if stage == 1:
                                        pe.wait_ge(s["cs_ready"], i - H // 2 + 1)
                                    if stage in (1, 6):
                                        pe.wait_ge(s["st_copied"], (u + 1) * T + T)
                                    ff_pe(pe, stage, loop_chunk, i - H // 2, ff_bank, comb_chunk)
                                if w in FIRST_OF and w > 0:
                                    turn_products(wg - 1)
                            turn_products(NWG - 1)
            with pe.Else():
                cos_pe(pe)
                with pe.Fori(0, LOOP_CHUNKS) as k:
                    pe.wait_ge(s["cs_ready"], k + 1)
                    for stage in STAGES:
                        ff_pe(pe, stage, loop_chunk, k, ff_bank, comb_chunk)
            pe.wait_ge(s["comb_done"], UNITS)
            pe.wait_ge(s["y2_ready"], LOOP_CHUNKS + 1)
            for stage in (1, 2, 3, 4, 6, 7):
                if stage == 3:
                    experts_weights_pe(pe)
                    pe.wait_ge(s["ew_ready"], 1)
                if stage == 6:
                    experts_hidden_pe(pe)
                if stage == 7:
                    experts_turn_pe(pe)
                    pe.wait_ge(s["ff_dve6"], LOOP_CHUNKS + TAIL_CHUNKS)
                for c in range(TAIL_CHUNKS):
                    ch, k, t0 = chunk_of(c)
                    ready = {3: (s["x1_act"], c - HALF + 1), 4: (s["tt_act"], c - HALF + 1)}[stage] if stage in (3, 4) and c >= HALF else None
                    ff_pe(pe, stage, ch, k, tail_bank(stage, c), comb[:, t0:t0 + ch.k, :], ready)
            experts_down_pe(pe)

        @block.vector
        def _(dve):
            nc.vector.memset(half_pi[:], float(np.pi / 2))
            nc.vector.memset(comb[:, NT - 3:NT - 1, :], 0.0).then_inc(s["sw3_zeroed"], 1)
            nc.vector.memset(m_pad[:], 0.0).then_inc(s["xg_loaded"], 16)
            nc.vector.memset(ones, 1.0)
            dve.wait_ge(s["pm_loaded"], 32)
            nc.vector.tensor_scalar(iw[:], iw[:], 1.0 / W, None, ALU.mult)
            nc.vector.tensor_scalar(pm[:, 1, :], pm[:, 0, :], float(1 / (2 * np.pi)), MAGIC, ALU.mult, ALU.add).then_inc(s["c2_step"], 1)
            dve.wait_ge(s["c2_step"], 1)
            nc.vector.tensor_scalar(pm[:, 1, :], pm[:, 1, :], MAGIC, None, ALU.subtract).then_inc(s["c2_step"], 1)
            dve.wait_ge(s["c2_step"], 2)
            for i, part in enumerate(TWO_PI_PARTS):
                nc.vector.scalar_tensor_tensor(out=pm[:, 0, :], in0=pm[:, 1, :], scalar=-part, in1=pm[:, 0, :],
                                               op0=ALU.mult, op1=ALU.add).then_inc(s["c2_step"], 1)
                dve.wait_ge(s["c2_step"], 3 + i)
            nc.vector.scalar_tensor_tensor(out=pm[:, 2, :], in0=pm[:, 0, :], scalar=-1.0, in1=pm[:, 0, :],
                                           op0=ALU.mult, op1=ALU.max).then_inc(s["c2_step"], 1)
            dve.wait_ge(s["cos_done"], 1)
            nc.vector.tensor_tensor(c2[:].rearrange("p w h -> p (w h)"), pm[:, 3, :], pm[:, 3, :], ALU.mult).then_inc(s["c2_step"], 1)

            def copy_x(g):
                for q in range(4):
                    dve.wait_ge(s["x_turned"], g * 4 + q + 1)
                    nc.vector.tensor_copy((x_group[:], x_next)[g][:, q * S:(q + 1) * S], psum[:, 4 + q % 2, :]).then_inc(s["x_copied"], 1)

            by_batch = ident[:].rearrange("p (b l) -> p b l", l=L)
            dve.wait_ge(s["masks_ready"], 1)
            link = Linked(dve, s["b_step"], 0)
            for i in range(2):
                nc.vector.tensor_reduce(row_dim[:, i, :], by_batch[:, :, 0:3 * D].rearrange("p b (m d) -> p d b m", d=D), AX.XY, ALU.add)
            link(nc.vector.tensor_reduce(row_dim[:, 2, :], by_batch[:, :, 0:D].rearrange("p b d -> p d b"), AX.X, ALU.add))
            link(nc.vector.tensor_reduce(no_dim, row_dim[:, 1:3, :], AX.X, ALU.add))
            nc.vector.tensor_scalar(no_dim, no_dim, -1.0, 1.0, ALU.mult, ALU.add)
            dve.wait_ge(s["b_loaded"], 16 * 3)
            by_dim = row_dim.rearrange("p i (o d) -> p i o d", o=1).broadcast_to([P, 3, H, D])
            link(nc.vector.tensor_tensor(b_own.rearrange("p i (h d) -> p i h d", d=D),
                                         b_rows.rearrange("p i (h d) -> p i h d", d=D), by_dim, ALU.mult))
            link(nc.vector.tensor_reduce(b_qkv[:], b_own.rearrange("p i (h d) -> p i h d", d=D), AX.X, ALU.add))
            link(nc.vector.tensor_tensor(b_qkv[:, 1:3, :], b_qkv[:, 1:3, :], no_dim.broadcast_to([P, 2, H]), ALU.add))
            assert link.n == B_LINKS, link.n
            copy_x(0)
            dve.wait_ge(s["w_loaded"], 16 * 3)
            w_qk = w_qkv[:, 0:2, :].rearrange("p i e -> p (i e)")
            nc.vector.tensor_tensor(w_sq, w_qk, w_qk, ALU.mult).then_inc(s["ones_ready"], 1)
            link = Linked(dve, s["low_step"], 0)
            nc.vector.tensor_reduce(low_rows[:, 0, 0:1], by_batch[:, :, 2 * D:3 * D], AX.XY, ALU.add)
            nc.vector.tensor_reduce(low_rows[:, 0, 1:2], by_batch[:, :, R_S + 1:R_S + 2], AX.XY, ALU.add)
            link(nc.vector.tensor_reduce(low_rows[:, 1, 0:1], by_batch[:, :, D:2 * D], AX.XY, ALU.add))
            link(nc.vector.tensor_tensor(low_rows[:, 0, 0:1], low_rows[:, 0, 0:1], low_rows[:, 0, 1:2], ALU.add))
            link(nc.vector.tensor_scalar(low_rows[:, :, 1:2], low_rows[:, :, 0:1], -2.0, 1.0, ALU.mult, ALU.add))
            dve.wait_ge(s["w_summed"], 1)
            nc.vector.tensor_copy(w_sums, psum[:, 7, 0:2 * E])

            def bound_of_scores():
                link = Linked(dve, s["bound_chain"], 0)
                link(nc.vector.tensor_tensor(b_sq, b_rows[:, 0:2, :], b_rows[:, 0:2, :], ALU.mult))
                dve.wait_ge(s["r_max"], 1)
                link(nc.vector.scalar_tensor_tensor(out=w_sums, in0=w_sums, scalar=x_sq[:, NT:NT + 1],
                                                    in1=b_sq.rearrange("p i e -> p (i e)"), op0=ALU.mult, op1=ALU.add))
                link(nc.vector.tensor_reduce(by_head, w_sums.rearrange("p (i h d) -> p i h d", i=2, d=D), AX.X, ALU.add))
                link(nc.vector.tensor_tensor(by_head[:, 0, :], by_head[:, 0, :], by_head[:, 1, :], ALU.mult))
                link(nc.vector.tensor_reduce(by_head[:, 1, 0:1], by_head[:, 0, :], AX.X, ALU.max))
                nc.vector.tensor_scalar(flag[:], by_head[:, 1, 0:1], COS_ONE / (4 * SCALE * SCALE), None, ALU.is_le) \
                    .then_inc(s["flag_ready"], 1)

            for step in range(W):
                prep_dve(dve, step, 0, 0, first=True)
                if step == 3:
                    dve.wait_ge(s["x_squared"], 1)
                    nc.vector.tensor_reduce(x_sq[:, NT:NT + 1], x_sq[:, 0:NT], AX.X, ALU.max).then_inc(s["r_ready"], 1)
                if step == 1:
                    nc.vector.memset(v_pad[:], 0.0)
                    nc.vector.memset(r_z[:], 0.0).then_inc(s["pv_done"], 2)
                    nc.vector.memset(loop_chunk.var, 0.0).then_inc(s["norm_done"], 1)
                    nc.vector.memset(loop_chunk.nt, 0.0).then_inc(s["y2_ready"], 1)
                    nc.vector.memset(cos_small[:], 0.0).then_inc(s["c_free"], 1)
                    nc.vector.memset(loop_chunk.rstd, 0.0).then_inc(s["x1_stored"], 16)
                    nc.vector.memset(loop_chunk.mean, 0.0).then_inc(s["out_stored"], 16)
                if step == 8:
                    bound_of_scores()
            for e in range(EXPERTS):
                nc.vector.memset(order[:, e:e + 1], float(EXPERTS - e))
            dve.wait_ge(s["i_loaded"], 32)
            nc.vector.scalar_tensor_tensor(out=index[:, 2, :], in0=index[:, 0, :], scalar=float(S), in1=index[:, 1, :],
                                           op0=ALU.mult, op1=ALU.add).then_inc(s["i_ready"], 1)
            copy_x(1)
            dve.wait_ge(s["x_copied"], 8)
            nc.vector.memset(psum[:, 4:6, :], 0.0)
            dve.wait_ge(s["xn_stored"], 16)
            dve.wait_ge(s["ffw_turned"], 1)
            nc.vector.tensor_copy(sw12_t[:], psum[:, 7, 0:P])
            nc.vector.tensor_copy(sw3_t[:].rearrange("p a n -> p (a n)"), psum[:, 7, P:3 * P]).then_inc(s["ffw_ready"], 1)
            dve.wait_ge(s["ffw_ready"], 1)
            nc.vector.memset(psum[:, 7, :], 0.0).then_inc(s["o_copied"], 2)
            dve.wait_ge(s["c2_step"], 7)
            nc.vector.tensor_scalar(c2_last[:], c2[:, W - 1, :], LOG2_E, None, ALU.mult).then_inc(s["piece_used"], 1)
            dve.wait_ge(s["st_shared"], T // 2)
            dve.wait_ge(s["piece_used"], 1)

            fast = one_way(dve)
            with dve.If(fast == 1):
                for g in range(NG):
                    with dve.Fori(g * H // 2, (g + 1) * H // 2) as i:
                        link = Linked(dve, s["chain"], (i - H // 2) * CHUNK_LINKS)
                        for p in range(2):
                            u = i * 2 + p

                            def weigh(wg):
                                w0, n = W_GROUPS[wg]
                                n1 = u * NWG + (wg + 1)
                                dve.wait_ge(s["ot_done"], n1)
                                ot = ot_ps[:, :, 0:n * A].rearrange("p j (r e) -> p j r e", e=A)
                                rz = r_z[:, 0:GT * n].rearrange("p (j r) -> p j r", r=n)
                                nc.vector.reciprocal(rz, ot[:, :, :, D]).then_inc(s["rz_done"], 1)
                                dve.wait_ge(s["rz_done"], n1 * 2 - 1)
                                nc.vector.tensor_tensor(rz, rz, iw[:, w0:w0 + n].rearrange("p (o r) -> p o r", o=1)
                                                        .broadcast_to([P, GT, n]), ALU.mult).then_inc(s["rz_done"], 1)
                                dve.wait_ge(s["rz_done"], n1 * 2)
                                nc.vector.tensor_tensor(
                                    weighted[:, w0:w0 + n, :].rearrange("p r (j d) -> p j r d", d=D), ot[:, :, :, 0:D],
                                    rz.rearrange("p j (r o) -> p j r o", o=1).broadcast_to([P, GT, n, D]),
                                    ALU.mult).then_inc(s["norm_done"], 1)

                            for w in range(W):
                                if w in PIECE_STEPS:
                                    piece_dve(dve, *PIECE_STEPS[w], u, p, u - g * H)
                                if w in LAST_OF:
                                    wg = LAST_OF[w]
                                    dve.wait_ge(s["pv_done"], u * W + (w + 3))
                                    nc.vector.tensor_copy(o_sb[:, wg % 2, :], products_of(wg)).then_inc(s["o_copied"], 1)
                                prep_dve(dve, w, u + 1, 1 - p)
                                if w in FIRST_OF and w > 0:
                                    weigh(FIRST_OF[w] - 1)
                                m = p * W + w
                                if g == 1 and m in FF_STEPS:
                                    ff_dve(dve, FF_STEPS[m], loop_chunk, i - H // 2, ff_bank, link)
                            weigh(NWG - 1)
                            dve.wait_ge(s["norm_done"], u * NWG + (NWG + 1))
                            nc.vector.tensor_reduce(
                                comb[:, bass.ds(g * GT, GT), bass.ds((u - g * H) * D, D)].rearrange("p (b t) e -> p t b e", b=NB),
                                weighted[:].rearrange("p w (t b d) -> p t b d w", t=T, b=NB), AX.X, ALU.add) \
                                .then_inc(s["comb_done"], 1)
                        if g == 1:
                            assert link.n == CHUNK_LINKS, (link.n, CHUNK_LINKS)
            with dve.Else():
                cos_dve(dve)
                with dve.Fori(0, LOOP_CHUNKS) as k:
                    link = Linked(dve, s["chain"], k * CHUNK_LINKS)
                    for stage in STAGES:
                        ff_dve(dve, stage, loop_chunk, k, ff_bank, link)
            tail_dve(dve)


_INS = ['L0_attn_x', 'L0_attn_Wq', 'L0_attn_bq', 'L0_attn_Wk', 'L0_attn_bk', 'L0_attn_Wv', 'L0_attn_bv', 'L0_attn_Wo',
        'L0_attn_bo', 'L0_attn_phase_modulators', 'L0_attn_interference_weights', 'L0_ffn_index_b', 'L0_ffn_index_t',
        'L0_ffn_sw1', 'L0_ffn_sb1', 'L0_ffn_sw2', 'L0_ffn_sb2', 'L0_ffn_sw3', 'L0_ffn_sb3', 'L0_ffn_s_ln_g',
        'L0_ffn_s_ln_b', 'L0_ffn_sg_w', 'L0_ffn_sg_b', 'L0_ffn_eg_w', 'L0_ffn_eg_b', 'L0_ffn_exp_bias', 'L0_ffn_ew1',
        'L0_ffn_eb1', 'L0_ffn_ew2', 'L0_ffn_eb2', 'L0_ffn_ew3', 'L0_ffn_eb3', 'L0_ffn_sel_ln_g', 'L0_ffn_sel_ln_b']
_OUT = (8, 512, 128)


def kernel(**inputs):
    import numpy as _np
    import concourse.bacc as _bacc
    from concourse import mybir as _mybir
    from concourse.bass_utils import run_bass_kernel_spmd as _run

    nc = _bacc.Bacc("TRN2", target_bir_lowering=False, num_devices=1)
    arrays, args = {}, {}
    for name in _INS:
        x = _np.ascontiguousarray(inputs[name])
        arrays[f"in_{name}_dram"] = x
        args[name] = nc.dram_tensor(f"in_{name}_dram", x.shape, _mybir.dt.from_np(x.dtype), kind="ExternalInput").ap()
    args["x1"] = nc.dram_tensor("x1_dram", (4096, 128), _mybir.dt.float32, kind="Internal").ap()
    args["x_next"] = nc.dram_tensor("x_next_dram", (128, 2048), _mybir.dt.float32, kind="Internal").ap()
    args["out"] = nc.dram_tensor("out_0_dram", _OUT, _mybir.dt.float32, kind="ExternalOutput").ap()
    postln_kernel(nc, args)
    r = _run(nc, [arrays], core_ids=[0])
    return r.results[0]["out_0_dram"]
```
